# Optimizing a Trainium2 kernel written in Bass

```python
import numpy as np
import jax
import jax.numpy as jnp

def _softmax(x, axis=-1):
    return jax.nn.softmax(x, axis=axis)

def _gelu(x):
    return jax.nn.gelu(x, approximate=True)

def _silu(x):
    return jax.nn.silu(x)

def _sigmoid(x):
    return jax.nn.sigmoid(x)

def _layernorm(x, axis=-1, eps=1e-05):
    m = jnp.mean(x, axis=axis, keepdims=True)
    v = jnp.var(x, axis=axis, keepdims=True)
    return (x - m) / jnp.sqrt(v + eps)

def _scatter_add(tgt, idx, src, axis=0):
    return tgt.at[idx].add(src)

def _segment_sum(src, seg, n):
    return jax.ops.segment_sum(src, seg, n)
kernel_name = 'mk_recurrent_d2_jaxref_r8_484435'

def setup_inputs(seed: int=0):
    np.random.seed(seed)
    _w = jnp.asarray

    def _L0_attn_setup():
        import jax, jax.numpy as jnp
        import numpy as np
        import math
        D_MODEL = 128
        N_HEADS = 16
        D_HEAD = D_MODEL // N_HEADS
        WINDOW = 32
        SCALE = 1.0 / math.sqrt(D_HEAD)

        def _window_mask(seq_len: int) -> jnp.ndarray:
            i = jnp.arange(seq_len)[:, None]
            j = jnp.arange(seq_len)[None, :]
            allowed = (j <= i) & (j > i - WINDOW)
            return jnp.where(allowed, 0.0, -jnp.inf).astype(jnp.float32)
        key = jax.random.key(seed)
        kx, kqkv, kout = jax.random.split(key, 3)
        x = jax.random.normal(kx, (2, 256, D_MODEL), dtype=jnp.float32)
        lim_qkv = math.sqrt(6.0 / (D_MODEL + 3 * D_MODEL))
        W_qkv = jax.random.uniform(kqkv, (D_MODEL, 3 * D_MODEL), dtype=jnp.float32, minval=-lim_qkv, maxval=lim_qkv)
        lim_out = math.sqrt(6.0 / (D_MODEL + D_MODEL))
        W_out = jax.random.uniform(kout, (D_MODEL, D_MODEL), dtype=jnp.float32, minval=-lim_out, maxval=lim_out)
        return {'x': x, 'W_qkv': W_qkv, 'W_out': W_out}
    _L0_attn_in = _L0_attn_setup()

    def _L0_ffn_setup():
        import jax, jax.numpy as jnp
        import numpy as np
        CAPACITY_FACTOR = 1.25
        key = jax.random.key(seed)
        k1, k2, k3, k4 = jax.random.split(key, 4)
        B, T, D, F, E = (4, 512, 128, 512, 8)
        s = 0.02
        return {'x': jax.random.normal(k1, (B, T, D), dtype=jnp.float32), 'wg': jax.random.normal(k2, (D, E), dtype=jnp.float32) * s, 'W1': jax.random.normal(k3, (E, D, F), dtype=jnp.float32) * s, 'b1': jnp.zeros((E, F), dtype=jnp.float32), 'W2': jax.random.normal(k4, (E, F, D), dtype=jnp.float32) * s, 'b2': jnp.zeros((E, D), dtype=jnp.float32)}
    _L0_ffn_in = _L0_ffn_setup()

    def _L1_attn_setup():
        import jax, jax.numpy as jnp
        import numpy as np
        import math
        DIM = 128
        HEADS = 16
        HEAD_DIM = DIM // HEADS
        key = jax.random.key(seed)
        ks = jax.random.split(key, 7)
        b, n = (2, 256)
        scale = 1.0 / math.sqrt(DIM)
        x = jax.random.normal(ks[0], (b, n, DIM), dtype=jnp.float32)
        Wq = jax.random.normal(ks[1], (DIM, DIM), dtype=jnp.float32) * scale
        Wk = jax.random.normal(ks[2], (DIM, DIM), dtype=jnp.float32) * scale
        Wv = jax.random.normal(ks[3], (DIM, DIM), dtype=jnp.float32) * scale
        Wo = jax.random.normal(ks[4], (DIM, DIM), dtype=jnp.float32) * scale
        bo = jnp.zeros((DIM,), dtype=jnp.float32)
        denom_bias = jnp.zeros((1, HEADS, 1, 1), dtype=jnp.float32)
        return {'x': x, 'Wq': Wq, 'Wk': Wk, 'Wv': Wv, 'Wo': Wo, 'bo': bo, 'denom_bias': denom_bias}
    _L1_attn_in = _L1_attn_setup()

    def _L1_ffn_setup():
        import jax, jax.numpy as jnp
        import numpy as np
        B, S, DIM = (4, 512, 128)
        BASE_COUPLING = 0.1
        NUM_CYCLES = 3

        def _gelu(x):
            return jax.nn.gelu(x, approximate=False)

        def _coupling_net(h, w1, b1, w2, b2, w3, b3, w4, b4):
            h = _gelu(h @ w1 + b1)
            h = _gelu(h @ w2 + b2)
            h = _gelu(h @ w3 + b3)
            return jax.nn.sigmoid(h @ w4 + b4)

        def _global_net(h, w1, b1, w2, b2, w3, b3):
            h = _gelu(h @ w1 + b1)
            h = _gelu(h @ w2 + b2)
            return jax.nn.sigmoid(h @ w3 + b3)

        def _twist(x):
            o_r, o_i, p_r, p_i = jnp.split(x, 4, axis=-1)
            return jnp.concatenate([p_r, -p_i, -o_r, o_i], axis=-1)
        key = jax.random.key(seed)
        ks = jax.random.split(key, 9)
        d = DIM

        def w(k, fan_in, fan_out):
            return jax.random.normal(k, (fan_in, fan_out), dtype=jnp.float32) / np.sqrt(fan_in).astype(np.float32)
        inp = {'x': jax.random.normal(ks[0], (B, S, d), dtype=jnp.float32)}
        cn_dims = [(d, d), (d, d // 2), (d // 2, d // 4), (d // 4, 1)]
        for i, (a, b) in enumerate(cn_dims):
            inp[f'cn_w{i + 1}'] = w(ks[1 + i], a, b)
            inp[f'cn_b{i + 1}'] = jnp.zeros((b,), dtype=jnp.float32)
        gc_dims = [(d, d // 2), (d // 2, d // 4), (d // 4, 1)]
        for i, (a, b) in enumerate(gc_dims):
            inp[f'gc_w{i + 1}'] = w(ks[5 + i], a, b)
            inp[f'gc_b{i + 1}'] = jnp.zeros((b,), dtype=jnp.float32)
        inp['adaptive_range'] = jnp.full((1,), 0.2, dtype=jnp.float32)
        return inp
    _L1_ffn_in = _L1_ffn_setup()
    _d = {'L0_attn_x': _L0_attn_in['x'], 'L0_attn_W_qkv': _L0_attn_in['W_qkv'], 'L0_attn_W_out': _L0_attn_in['W_out'], 'L0_ffn_wg': _L0_ffn_in['wg'], 'L0_ffn_W1': _L0_ffn_in['W1'], 'L0_ffn_b1': _L0_ffn_in['b1'], 'L0_ffn_W2': _L0_ffn_in['W2'], 'L0_ffn_b2': _L0_ffn_in['b2'], 'L1_attn_Wq': _L1_attn_in['Wq'], 'L1_attn_Wk': _L1_attn_in['Wk'], 'L1_attn_Wv': _L1_attn_in['Wv'], 'L1_attn_Wo': _L1_attn_in['Wo'], 'L1_attn_bo': _L1_attn_in['bo'], 'L1_attn_denom_bias': _L1_attn_in['denom_bias'], 'L1_ffn_cn_w1': _L1_ffn_in['cn_w1'], 'L1_ffn_cn_b1': _L1_ffn_in['cn_b1'], 'L1_ffn_cn_w2': _L1_ffn_in['cn_w2'], 'L1_ffn_cn_b2': _L1_ffn_in['cn_b2'], 'L1_ffn_cn_w3': _L1_ffn_in['cn_w3'], 'L1_ffn_cn_b3': _L1_ffn_in['cn_b3'], 'L1_ffn_cn_w4': _L1_ffn_in['cn_w4'], 'L1_ffn_cn_b4': _L1_ffn_in['cn_b4'], 'L1_ffn_gc_w1': _L1_ffn_in['gc_w1'], 'L1_ffn_gc_b1': _L1_ffn_in['gc_b1'], 'L1_ffn_gc_w2': _L1_ffn_in['gc_w2'], 'L1_ffn_gc_b2': _L1_ffn_in['gc_b2'], 'L1_ffn_gc_w3': _L1_ffn_in['gc_w3'], 'L1_ffn_gc_b3': _L1_ffn_in['gc_b3'], 'L1_ffn_adaptive_range': _L1_ffn_in['adaptive_range']}
    _x0 = _d['L0_attn_x']
    _d['L0_attn_x'] = jax.random.normal(jax.random.fold_in(jax.random.key(seed), 1), (16, 256, 128), dtype=_x0.dtype)
    del _x0
    return _d

def reference(L0_attn_x, L0_attn_W_qkv, L0_attn_W_out, L0_ffn_wg, L0_ffn_W1, L0_ffn_b1, L0_ffn_W2, L0_ffn_b2, L1_attn_Wq, L1_attn_Wk, L1_attn_Wv, L1_attn_Wo, L1_attn_bo, L1_attn_denom_bias, L1_ffn_cn_w1, L1_ffn_cn_b1, L1_ffn_cn_w2, L1_ffn_cn_b2, L1_ffn_cn_w3, L1_ffn_cn_b3, L1_ffn_cn_w4, L1_ffn_cn_b4, L1_ffn_gc_w1, L1_ffn_gc_b1, L1_ffn_gc_w2, L1_ffn_gc_b2, L1_ffn_gc_w3, L1_ffn_gc_b3, L1_ffn_adaptive_range):

    def _L0_attn_ref(x, W_qkv, W_out):
        import jax, jax.numpy as jnp
        import numpy as np
        import math
        D_MODEL = 128
        N_HEADS = 16
        D_HEAD = D_MODEL // N_HEADS
        WINDOW = 32
        SCALE = 1.0 / math.sqrt(D_HEAD)

        def _window_mask(seq_len: int) -> jnp.ndarray:
            i = jnp.arange(seq_len)[:, None]
            j = jnp.arange(seq_len)[None, :]
            allowed = (j <= i) & (j > i - WINDOW)
            return jnp.where(allowed, 0.0, -jnp.inf).astype(jnp.float32)
        B, S, _ = x.shape
        qkv = x @ W_qkv
        qkv = qkv.reshape(B, S, 3, N_HEADS, D_HEAD)
        qkv = jnp.transpose(qkv, (2, 0, 3, 1, 4))
        q, k, v = (qkv[0], qkv[1], qkv[2])
        scores = jnp.einsum('bhsd,bhtd->bhst', q, k) * SCALE
        scores = scores + _window_mask(S)[None, None]
        weights = jax.nn.softmax(scores, axis=-1)
        out = jnp.einsum('bhst,bhtd->bhsd', weights, v)
        out = jnp.transpose(out, (0, 2, 1, 3)).reshape(B, S, D_MODEL)
        return out @ W_out

    def _L0_ffn_ref(x, wg, W1, b1, W2, b2):
        import jax, jax.numpy as jnp
        import numpy as np
        CAPACITY_FACTOR = 1.25
        B, T, D = x.shape
        E = wg.shape[1]
        N = B * T
        capacity = int(N / E * CAPACITY_FACTOR) + 1
        xf = x.reshape(N, D)
        logits = xf @ wg
        scores = jax.nn.softmax(logits, axis=-1)
        top1 = jnp.argmax(scores, axis=-1)
        combine_w = jnp.take_along_axis(scores, top1[:, None], axis=1)[:, 0]
        oh = jax.nn.one_hot(top1, E, dtype=jnp.int32)
        rank = jnp.take_along_axis(jnp.cumsum(oh, axis=0), top1[:, None], axis=1)[:, 0] - 1
        valid = rank < capacity
        trash = E * capacity
        slot = jnp.where(valid, top1 * capacity + rank, trash)
        buf = jnp.zeros((E * capacity + 1, D), dtype=x.dtype).at[slot].set(xf)
        eb = buf[:E * capacity].reshape(E, capacity, D)
        h = jax.nn.gelu(jnp.einsum('ecd,edf->ecf', eb, W1) + b1[:, None, :], approximate=False)
        y = jnp.einsum('ecf,efd->ecd', h, W2) + b2[:, None, :]
        yf = y.reshape(E * capacity, D)
        gathered = yf[jnp.minimum(slot, E * capacity - 1)]
        out_flat = jnp.where(valid[:, None], gathered, 0.0) * combine_w[:, None]
        return out_flat.reshape(B, T, D)

    def _L1_attn_ref(x, Wq, Wk, Wv, Wo, bo, denom_bias):
        import jax, jax.numpy as jnp
        import numpy as np
        import math
        DIM = 128
        HEADS = 16
        HEAD_DIM = DIM // HEADS
        b, n, d = x.shape
        h, hd = (HEADS, HEAD_DIM)

        def split_heads(t):
            return t.reshape(b, n, h, hd).transpose(0, 2, 1, 3)
        q = split_heads(x @ Wq.T)
        k = split_heads(x @ Wk.T)
        v = split_heads(x @ Wv.T)
        sim = jnp.einsum('bhid,bhjd->bhij', q, k) / math.sqrt(hd)
        causal_mask = jnp.triu(jnp.ones((n, n), dtype=bool), k=1)
        neg = -jnp.finfo(sim.dtype).max
        sim = jnp.where(causal_mask, neg, sim)
        sim_max = jnp.max(sim, axis=-1, keepdims=True)
        exp_sim = jnp.exp(sim - sim_max)
        denom = jnp.sum(exp_sim, axis=-1, keepdims=True) + jnp.exp(denom_bias)
        attn = exp_sim / denom
        out = jnp.einsum('bhij,bhjd->bhid', attn, v)
        out = out.transpose(0, 2, 1, 3).reshape(b, n, d)
        return out @ Wo.T + bo

    def _L1_ffn_ref(x, cn_w1, cn_b1, cn_w2, cn_b2, cn_w3, cn_b3, cn_w4, cn_b4, gc_w1, gc_b1, gc_w2, gc_b2, gc_w3, gc_b3, adaptive_range):
        import jax, jax.numpy as jnp
        import numpy as np
        B, S, DIM = (4, 512, 128)
        BASE_COUPLING = 0.1
        NUM_CYCLES = 3

        def _gelu(x):
            return jax.nn.gelu(x, approximate=False)

        def _coupling_net(h, w1, b1, w2, b2, w3, b3, w4, b4):
            h = _gelu(h @ w1 + b1)
            h = _gelu(h @ w2 + b2)
            h = _gelu(h @ w3 + b3)
            return jax.nn.sigmoid(h @ w4 + b4)

        def _global_net(h, w1, b1, w2, b2, w3, b3):
            h = _gelu(h @ w1 + b1)
            h = _gelu(h @ w2 + b2)
            return jax.nn.sigmoid(h @ w3 + b3)

        def _twist(x):
            o_r, o_i, p_r, p_i = jnp.split(x, 4, axis=-1)
            return jnp.concatenate([p_r, -p_i, -o_r, o_i], axis=-1)
        global_context = x.mean(axis=1, keepdims=True)
        gf = _global_net(global_context, gc_w1, gc_b1, gc_w2, gc_b2, gc_w3, gc_b3)
        out = x
        for _ in range(NUM_CYCLES):
            tf = _coupling_net(out, cn_w1, cn_b1, cn_w2, cn_b2, cn_w3, cn_b3, cn_w4, cn_b4)
            combined = 0.7 * gf + 0.3 * tf
            coupling = BASE_COUPLING + adaptive_range * (combined - 0.5) * 2.0
            out = out + coupling * _twist(out)
        return out
    x = L0_attn_x
    xn = _layernorm(x, axis=-1)
    s = _L0_attn_ref(xn, L0_attn_W_qkv, L0_attn_W_out)
    g = _silu(_L0_ffn_ref(xn, L0_ffn_wg, L0_ffn_W1, L0_ffn_b1, L0_ffn_W2, L0_ffn_b2))
    x = x + s * g
    xn = _layernorm(x, axis=-1)
    s = _L1_attn_ref(xn, L1_attn_Wq, L1_attn_Wk, L1_attn_Wv, L1_attn_Wo, L1_attn_bo, L1_attn_denom_bias)
    g = _silu(_L1_ffn_ref(xn, L1_ffn_cn_w1, L1_ffn_cn_b1, L1_ffn_cn_w2, L1_ffn_cn_b2, L1_ffn_cn_w3, L1_ffn_cn_b3, L1_ffn_cn_w4, L1_ffn_cn_b4, L1_ffn_gc_w1, L1_ffn_gc_b1, L1_ffn_gc_w2, L1_ffn_gc_b2, L1_ffn_gc_w3, L1_ffn_gc_b3, L1_ffn_adaptive_range))
    x = x + s * g
    return x

_drawn_inputs = setup_inputs


def setup_inputs(seed=0):
    import zlib

    import numpy as np

    out = dict(_drawn_inputs(seed))
    spreads = {'L0_ffn_b1': (0.0, 0.8),
     'L0_ffn_b2': (0.0, 0.8),
     'L1_attn_bo': (0.0, 0.8),
     'L1_attn_denom_bias': (0.0, 2.0),
     'L1_ffn_cn_b1': (0.0, 2.0),
     'L1_ffn_cn_b2': (0.0, 2.0),
     'L1_ffn_cn_b3': (0.0, 2.0),
     'L1_ffn_gc_b1': (0.0, 2.0),
     'L1_ffn_gc_b2': (0.0, 2.0)}
    factors = {'L0_attn_W_qkv': 8.0,
     'L0_attn_W_out': 8.0,
     'L0_ffn_wg': 8.0,
     'L0_ffn_W1': 8.0,
     'L0_ffn_W2': 8.0,
     'L1_ffn_cn_w1': 64.0,
     'L1_ffn_cn_w2': 64.0,
     'L1_ffn_cn_w3': 64.0,
     'L1_ffn_cn_w4': 64.0,
     'L1_ffn_gc_w1': 64.0,
     'L1_ffn_gc_w2': 64.0,
     'L1_ffn_gc_w3': 64.0,
     'L1_attn_Wq': 8.0,
     'L1_attn_Wk': 8.0,
     'L1_attn_Wv': 8.0,
     'L1_attn_Wo': 8.0}
    for name, (base, spread) in spreads.items():
        noise = np.random.default_rng([zlib.crc32(name.encode()), seed]).standard_normal(out[name].shape)
        drawn = base * np.exp(spread * noise) if base else spread * noise
        out[name] = jnp.asarray(drawn.astype(out[name].dtype))
    for name, factor in factors.items():
        out[name] = (out[name] * factor).astype(out[name].dtype)
    return out
```

```python
from contextlib import ExitStack

import numpy as np

import concourse.bass as bass
from concourse import mybir

F32 = mybir.dt.float32
BF16 = mybir.dt.bfloat16
U32 = mybir.dt.uint32
ALU = mybir.AluOpType
ACT = mybir.ActivationFunctionType
AX = mybir.AxisListType

P = 128
B, S, D = 16, 256, 128
N = B * S
TILES = N // P
HEADS, HD = 16, 8
HG = 4
WINDOW = 32
QB = 32
JB = S // QB
EXPERTS, FF = 8, 512
FC = FF // P
CAPACITY = int(N / EXPERTS * 1.25) + 1
ET = 6
ER = -(-CAPACITY // ET)
EROWS = ET * ER
TRASH = EXPERTS * EROWS
CT = 4
CHUNKS = TILES // CT
CW = CT * P
CYCLES = 3
EPS = 1e-5
MASKED = -3.0e38
C2 = EROWS // 2

_AT = {}
_WIDTH = 0
for _name, _w in (("ident", 128), ("twist", 128), ("tri", 128), ("identrep", 128), ("vmask", 128), ("onesbd", 32),
                  ("mask0", 64), ("qmask", 4), ("iota", 8), ("reset", 256)):
    _AT[_name] = (_WIDTH, _WIDTH + _w)
    _WIDTH += _w


def constants():
    c = np.zeros((P, _WIDTH), np.float32)
    p = np.arange(P)

    def put(name, a):
        c[:, _AT[name][0]:_AT[name][1]] = a

    put("ident", np.eye(P))
    twist = np.zeros((P, P))
    for m in range(P):
        q = m // 32
        twist[m + 64 if q < 2 else m - 64, m] = (1, -1, -1, 1)[q]
    put("twist", twist)
    put("tri", p[:, None] <= p[None, :])
    put("identrep", p[:, None] % 32 == p[None, :] % 32)
    put("vmask", p[:, None] // 32 == (p[None, :] // HD) % HG)
    put("onesbd", p[:, None] // 32 == np.arange(32)[None, :] // HD)
    q, k = (p % 32)[:, None], np.arange(32)[None, :]
    put("mask0", np.concatenate([np.where(k > q, 0, MASKED), np.where(k <= q, 0, MASKED)], 1))
    put("qmask", ((p[:, None] // HD) % HG == np.arange(4)[None, :]) * (1.0 / np.sqrt(np.float32(HD))))
    put("iota", np.arange(8)[None, :] - 8.0)
    put("reset", (np.arange(256) % TILES != 0)[None, :])
    return c


class Layer:

    def __init__(self, nc, sem, name, rounds, window):
        self.name, self.window = name, window
        self.units = [(r, pair) for r in rounds for pair in (0, 1)]
        self.U = len(self.units)
        self.x_staged = sem(f"{name}_x_staged")
        self.qk_made = sem(f"{name}_qk_made")
        self.v_made = sem(f"{name}_v_made")
        self.k_ready = sem(f"{name}_k_ready")
        self.q_ready = sem(f"{name}_q_ready")
        self.v_ready = sem(f"{name}_v_ready")
        self.scores_made = sem(f"{name}_scores_made")
        self.max_made = sem(f"{name}_max_made")
        self.shifted = sem(f"{name}_shifted")
        self.probs_made = sem(f"{name}_probs_made")
        self.turned = sem(f"{name}_turned")
        self.pv_made = sem(f"{name}_pv_made")
        self.o_ready = sem(f"{name}_o_ready")
        self.out_made = sem(f"{name}_out_made")
        self.out_taken = sem(f"{name}_out_taken")
        self.vec = sem(f"{name}_vec")
        self.divided = sem(f"{name}_divided")
        self.fin_ready = sem(f"{name}_fin_ready")

    def keys(self, j):
        return (max(0, 32 * (j - 1)), 64 if j else 32) if self.window else (0, 32 * (j + 1))

    def offsets(self, blocks):
        at, out = 0, []
        for j in blocks:
            out.append((j, at))
            at += self.keys(j)[1]
        return out, at


def after(eng, sem, value):
    if isinstance(value, int) and value <= 0:
        return
    eng.wait_ge(sem, value)


def each(eng, count, step):
    step(0, 0, False)
    step(1, 1, False)
    with eng.Fori(2, count - 2, 2) as n:
        step(n, 0, False)
        step(n + 1, 1, False)
    step(count - 2, 0, False)
    step(count - 1, 1, True)


class Chain:

    def __init__(self, eng, sem, per):
        self.eng, self.sem, self.per, self.k = eng, sem, per, 0

    def mark(self, ins):
        ins.then_inc(self.sem, 1)
        self.k += 1
        return self.k

    def wait(self, n, k=None):
        self.eng.wait_ge(self.sem, n * self.per + (self.k if k is None else k))

    def end(self):
        assert self.k == self.per, (self.k, self.per)
        self.k = 0


def two_blocks(nc, d, out, stop=None):
    ds = bass.ds
    with ExitStack() as ctx:
        def sb(name, shape, dt=F32):
            return ctx.enter_context(nc.sbuf_tensor(name, shape, dt))

        def sem(name):
            return ctx.enter_context(nc.semaphore(name))

        xin_rows = nc.dram_tensor("xin_rows", (TRASH, D), F32).ap()
        y_rows = nc.dram_tensor("y_rows", (TRASH + 1, D), F32).ap()
        x_dram = d["L0_attn_x"].rearrange("a (s p) d -> p (a s) d", p=P)
        out_dram = out.rearrange("a (s p) d -> p (a s) d", p=P)

        cf = sb("cf", [P, _WIDTH])
        const = {k: cf[:, a:b] for k, (a, b) in _AT.items()}
        identrep = sb("identrep", [P, P], BF16)
        mask0 = sb("mask0", [P, 64], BF16)
        tri = sb("tri", [P, P], BF16)
        ones = sb("ones", [P, P], BF16)
        zeros = sb("zeros", [P, D])
        powc = sb("powc", [P, CT])
        w_qkv0 = sb("w_qkv0", [P, 3 * D])
        w_out0 = sb("w_out0", [P, D])
        wg = sb("wg", [P, EXPERTS])
        b1 = sb("b1", [P, EXPERTS * FC])
        b2 = sb("b2", [P, EXPERTS, D])
        w_qkv1 = sb("w_qkv1", [P, 3 * D])
        w_out1 = sb("w_out1", [P, D])
        bo = sb("bo", [P, D])
        ebias = sb("ebias", [P, 1])
        cn_w = [sb("cn_w1", [P, 128]), sb("cn_w2", [P, 64]), sb("cn_w3", [64, 32]), sb("cn_w4", [32, 1])]
        cn_w4r = sb("cn_w4r", [32, P])
        cn_b = [sb("cn_b1", [P, 1]), sb("cn_b2", [64, 1]), sb("cn_b3", [32, 1]), sb("cn_b4", [P, 1])]
        gc_w = [sb("gc_w1", [P, 64]), sb("gc_w2", [64, 32]), sb("gc_w3", [32, 1])]
        gc_w3r = sb("gc_w3r", [32, P])
        gc_b = [sb("gc_b1", [64, 1]), sb("gc_b2", [32, 1]), sb("gc_b3", [P, 1])]
        arange = sb("arange", [P, 1])

        X = sb("X", [P, TILES, D])
        XN = sb("XN", [P, TILES, D])
        XNT = sb("XNT", [P, N])
        BIG = sb("BIG", [P, 2 * HG * JB * S])
        SRES = BIG[:, 0:N].rearrange("p (t d) -> p t d", d=D)
        G = BIG[:, N:2 * N].rearrange("p (t d) -> p t d", d=D)
        PT0 = BIG[:, 2 * N:3 * N].rearrange("p (a g c) -> p a g c", a=2, g=HG)
        PT1 = BIG[:, :].rearrange("p (a g k q) -> p a g k q", a=2, g=HG, k=JB)

        XNS = sb("XNS", [P, 2, CT, D])
        XTS = sb("XTS", [P, 2, CW])
        ST = sb("ST", [P, 2, CT, 6])
        MV = sb("MV", [P, 2, CT, 2])
        VE = sb("VE", [P, 2, CT])
        RS = sb("RS", [P, 2, CT])
        TH = sb("TH", [P, 2, CT, D])
        SG = sb("SG", [P, 2, CT, D])
        LG = sb("LG", [P, TILES, EXPERTS])
        RA, RB = (TH[:, 0, 2 * i:2 * i + 2, :].rearrange("p a (t e) -> p (a t) e", e=EXPERTS) for i in (0, 1))
        OH = SG[:, 0, 0:2, :].rearrange("p a (e t) -> p (a e) t", t=TILES)
        OHB = sb("OHB", [P, EXPERTS, TILES], BF16)
        CN, CS = (SG[:, i, 2:4, :].rearrange("p a c -> p (a c)") for i in (0, 1))
        R1 = sb("R1", [P, TILES])
        R2 = sb("R2", [P, TILES])
        R3 = sb("R3", [P, TILES])
        R4 = sb("R4", [P, TILES])
        PROB = sb("PROB", [P, TILES])
        SLOT = sb("SLOT", [P, TILES], U32)
        xT = sb("xT", [P, 2, S])
        qkT = sb("qkT", [P, 2, 2 * S])
        qx = sb("qx", [P, 2, JB, HG, QB])
        Vbd = sb("Vbd", [P, 2, JB, P])
        MX = sb("MX", [P, 2, 2, JB])
        PR = sb("PR", [P, 2, 2, 480])
        RD = sb("RD", [P, 2, S])
        oT = sb("oT", [P, 2, S])
        OB = sb("OB", [P, 2, 2, D])
        W1s = sb("W1s", [P, 2, FF])
        W2s = sb("W2s", [P, 2, FC, D])
        EB = sb("EB", [ER, 2, ET, D])
        EBT = BIG[:, 3 * N:3 * N + 2 * EROWS].rearrange("p (a c) -> p a c", a=2)
        HT = BIG[:, 3 * N + 2 * EROWS:3 * N + (2 + FC) * EROWS].rearrange("p (f c) -> p f c", f=FC)
        YB = sb("YB", [ER, 2, ET, D])
        UU, hA, hB, hC, TC, TM = (BIG[0:rows, 2 * N + 2 * CW * i:2 * N + 2 * CW * (i + 1)].rearrange("p (a c) -> p a c", a=2)
                                  for i, rows in enumerate((P, P, 64, 32, P, P)))
        CTX = sb("CTX", [P, B])
        g1 = sb("g1", [64, B])
        g2 = sb("g2", [32, B])
        GA = sb("GA", [P, B])
        AB = sb("AB", [P, B])
        sc = sb("sc", [P, 4])
        HZ = TM

        PS = [ctx.enter_context(nc.psum_tensor(f"ps{i}", [P, 2, 512], F32)) for i in range(4)]

        consts_in = sem("consts_in")
        x_first = sem("x_first")
        x_rest = sem("x_rest")
        w_in = sem("w_in")
        wb_in = sem("wb_in")
        pool_consts = sem("pool_consts")
        vector_consts = sem("vector_consts")
        net_consts = sem("net_consts")
        zero_filled = sem("zero_filled")
        zeros_made = sem("zeros_made")
        norm = [{s: sem(f"n{i}_{s}") for s in ("stats", "scale", "rows", "turned", "cols", "staged", "kept", "logits",
                                                "logits_kept", "vec", "gathered", "half", "tanh", "added", "prod")}
                for i in (0, 1)]
        route = {s: sem(f"r_{s}") for s in ("vec", "shifted", "exp", "onehot", "counts", "slots", "tail")}
        scattered = sem("scattered")
        L0 = Layer(nc, sem, "a0", [list(range(JB))], True)
        L1 = Layer(nc, sem, "a1", [[7, 2, 0], [6, 4], [5, 3, 1]], False)
        moe = {s: sem(f"m_{s}") for s in ("rows_in", "w_in0", "turned", "cols", "up", "gelu", "down", "y", "stored",
                                          "w_in1", "rows_in1", "stored1", "rows_in0")}
        gathered = sem("gathered")
        ffn = {s: sem(f"f_{s}") for s in ("start", "h1", "twist", "g1", "h2", "g2", "h3", "g3", "h4", "t4", "vec", "state",
                                          "last", "t5", "z5", "gate", "ctx", "c1", "e1", "c2", "e2", "c3", "e3", "ab")}
        stored = sem("stored")
        stored1 = sem("stored1")
        block = ctx.enter_context(nc.Block())

        N_W = 22

        turn_of = {}

        def alone(eng):
            name = str(eng.engine).split(".")[-1]
            if name not in turn_of:
                turn_of[name] = sem(f"turn_{name}")
            eng.sem_inc(turn_of[name], 1)

        @block.sync
        def _(sp):
            sp.dma_start(cf[:, :], d["consts"]).then_inc(consts_in, 16)
            for c in range(4):
                sp.dma_start(X[:, 8 * c:8 * c + 8, :], x_dram[:, 8 * c:8 * c + 8, :]).then_inc(x_rest if c else x_first, 16)

            def col(a):
                return a.rearrange("(p a) -> p a", a=1)

            def everywhere(a):
                return a.partition_broadcast(P)

            loads = [
                (wg[:, :], d["L0_ffn_wg"]), (w_qkv0[:, :], d["L0_attn_W_qkv"]), (w_out0[:, :], d["L0_attn_W_out"]),
                (b1[:, :], d["b1_cols"]), (w_qkv1[:, :], d["w_qkv1"]), (w_out1[:, :], d["w_out1"]),
                (cn_w[0][:, :], d["L1_ffn_cn_w1"]), (cn_w[1][:, :], d["L1_ffn_cn_w2"]), (cn_w[2][:, :], d["L1_ffn_cn_w3"]),
                (cn_w[3][:, :], d["L1_ffn_cn_w4"]), (cn_b[0][:, :], col(d["L1_ffn_cn_b1"])),
                (cn_b[1][:, :], col(d["L1_ffn_cn_b2"])), (cn_b[2][:, :], col(d["L1_ffn_cn_b3"])),
                (gc_w[0][:, :], d["L1_ffn_gc_w1"]), (gc_w[1][:, :], d["L1_ffn_gc_w2"]), (gc_w[2][:, :], d["L1_ffn_gc_w3"]),
                (gc_b[0][:, :], col(d["L1_ffn_gc_b1"])), (gc_b[1][:, :], col(d["L1_ffn_gc_b2"])),
                (b2[:, :, :], everywhere(d["L0_ffn_b2"])), (bo[:, :], everywhere(d["L1_attn_bo"])),
                (cn_b[3][:, :], everywhere(d["L1_ffn_cn_b4"])), (gc_b[2][:, :], everywhere(d["L1_ffn_gc_b3"])),
            ]
            assert len(loads) == N_W
            for dst, src in loads:
                sp.dma_start(dst, src).then_inc(w_in, 16)
            sp.dma_start(arange[:, :], everywhere(d["L1_ffn_adaptive_range"])).then_inc(wb_in, 16)
            bias = d["L1_attn_denom_bias"].rearrange("a h b c -> (a h) (b c)")
            for h in range(HEADS):
                sp.dma_start(ebias[HD * h:HD * h + HD, :], bias[h:h + 1, :].partition_broadcast(HD)
).then_inc(wb_in, 16)
            sp.wait_ge(zeros_made, 1)
            rows = xin_rows.rearrange("(p r) d -> p r d", p=ER)
            sp.dma_start(rows, zeros[0:ER, :].unsqueeze(1).broadcast_to([ER, TRASH // ER, D])).then_inc(zero_filled, 16)
            sp.dma_start(y_rows[TRASH:TRASH + 1, :], zeros[0:1, 0:D]).then_inc(zero_filled, 16)

            def expert(e, par, last):
                after(sp, moe["down"], 2 * e - 2)
                w = moe[f"w_in{par}"]
                sp.dma_start(W1s[:, par, :], w1_dram[:, ds(e * FF, FF)]).then_inc(w, 16)
                sp.dma_start(W2s[:, par, :, :], w2_dram[:, ds(e * FC, FC), :]).then_inc(w, 16)
                if isinstance(e, int) and e == 0:
                    sp.wait_ge(scattered, 16 * TILES)
                sp.dma_start(EB[:, par, :, :], xin_view[:, ds(e, 1), :, :].rearrange("r a i d -> r (a i) d")
                             ).then_inc(moe[f"rows_in{par}"], 16)
                if not (isinstance(e, int) and e == 0):
                    store(e - 1, 1 - par)
                if last:
                    store(e, par)

            def store(e, par):
                sp.wait_ge(moe["y"], 2 * e + 2)
                sp.dma_start(y_view[:, ds(e, 1), :, :].rearrange("r a i d -> r (a i) d"), YB[:, par, :, :]
                             ).then_inc(moe["stored"] if par == 0 else moe["stored1"], 16)

            w1_dram = d["L0_ffn_W1"]
            w2_dram = d["L0_ffn_W2"]
            xin_view = xin_rows.rearrange("(e r i) d -> r e i d", r=ER, i=ET)
            y_view = y_rows[0:TRASH, :].rearrange("(e r i) d -> r e i d", r=ER, i=ET)
            each(sp, EXPERTS, expert)

            def keep(n, par, last):
                sp.wait_ge(L1.fin_ready, n + 1)
                sp.dma_start(out_dram[:, ds(2 * n, 2), :], OB[:, par, :, :]).then_inc(stored if par == 0 else stored1, 16)

            each(sp, B, keep)
            sp.wait_ge(stored, 16 * (B // 2))
            sp.wait_ge(stored1, 16 * (B // 2))

        @block.gpsimd
        def _(pool):
            pool.memset(zeros[:, :], 0.0).then_inc(zeros_made, 1)
            pool.memset(powc[:, :], -0.5).then_inc(pool_consts, 1)
            pool.memset(ones[:, :], 1.0).then_inc(pool_consts, 1)
            pool.wait_ge(pool_consts, 2)

            def inverse_root(i, c, par):
                m = norm[i]
                pool.wait_ge(m["stats"], c + 1)
                alone(pool)
                pool.tensor_scalar(VE[:, par, :], MV[:, par, :, 1], EPS, None, ALU.add).then_inc(m["half"], 1)
                pool.wait_ge(m["half"], c + 1)
                pool.tensor_tensor(RS[:, par, :], VE[:, par, :], powc[:, :], ALU.pow).then_inc(m["scale"], 1)

            each(pool, CHUNKS, lambda c, par, last: inverse_root(0, c, par))

            pool.wait_ge(route["slots"], 1)
            pool.wait_ge(zero_filled, 2 * 16)
            pool.wait_ge(norm[0]["kept"], CHUNKS)
            for t in range(TILES):
                pool.indirect_dma_start(xin_rows, bass.IndirectOffsetOnAxis(SLOT[:, t:t + 1], 0), XN[:, t, :], None,
                                        bounds_check=TRASH - 1, oob_is_err=False).then_inc(scattered, 16)
            pool.wait_ge(moe["stored"], 16 * (EXPERTS // 2))
            pool.wait_ge(moe["stored1"], 16 * (EXPERTS // 2))
            for t in range(TILES):
                pool.indirect_dma_start(G[:, t, :], None, y_rows, bass.IndirectOffsetOnAxis(SLOT[:, t:t + 1], 0)
                                        ).then_inc(gathered, 16)

            def second_norm(c, par, last):
                m = norm[1]
                pool.wait_ge(m["prod"], c + 1)
                pool.tensor_tensor(X[:, ds(CT * c, CT), :], X[:, ds(CT * c, CT), :], SG[:, par, :, :], ALU.add
                                   ).then_inc(m["added"], 1)
                inverse_root(1, c, par)

            each(pool, CHUNKS, second_norm)

            def attend(n, par, last):
                A = L1

                def stage(n, par):
                    after(pool, A.v_made, 2 * n - 2)
                    pool.tensor_copy(xT[:, par, :], XNT[:, ds(n * S, S)]).then_inc(A.x_staged, 1)

                def widen(n, par):
                    pool.wait_ge(A.k_ready, n + 1)
                    after(pool, A.scores_made, A.U * n - A.U)
                    alone(pool)
                    for hh in range(HG):
                        q = pool.tensor_scalar(qx[:, par, :, hh, :], qkT[:, par, 0:S].rearrange("p (j q) -> p j q", q=QB),
                                               const["qmask"][:, hh:hh + 1], None, ALU.mult)
                    q.then_inc(A.q_ready, 1)

                if isinstance(n, int) and n == 0:
                    stage(0, 0)
                    widen(0, 0)
                if not last:
                    stage(n + 1, 1 - par)
                if not (isinstance(n, int) and n == 0):
                    finish(n - 1, 1 - par)
                if not last:
                    widen(n + 1, 1 - par)
                if last:
                    finish(n, par)

            def finish(n, par):
                A = L1
                pool.wait_ge(A.out_taken, n + 1)
                pool.tensor_tensor(SG[:, par, 0:2, :], TH[:, par, 0:2, :], XN[:, ds(2 * n, 2), :], ALU.mult
                                   ).then_inc(A.shifted, 1)
                pool.wait_ge(A.shifted, n + 1)
                s = stored if par == 0 else stored1
                if isinstance(n, int):
                    after(pool, s, 16 * (n // 2))
                else:
                    pool.wait_ge(s, 8 * (n - par))
                pool.tensor_tensor(OB[:, par, :, :], X[:, ds(2 * n, 2), :], SG[:, par, 0:2, :], ALU.add
                                   ).then_inc(A.fin_ready, 1)

            pool.wait_ge(ffn["gate"], CHUNKS)
            each(pool, B, attend)


        @block.tensor
        def _(pe):
            pe.wait_ge(consts_in, 16)
            pe.wait_ge(w_in, 16 * N_W)
            pe.wait_ge(pool_consts, 2)
            pe.wait_ge(vector_consts, 3)

            def turn_chunk(i, c, par):
                m = norm[i]
                pe.wait_ge(m["rows"], c + 1)
                after(pe, m["cols"], c - 1)
                for t in range(CT):
                    last = pe.transpose(PS[0][:, par, P * t:P * t + P], XNS[:, par, t, :], const["ident"])
                last.then_inc(m["turned"], 1)
                if i == 0:
                    pe.wait_ge(m["staged"], c + 1)
                    after(pe, m["logits_kept"], c - 1)
                    for t in range(CT):
                        last = pe.matmul(PS[1][:, par, 8 * t:8 * t + 8], XTS[:, par, P * t:P * t + P], wg[:, :],
                                         start=True, stop=True)
                    last.then_inc(m["logits"], 1)

            each(pe, CHUNKS, lambda c, par, last: turn_chunk(0, c, par))

            pe.wait_ge(route["onehot"], 1)
            ohb = OHB[:, :, :].rearrange("p e t -> p (e t)")
            pe.matmul(PS[2][:, 0, 0:256], tri[:, :], ohb, start=True, stop=True)
            pe.matmul(PS[2][:, 1, 0:256], ones[:, :], ohb, start=True, stop=True).then_inc(route["counts"], 1)

            def attention(A, w_qkv, w_out, PTa):
                psS = [PS[0], PS[1]]
                psO, psQK, psV = PS[2][:, 0, :], PS[2][:, 1, :], PS[3]

                def qkv(n, par):
                    pe.wait_ge(A.x_staged, n + 1)
                    after(pe, A.k_ready, n)
                    for i in (0, 1):
                        last = pe.matmul(psQK[:, i * S:(i + 1) * S], w_qkv[:, i * D:(i + 1) * D], xT[:, par, :],
                                         start=True, stop=True)
                    last.then_inc(A.qk_made, 1)
                    after(pe, A.v_ready, 2 * n)
                    after(pe, A.out_taken, n - 1)
                    for kb in range(JB):
                        for hh in range(HG):
                            last = pe.matmul(psV[32 * hh:32 * hh + 32, kb // 4, P * (kb % 4):P * (kb % 4) + P],
                                             xT[:, par, 32 * kb:32 * kb + 32], w_qkv[:, 2 * D:3 * D],
                                             start=True, stop=True, tile_position=(0, 32 * hh))
                        if kb % 4 == 3:
                            last.then_inc(A.v_made, 1)

                def scores(n, par, u):
                    blocks, pair = A.units[u]
                    slot = u % 2
                    if u == 0:
                        pe.wait_ge(A.q_ready, n + 1)
                        pe.wait_ge(A.k_ready, n + 1)
                    after(pe, A.probs_made if not A.window else A.shifted, A.U * n + u - 1)
                    for j, at in A.offsets(blocks)[0]:
                        k0, kn = A.keys(j)
                        for g in (0, 1):
                            r = 32 * (2 * pair + g)
                            pe.matmul(psS[slot][:, g, at:at + kn], qx[r:r + 32, par, j, :, :].rearrange("p h q -> p (h q)"),
                                      qkT[r:r + 32, par, S + k0:S + k0 + kn], start=True, stop=False)
                        for g in (0, 1):
                            r = 32 * (2 * pair + g)
                            mk = mask0[r:r + 32, 64 - kn if A.window else 32:64]
                            last = pe.matmul(psS[slot][:, g, at + kn - mk.shape[1]:at + kn], identrep[r:r + 32, :], mk,
                                             start=False, stop=True)
                    last.then_inc(A.scores_made, 1)

                def values(n, par):
                    pe.wait_ge(A.turned, A.U * (n + 1))
                    pe.wait_ge(A.v_ready, 2 * n + 2)
                    after(pe, A.o_ready, n)
                    for kb in range(JB):
                        qn = min(S - 32 * kb, 64 if A.window else S)
                        q0 = 32 * kb
                        for part in (0, 1):
                            for g in range(HG):
                                rhs = PT0[:, par, g, 64 * kb:64 * kb + qn] if A.window else PT1[:, par, g, kb, q0:S]
                                w = Vbd[:, par, kb, 32 * g:32 * g + 32] if part == 0 else const["onesbd"]
                                last = pe.matmul(psO[32 * g:32 * g + 32, part * S + q0:part * S + q0 + qn], w, rhs,
                                                 start=(kb == 0 and part == 0), stop=(kb == JB - 1),
                                                 skip_group_check=True, tile_position=(0, 32 * g))
                    last.then_inc(A.pv_made, 1)

                def project(n, par):
                    pe.wait_ge(A.o_ready, n + 1)
                    pe.wait_ge(A.v_ready, V_AT_PROJECT(n))
                    after(pe, A.out_taken, n)
                    for t in (0, 1):
                        last = pe.matmul(psV[:, 0, t * D:t * D + D], oT[:, par, t * P:t * P + P], w_out[:, :],
                                         start=True, stop=True)
                    last.then_inc(A.out_made, 1)

                def V_AT_PROJECT(n):
                    return 2 * n + 4 if not (isinstance(n, int) and n == B - 1) else 2 * n + 2

                def step(n, par, last):
                    first = isinstance(n, int) and n == 0
                    if first:
                        qkv(0, 0)
                    for u in range(A.U):
                        scores(n, par, u)
                        if u == (1 if A.U > 2 else 0) and not first:
                            values(n - 1, 1 - par)
                        if u == (3 if A.U > 2 else 1) and not first:
                            project(n - 1, 1 - par)
                        if u == (4 if A.U > 2 else 1) and not last:
                            qkv(n + 1, 1 - par)
                    if last:
                        values(n, par)
                        project(n, par)

                each(pe, B, step)

            pe.wait_ge(route["vec"], 12)
            attention(L0, w_qkv0, w_out0, PT0)

            def expert(e, par, last):
                if par == 0:
                    wv = 8 * e + 16 if not isinstance(e, int) else 16 * (e // 2 + 1)
                else:
                    wv = 8 * (e - 1) + 16 if not isinstance(e, int) else 16 * (e // 2 + 1)
                pe.wait_ge(moe[f"rows_in{par}"], wv)
                after(pe, moe["cols"], 2 * e)
                for i in range(ET):
                    t = pe.transpose(PS[0][:, i // 3, ER * (i % 3):ER * (i % 3) + ER], EB[:, par, i, :],
                                     const["ident"][0:ER, 0:ER])
                    if i % 3 == 2:
                        t.then_inc(moe["turned"], 1)
                pe.wait_ge(moe[f"w_in{par}"], 2 * wv)
                for f in range(FC):
                    for h in (0, 1):
                        k = 2 * f + h
                        if f == 0:
                            pe.wait_ge(moe["cols"], 2 * e + h + 1)
                        after(pe, moe["gelu"], 8 * e + k - 3)
                        pe.matmul(PS[1 + (k % 4) // 2][:, k % 2, 0:C2], W1s[:, par, P * f:P * f + P],
                                  EBT[:, par, C2 * h:C2 * h + C2], start=True, stop=True).then_inc(moe["up"], 1)
                for h in (0, 1):
                    pe.wait_ge(moe["gelu"], 8 * e + 8)
                    after(pe, moe["y"], 2 * e + h - 1)
                    for i in range(3):
                        for f in range(FC):
                            at = C2 * h + ER * i
                            last_ = pe.matmul(PS[3][0:ER, h, D * i:D * i + D], HT[:, f, at:at + ER], W2s[:, par, f, :],
                                              start=(f == 0), stop=(f == FC - 1))
                    last_.then_inc(moe["down"], 1)

            pe.wait_ge(L0.out_taken, B)
            each(pe, EXPERTS, expert)

            pe.wait_ge(moe["y"], 2 * EXPERTS)
            each(pe, CHUNKS, lambda c, par, last: turn_chunk(1, c, par))

            f = ffn
            pe.wait_ge(f["ctx"], 1)
            pe.matmul(PS[3][0:64, 0, 0:B], gc_w[0][:, :], CTX[:, :], start=True, stop=True).then_inc(f["c1"], 1)
            pe.wait_ge(f["e1"], 1)
            pe.matmul(PS[3][0:32, 0, 64:64 + B], gc_w[1][:, :], g1[:, :], start=True, stop=True).then_inc(f["c2"], 1)
            pe.wait_ge(f["e2"], 1)
            pe.matmul(PS[3][:, 0, 128:128 + B], gc_w3r[:, :], g2[:, :], start=True, stop=True).then_inc(f["c3"], 1)
            pe.wait_ge(f["ab"], 1)

            def couple(i, par_, last):
                for cyc in range(CYCLES):
                    for s in (0, 1):
                        k = i * (2 * CYCLES) + 2 * cyc + s
                        H0, H1, TW = PS[2 * s][:, 0, :], PS[2 * s][:, 1, :], PS[2 * s + 1][:, 0, :]
                        pe.wait_ge(f["state"], SB + 8 * i + 2 * cyc + s)
                        pe.matmul(H0, cn_w[0][:, :], UU[:, s, :], start=True, stop=True).then_inc(f["h1"], 1)
                        pe.matmul(TW, const["twist"], UU[:, s, :], start=True, stop=True).then_inc(f["twist"], 1)
                    for s in (0, 1):
                        k = i * (2 * CYCLES) + 2 * cyc + s
                        H0, H1 = PS[2 * s][:, 0, :], PS[2 * s][:, 1, :]
                        pe.wait_ge(f["g1"], k + 1)
                        pe.matmul(H1[0:64, :], cn_w[1][:, :], hA[:, s, :], start=True, stop=True).then_inc(f["h2"], 1)
                    for s in (0, 1):
                        k = i * (2 * CYCLES) + 2 * cyc + s
                        H0, H1 = PS[2 * s][:, 0, :], PS[2 * s][:, 1, :]
                        pe.wait_ge(f["g2"], k + 1)
                        alone(pe)
                        pe.matmul(H0[0:32, :], cn_w[2][:, :], hB[:, s, :], start=True, stop=True).then_inc(f["h3"], 1)
                    for s in (0, 1):
                        k = i * (2 * CYCLES) + 2 * cyc + s
                        H0, H1 = PS[2 * s][:, 0, :], PS[2 * s][:, 1, :]
                        pe.wait_ge(f["g3"], k + 1)
                        pe.matmul(H1, cn_w4r[:, :], hC[:, s, :], start=True, stop=True).then_inc(f["h4"], 1)
                for s in (0, 1):
                    pe.wait_ge(f["state"], SB + 8 * i + 2 * CYCLES + s)
                    after(pe, f["gate"], 2 * i + s - 1)
                    for t in range(CT):
                        last_ = pe.transpose(PS[2 * s + 1][:, 1, P * t:P * t + P], UU[:, s, P * t:P * t + P], const["ident"])
                    last_.then_inc(f["last"], 1)

            small(pe, CHUNKS // 2, couple)

            pe.wait_ge(ffn["gate"], CHUNKS)
            attention(L1, w_qkv1, w_out1, PT1)

        @block.scalar
        def _(act):
            def keep_chunk(i, c, par):
                m = norm[i]
                act.wait_ge(m["turned"], c + 1)
                if i == 0:
                    after(act, m["logits"], c - 1)
                    act.activation(XTS[:, par, :], PS[0][:, par, :], ACT.Copy).then_inc(m["staged"], 1)
                alone(act)
                act.activation(XNT[:, ds(CW * c, CW)], PS[0][:, par, :], ACT.Copy).then_inc(m["cols"], 1)
                if i == 0:
                    act.activation(XN[:, ds(CT * c, CT), :], XNS[:, par, :, :], ACT.Copy).then_inc(m["kept"], 1)

            each(act, CHUNKS, lambda c, par, last: keep_chunk(0, c, par))
            act.wait_ge(route["shifted"], 1)
            act.activation(RB[:, :, :], RA[:, :, :], ACT.Exp).then_inc(route["exp"], 1)
            act.wait_ge(wb_in, 17 * 16)
            act.activation(ebias[:, :], ebias[:, :], ACT.Exp).then_inc(L1.vec, 1)
            act.wait_ge(norm[0]["cols"], CHUNKS)

            def attention(A):
                psS = [PS[0], PS[1]]
                psQK, psV = PS[2][:, 1, :], PS[3]

                def stage(n, par):
                    if not A.window:
                        return
                    after(act, A.v_made, 2 * n - 2)
                    alone(act)
                    act.activation(xT[:, par, :], XNT[:, ds(n * S, S)], ACT.Copy).then_inc(A.x_staged, 1)

                def split(n, par):
                    act.wait_ge(A.qk_made, n + 1)
                    after(act, A.scores_made, A.U * n - A.U)
                    if A.window:
                        for hh in range(HG):
                            q = act.activation(qx[:, par, :, hh, :], psQK[:, 0:S].rearrange("p (j q) -> p j q", q=QB),
                                               ACT.Copy, scale=const["qmask"][:, hh:hh + 1])
                        q.then_inc(A.q_ready, 1)
                        act.activation(qkT[:, par, S:2 * S], psQK[:, S:2 * S], ACT.Copy).then_inc(A.k_ready, 1)
                    else:
                        act.activation(qkT[:, par, :], psQK[:, :], ACT.Copy).then_inc(A.k_ready, 1)

                def probs(n, par, u):
                    blocks, pair = A.units[u]
                    slot = u % 2
                    cols, width = A.offsets(blocks)
                    after(act, A.turned, A.U * n + u - 1)
                    if A.window:
                        act.wait_ge(A.shifted, A.U * n + u + 1)
                        act.activation(PR[:, slot, :, 0:width], PR[:, slot, :, 0:width], ACT.Exp).then_inc(A.probs_made, 1)
                        return
                    act.wait_ge(A.max_made, A.U * n + u + 1)
                    for j, at in cols:
                        kn = A.keys(j)[1]
                        for g in (0, 1):
                            last = act.activation(PR[:, slot, g, at:at + kn], psS[slot][:, g, at:at + kn], ACT.Exp,
                                                  bias=MX[:, slot, g, j:j + 1])
                    last.then_inc(A.probs_made, 1)

                def keep(n, par):
                    if not A.window:
                        return
                    act.wait_ge(A.out_made, n + 1)
                    alone(act)
                    act.activation(SRES[:, ds(2 * n, 2), :].rearrange("p t d -> p (t d)"), psV[:, 0, 0:S], ACT.Copy
                                   ).then_inc(A.out_taken, 1)

                def step(n, par, last):
                    first = isinstance(n, int) and n == 0
                    if first:
                        stage(0, 0)
                        split(0, 0)
                    if not last:
                        stage(n + 1, 1 - par)
                    for u in range(A.U):
                        probs(n, par, u)
                    if not first:
                        keep(n - 1, 1 - par)
                    if not last:
                        split(n + 1, 1 - par)
                    if last:
                        keep(n, par)

                each(act, B, step)

            attention(L0)

            def expert(e, par, last):
                for f in range(FC):
                    for h in (0, 1):
                        k = 2 * f + h
                        act.wait_ge(moe["up"], 8 * e + k + 1)
                        if k == 0:
                            after(act, moe["down"], 2 * e)
                        alone(act)
                        act.activation(HT[:, f, C2 * h:C2 * h + C2], PS[1 + (k % 4) // 2][:, k % 2, 0:C2], ACT.Gelu,
                                       bias=b1[:, ds(FC * e + f, 1)]).then_inc(moe["gelu"], 1)

            each(act, EXPERTS, expert)

            def second_norm(c, par, last):
                m = norm[1]
                act.wait_ge(m["gathered"], c + 1)
                alone(act)
                act.activation(TH[:, par, :, :], G[:, ds(CT * c, CT), :], ACT.Tanh).then_inc(m["tanh"], 1)
                keep_chunk(1, c, par)

            each(act, CHUNKS, second_norm)

            f = ffn
            act.wait_ge(f["c1"], 1)
            act.activation(g1[:, :], PS[3][0:64, 0, 0:B], ACT.Gelu, bias=gc_b[0][:, :], scale=1.0 / S).then_inc(f["e1"], 1)
            act.wait_ge(f["c2"], 1)
            act.activation(g2[:, :], PS[3][0:32, 0, 64:64 + B], ACT.Gelu, bias=gc_b[1][:, :]).then_inc(f["e2"], 1)
            act.wait_ge(f["c3"], 1)
            act.wait_ge(net_consts, 1)
            act.activation(GA[:, :], PS[3][:, 0, 128:128 + B], ACT.Tanh, bias=sc[:, 2:3], scale=0.5).then_inc(f["e3"], 1)

            def couple(i, par_, last):
                for cyc in range(CYCLES):
                    for st, (w, src, dst, hin, hout) in enumerate((
                            ("h1", 0, hA, P, "g1"), ("h2", 1, hB, 64, "g2"), ("h3", 0, hC, 32, "g3"), ("h4", 1, TC, P, "t4"))):
                        for s in (0, 1):
                            k = i * (2 * CYCLES) + 2 * cyc + s
                            act.wait_ge(f[w], k + 1)
                            src_ = PS[2 * s][0:hin, src, :]
                            if st < 3:
                                act.activation(dst[:, s, :], src_, ACT.Gelu, bias=cn_b[st][:, :]).then_inc(f[hout], 1)
                            else:
                                after(act, f["state"], SB + 8 * i + 2 * cyc + s)
                                act.activation(dst[:, s, :], src_, ACT.Tanh, bias=sc[:, 3:4], scale=0.5).then_inc(f[hout], 1)
                for s in (0, 1):
                    act.wait_ge(f["last"], 2 * i + s + 1)
                    z = PS[2 * s + 1][:, 1, :]
                    act.activation(TC[:, s, :], z, ACT.Tanh, scale=0.5).then_inc(f["t5"], 1)
                    act.activation(HZ[:, s, :], z, ACT.Copy, scale=0.5).then_inc(f["z5"], 1)

            small(act, CHUNKS // 2, couple)
            attention(L1)

        @block.vector
        def _(dve):
            dve.wait_ge(consts_in, 16)
            dve.tensor_copy(identrep[:, :], const["identrep"]).then_inc(vector_consts, 1)
            dve.tensor_copy(mask0[:, :], const["mask0"]).then_inc(vector_consts, 1)
            dve.tensor_copy(tri[:, :], const["tri"]).then_inc(vector_consts, 1)

            def normalise(i, c, par, ch):
                m = norm[i]
                for t in range(CT):
                    a = dve.bn_stats(ST[:, par, t, :], X[:, ds(CT * c + t, 1), :].rearrange("p a d -> p (a d)"))
                ch.mark(a)
                ch.wait(c)
                alone(dve)
                for t in range(CT):
                    a = dve.bn_aggr(MV[:, par, t, :], ST[:, par, t, :])
                a.then_inc(m["stats"], 1)
                dve.wait_ge(m["scale"], c + 1)
                after(dve, m["turned"], c - 1)
                if i == 0:
                    after(dve, m["kept"], c - 1)
                for t in range(CT):
                    a = dve.tensor_scalar(XNS[:, par, t, :], X[:, ds(CT * c + t, 1), :].rearrange("p a d -> p (a d)"),
                                          MV[:, par, t, 0:1], RS[:, par, t:t + 1], ALU.subtract, ALU.mult)
                a.then_inc(m["rows"], 1)

            def first_norm(c, par, last):
                m = norm[0]
                if isinstance(c, int) and c == 0:
                    dve.wait_ge(x_first, 16)
                if isinstance(c, int) and c == 1:
                    dve.wait_ge(x_rest, 48)
                normalise(0, c, par, ch0)
                dve.wait_ge(m["logits"], c + 1)
                dve.tensor_copy(LG[:, ds(CT * c, CT), :].rearrange("p t e -> p (t e)"), PS[1][:, par, 0:CT * EXPERTS]
                                ).then_inc(m["logits_kept"], 1)
                ch0.end()

            ch0 = Chain(dve, norm[0]["vec"], 1)
            each(dve, CHUNKS, first_norm)

            r = Chain(dve, route["vec"], 12)
            dve.wait_ge(norm[0]["logits_kept"], CHUNKS)

            def over_e(a):
                return a.unsqueeze(2).broadcast_to([P, TILES, EXPERTS])

            def bcast_t(a):
                return a.unsqueeze(1).broadcast_to([P, TILES, EXPERTS])

            r.mark(dve.tensor_reduce(R1[:, :], LG[:, :, :], AX.X, ALU.max))
            r.wait(0)
            dve.tensor_tensor(RA[:, :, :], LG[:, :, :], over_e(R1[:, :]), ALU.subtract).then_inc(route["shifted"], 1)
            dve.wait_ge(route["shifted"], 1)
            r.mark(dve.tensor_scalar(LG[:, :, :], RA[:, :, :], 0.0, None, ALU.is_ge))
            r.wait(0)
            r.mark(dve.tensor_tensor(LG[:, :, :], LG[:, :, :], bcast_t(const["iota"]), ALU.mult))
            r.wait(0)
            r.mark(dve.tensor_reduce(R2[:, :], LG[:, :, :], AX.X, ALU.min))
            r.wait(0)
            oh = OH[:, :, :].rearrange("p e t -> p t e")
            r.mark(dve.tensor_tensor(oh, bcast_t(const["iota"]), over_e(R2[:, :]), ALU.is_equal))
            r.wait(0)
            dve.tensor_copy(OHB[:, :, :], OH[:, :, :]).then_inc(route["onehot"], 1)
            dve.wait_ge(route["exp"], 1)
            r.mark(dve.tensor_reduce(R1[:, :], RB[:, :, :], AX.X, ALU.add))
            r.wait(0)
            r.mark(dve.reciprocal(PROB[:, :], R1[:, :]))
            dve.wait_ge(route["counts"], 1)
            r.mark(dve.tensor_copy(CN[:, :], PS[2][:, 1, 0:256]))
            r.wait(0)
            r.mark(dve.tensor_tensor_scan(CS[:, :], const["reset"], CN[:, :], 0.0, ALU.mult, ALU.add))
            r.wait(0)
            r.mark(dve.tensor_tensor(CS[:, :], CS[:, :], CN[:, :], ALU.subtract))
            r.wait(0)
            r.mark(dve.tensor_tensor(CS[:, :], PS[2][:, 0, 0:256], CS[:, :], ALU.add))
            r.wait(0)
            r.mark(dve.tensor_tensor(CS[:, :], CS[:, :], OH[:, :, :].rearrange("p e t -> p (e t)"), ALU.mult))
            r.wait(0)
            q = Chain(dve, route["tail"], 0)

            def link(ins):
                q.mark(ins)
                q.wait(0)

            link(dve.tensor_reduce(R1[:, :], CS[:, :].rearrange("p (e t) -> p t e", e=EXPERTS), AX.X, ALU.add))
            link(dve.tensor_scalar(R3[:, :], R2[:, :], float(EXPERTS), float(EROWS), ALU.add, ALU.mult))
            link(dve.tensor_tensor(R3[:, :], R3[:, :], R1[:, :], ALU.add))
            link(dve.tensor_scalar(R3[:, :], R3[:, :], -1.0 - TRASH, None, ALU.add))
            link(dve.tensor_scalar(R4[:, :], R1[:, :], float(CAPACITY), None, ALU.is_le))
            link(dve.tensor_tensor(R3[:, :], R3[:, :], R4[:, :], ALU.mult))
            link(dve.tensor_scalar(R3[:, :], R3[:, :], float(TRASH), None, ALU.add))
            dve.tensor_copy(SLOT[:, :], R3[:, :]).then_inc(route["slots"], 1)
            link(dve.tensor_scalar(PROB[:, :], PROB[:, :], 0.5, None, ALU.mult))

            def attention(A, PTa):
                psS = [PS[0], PS[1]]
                psO, psQK, psV = PS[2][:, 0, :], PS[2][:, 1, :], PS[3]
                ch = Chain(dve, A.vec, A.U if A.window else 0)

                def spread(n, par):
                    after(dve, A.pv_made, n - 1)
                    for h in (0, 1):
                        dve.wait_ge(A.v_made, 2 * n + h + 1)
                        dve.tensor_tensor(Vbd[:, par, 4 * h:4 * h + 4, :], psV[:, h, :].rearrange("p (k c) -> p k c", c=P),
                                          const["vmask"].unsqueeze(1).broadcast_to([P, 4, P]), ALU.mult).then_inc(A.v_ready, 1)

                def largest(n, par, u):
                    blocks, pair = A.units[u]
                    slot = u % 2
                    cols, width = A.offsets(blocks)
                    dve.wait_ge(A.scores_made, A.U * n + u + 1)
                    if A.window:
                        dve.tensor_reduce(MX[:, slot, :, 0:1], psS[slot][:, :, 0:32], AX.X, ALU.max)
                        wide = psS[slot][:, :, 32:480].rearrange("p g (j k) -> p g j k", k=64)
                        ch.mark(dve.tensor_reduce(MX[:, slot, :, 1:JB], wide, AX.X, ALU.max))
                        after(dve, A.turned, A.U * n + u - 1)
                        ch.wait(n)
                        dve.tensor_tensor(PR[:, slot, :, 0:32], psS[slot][:, :, 0:32],
                                          MX[:, slot, :, 0:1].broadcast_to([P, 2, 32]), ALU.subtract)
                        for g in (0, 1):
                            a = dve.tensor_tensor(PR[:, slot, g, 32:480].rearrange("p (j k) -> p j k", k=64), wide[:, g],
                                                  MX[:, slot, g, 1:JB].unsqueeze(2).broadcast_to([P, JB - 1, 64]),
                                                  ALU.subtract)
                        a.then_inc(A.shifted, 1)
                    else:
                        after(dve, A.probs_made, A.U * n + u - 1)
                        for j, at in cols:
                            kn = A.keys(j)[1]
                            a = dve.tensor_reduce(MX[:, slot, :, j:j + 1], psS[slot][:, :, at:at + kn], AX.X, ALU.max,
                                                  negate=True)
                        a.then_inc(A.max_made, 1)

                def turn(n, par, u):
                    blocks, pair = A.units[u]
                    slot = u % 2
                    dve.wait_ge(A.probs_made, A.U * n + u + 1)
                    if u == 0:
                        after(dve, A.pv_made, n - 1)
                    for g in (0, 1):
                        gg = 2 * pair + g
                        if A.window:
                            a = dve.transpose(PT0[:, par, gg, 0:480], PR[:, slot, g, 0:480])
                        else:
                            for j, at in A.offsets(blocks)[0]:
                                a = dve.transpose(PT1[:, par, gg, 0:j + 1, 32 * j:32 * j + 32],
                                                  PR[:, slot, g, at:at + 32 * (j + 1)].rearrange("p (k q) -> p k q", q=32))
                    a.then_inc(A.turned, 1)

                def divide(n, par):
                    dve.wait_ge(A.pv_made, n + 1)
                    if A.window:
                        dve.reciprocal(RD[:, par, :], psO[:, S:2 * S]).then_inc(A.divided, 1)
                        dve.wait_ge(A.divided, n + 1)
                    else:
                        dve.tensor_scalar(RD[:, par, :], psO[:, S:2 * S], ebias[:, 0:1], None, ALU.add).then_inc(A.divided, 1)
                        dve.wait_ge(A.divided, 2 * n + 1)
                        dve.reciprocal(RD[:, par, :], RD[:, par, :]).then_inc(A.divided, 1)
                        dve.wait_ge(A.divided, 2 * n + 2)
                    after(dve, A.out_made, n - 1)
                    dve.tensor_tensor(oT[:, par, :], psO[:, 0:S], RD[:, par, :], ALU.mult).then_inc(A.o_ready, 1)

                def take(n, par):
                    if A.window:
                        return
                    dve.wait_ge(A.out_made, n + 1)
                    after(dve, A.shifted, n - 1)
                    dve.tensor_tensor(TH[:, par, 0:2, :], psV[:, 0, 0:S].rearrange("p (t d) -> p t d", d=D),
                                      bo[:, :].unsqueeze(1).broadcast_to([P, 2, D]), ALU.add).then_inc(A.out_taken, 1)

                def step(n, par, last):
                    first = isinstance(n, int) and n == 0
                    if first:
                        spread(0, 0)
                    for u in range(A.U):
                        largest(n, par, u)
                        if u > 0:
                            turn(n, par, u - 1)
                        elif not first:
                            turn(n - 1, 1 - par, A.U - 1)
                        if u == (2 if A.U > 2 else 0) and not first:
                            divide(n - 1, 1 - par)
                        if u == (4 if A.U > 2 else 1) and not first:
                            take(n - 1, 1 - par)
                    if not last:
                        spread(n + 1, 1 - par)
                    ch.end()
                    if last:
                        turn(n, par, A.U - 1)
                        divide(n, par)
                        take(n, par)

                each(dve, B, step)

            attention(L0, PT0)

            def expert(e, par, last):
                for h in (0, 1):
                    dve.wait_ge(moe["turned"], 2 * e + h + 1)
                    after(dve, moe["up"], 8 * e - 8)
                    dve.tensor_copy(EBT[:, par, C2 * h:C2 * h + C2], PS[0][:, h, 0:C2]).then_inc(moe["cols"], 1)
                s = moe["stored"] if par == 0 else moe["stored1"]
                if isinstance(e, int):
                    after(dve, s, 16 * (e // 2))
                else:
                    dve.wait_ge(s, 8 * (e - par))
                for h in (0, 1):
                    dve.wait_ge(moe["down"], 2 * e + h + 1)
                    dve.tensor_tensor(YB[:, par, 3 * h:3 * h + 3, :], PS[3][0:ER, h, 0:3 * D].rearrange("p (i d) -> p i d", d=D),
                                      b2[0:ER, ds(e, 1), :].broadcast_to([ER, 3, D]), ALU.add).then_inc(moe["y"], 1)

            each(dve, EXPERTS, expert)

            ch1 = Chain(dve, norm[1]["vec"], 2)

            def second_norm(c, par, last):
                m = norm[1]
                if isinstance(c, int):
                    dve.wait_ge(gathered, 16 * TILES)
                Gc = G[:, ds(CT * c, CT), :]
                dve.tensor_tensor(Gc, Gc, PROB[:, ds(CT * c, CT)].unsqueeze(2).broadcast_to([P, CT, D]), ALU.mult
                                  ).then_inc(m["gathered"], 1)
                dve.wait_ge(m["tanh"], c + 1)
                ch1.mark(dve.scalar_tensor_tensor(SG[:, par, :, :].rearrange("p t d -> p (t d)"),
                                                  TH[:, par, :, :].rearrange("p t d -> p (t d)"), 1.0,
                                                  Gc.rearrange("p t d -> p (t d)"), ALU.add, ALU.mult))
                ch1.wait(c)
                dve.tensor_tensor(SG[:, par, :, :], SG[:, par, :, :], SRES[:, ds(CT * c, CT), :], ALU.mult
                                  ).then_inc(m["prod"], 1)
                dve.wait_ge(m["added"], c + 1)
                normalise(1, c, par, ch1)
                ch1.end()

            each(dve, CHUNKS, second_norm)

            f = ffn
            dve.wait_ge(wb_in, 17 * 16)
            dve.wait_ge(norm[1]["cols"], CHUNKS)
            dve.tensor_copy(cn_w4r[:, :], cn_w[3][:, 0:1].broadcast_to([32, P]))
            dve.tensor_copy(gc_w3r[:, :], gc_w[2][:, 0:1].broadcast_to([32, P]))
            dve.tensor_scalar(sc[:, 0:1], arange[:, :], 0.3, None, ALU.mult)
            dve.tensor_scalar(sc[:, 2:3], gc_b[2][:, :], 0.5, None, ALU.mult)
            dve.tensor_scalar(sc[:, 3:4], cn_b[3][:, :], 0.5, None, ALU.mult).then_inc(net_consts, 1)
            dve.tensor_reduce(CTX[:, :], XNT[:, :].rearrange("p (b s) -> p b s", s=S), AX.X, ALU.add).then_inc(f["ctx"], 1)
            dve.wait_ge(f["e3"], 1)
            dve.tensor_scalar(AB[:, :], GA[:, :], 0.7, None, ALU.mult).then_inc(f["vec"], 1)
            dve.wait_ge(f["vec"], 1)
            dve.tensor_scalar(AB[:, :], AB[:, :], arange[:, 0:1], 0.1, ALU.mult, ALU.add).then_inc(f["ab"], 1)
            dve.wait_ge(f["ab"], 1)

            def couple(i, par_, last):
                for s in (0, 1):
                    after(dve, f["last"], 2 * i + s - 1)
                    dve.tensor_copy(UU[:, s, :], XNT[:, ds(2 * CW * i + CW * s, CW)]).then_inc(f["state"], 1)
                for cyc in range(CYCLES):
                    for s in (0, 1):
                        k = i * (2 * CYCLES) + 2 * cyc + s
                        dve.wait_ge(f["t4"], k + 1)
                        for b in (0, 1):
                            a = dve.tensor_scalar(TC[:, s, S * b:S * b + S], TC[:, s, S * b:S * b + S], sc[:, 0:1],
                                                  AB[:, ds(4 * i + 2 * s + b, 1)], ALU.mult, ALU.add)
                        a.then_inc(f["vec"], 1)
                        dve.wait_ge(f["vec"], 1 + 2 * k + 1)
                        dve.wait_ge(f["twist"], k + 1)
                        dve.tensor_tensor(TM[:, s, :], PS[2 * s + 1][:, 0, :], TC[:, s, :], ALU.mult).then_inc(f["vec"], 1)
                        dve.wait_ge(f["vec"], 1 + 2 * k + 2)
                        dve.tensor_tensor(UU[:, s, :], UU[:, s, :], TM[:, s, :], ALU.add).then_inc(f["state"], 1)
                for s in (0, 1):
                    dve.wait_ge(f["t5"], 2 * i + s + 1)
                    dve.wait_ge(f["z5"], 2 * i + s + 1)
                    dve.scalar_tensor_tensor(XN[:, ds(8 * i + 4 * s, CT), :].rearrange("p t d -> p (t d)"), TC[:, s, :], 1.0,
                                             HZ[:, s, :], ALU.add, ALU.mult).then_inc(f["gate"], 1)

            small(dve, CHUNKS // 2, couple)
            dve.wait_ge(L1.vec, 1)
            attention(L1, PT1)


SB = 1


def small(eng, count, step):
    step(0, 0, False)
    with eng.Fori(1, count) as n:
        step(n, 0, False)


_NATURAL = ["L0_attn_x", "L0_attn_W_qkv", "L0_attn_W_out", "L0_ffn_wg", "L0_ffn_b2", "L1_attn_bo", "L1_attn_denom_bias",
            "L1_ffn_cn_w1", "L1_ffn_cn_b1", "L1_ffn_cn_w2", "L1_ffn_cn_b2", "L1_ffn_cn_w3", "L1_ffn_cn_b3",
            "L1_ffn_cn_w4", "L1_ffn_cn_b4", "L1_ffn_gc_w1", "L1_ffn_gc_b1", "L1_ffn_gc_w2", "L1_ffn_gc_b2",
            "L1_ffn_gc_w3", "L1_ffn_gc_b3", "L1_ffn_adaptive_range"]


def host_arrays(inputs):
    a = {k: np.ascontiguousarray(inputs[k]) for k in _NATURAL}
    t = [np.ascontiguousarray(inputs[k]).T for k in ("L1_attn_Wq", "L1_attn_Wk", "L1_attn_Wv")]
    a["w_qkv1"] = np.ascontiguousarray(np.concatenate(t, axis=1))
    a["w_out1"] = np.ascontiguousarray(np.ascontiguousarray(inputs["L1_attn_Wo"]).T)
    a["b1_cols"] = np.ascontiguousarray(np.ascontiguousarray(inputs["L0_ffn_b1"]).reshape(EXPERTS * FC, P).T)
    a["L0_ffn_W1"] = np.ascontiguousarray(np.ascontiguousarray(inputs["L0_ffn_W1"]).transpose(1, 0, 2).reshape(D, -1))
    w2 = np.ascontiguousarray(inputs["L0_ffn_W2"]).reshape(EXPERTS * FC, P, D)
    a["L0_ffn_W2"] = np.ascontiguousarray(w2.transpose(1, 0, 2))
    a["consts"] = constants()
    return a


def kernel(**inputs):
    import concourse.bacc as _bacc
    from concourse.bass_utils import run_bass_kernel_spmd as _run

    arrays = host_arrays(inputs)
    nc = _bacc.Bacc("TRN2", target_bir_lowering=False, num_devices=1)
    d = {k: nc.dram_tensor(f"in_{k}_dram", a.shape, mybir.dt.from_np(a.dtype), kind="ExternalInput").ap()
         for k, a in arrays.items()}
    out = nc.dram_tensor("out_dram", (B, S, D), F32, kind="ExternalOutput").ap()
    two_blocks(nc, d, out)
    r = _run(nc, [{f"in_{k}_dram": a for k, a in arrays.items()}], core_ids=[0])
    return r.results[0]["out_dram"]
```

```python
from contextlib import ExitStack

import numpy as np

import concourse.bass as bass
from concourse import mybir

F32 = mybir.dt.float32
BF16 = mybir.dt.bfloat16
U32 = mybir.dt.uint32
ALU = mybir.AluOpType
ACT = mybir.ActivationFunctionType
AX = mybir.AxisListType

P = 128
B, S, D = 16, 256, 128
N = B * S
TILES = N // P
HEADS, HD = 16, 8
HG = 4
WINDOW = 32
QB = 32
JB = S // QB
EXPERTS, FF = 8, 512
FC = FF // P
CAPACITY = int(N / EXPERTS * 1.25) + 1
ET = 6
ER = -(-CAPACITY // ET)
EROWS = ET * ER
TRASH = EXPERTS * EROWS
CT = 4
CHUNKS = TILES // CT
CW = CT * P
CYCLES = 3
EPS = 1e-5
MASKED = -3.0e38
N_SECOND = 26
C2 = EROWS // 2

_AT = {}
_WIDTH = 0
for _name, _w in (("ident", 128), ("tri", 128), ("identrep", 128), ("onesbd", 32),
                  ("mask0", 64), ("qmask", HEADS), ("iota", 8), ("sign", 1), ("reset", 256)):
    _AT[_name] = (_WIDTH, _WIDTH + _w)
    _WIDTH += _w


def constants():
    c = np.zeros((P, _WIDTH), np.float32)
    p = np.arange(P)

    def put(name, a):
        c[:, _AT[name][0]:_AT[name][1]] = a

    put("ident", np.eye(P))
    put("tri", p[:, None] <= p[None, :])
    put("identrep", (p[:, None] % 32 == p[None, :] % 32) & (p[:, None] < 32))
    put("sign", np.where(p[:, None] // 32 % 3 == 0, 1, -1))
    put("onesbd", p[:, None] // 32 == np.arange(32)[None, :] // HD)
    q, k = (p % 32)[:, None], np.arange(32)[None, :]
    put("mask0", np.concatenate([np.where(k > q, 0, MASKED), np.where(k <= q, 0, MASKED)], 1))
    put("qmask", (p[:, None] // HD == np.arange(HEADS)[None, :]) / np.sqrt(np.float32(HD)))
    put("iota", np.arange(8)[None, :] - 8.0)
    put("reset", (np.arange(256) % TILES != 0)[None, :])
    return c


class Layer:

    def __init__(self, sem, name, rounds, window):
        self.name, self.window = name, window
        self.units = [(r, pair) for r in rounds for pair in (0, 1)]
        self.U = len(self.units)
        self.x_staged = sem(f"{name}_x_staged")
        self.qk_made = sem(f"{name}_qk_made")
        self.v_made = sem(f"{name}_v_made")
        self.k_ready = sem(f"{name}_k_ready")
        self.q_ready_pool = sem(f"{name}_q_ready_pool")
        self.q_ready = sem(f"{name}_q_ready")
        self.v_ready = sem(f"{name}_v_ready")
        self.scores_made = sem(f"{name}_scores_made")
        self.max_made = sem(f"{name}_max_made")
        self.shifted = sem(f"{name}_shifted")
        self.probs_made = sem(f"{name}_probs_made")
        self.turned = sem(f"{name}_turned")
        self.pv_made = sem(f"{name}_pv_made")
        self.divided = sem(f"{name}_divided")
        self.o_ready = sem(f"{name}_o_ready")
        self.out_made = sem(f"{name}_out_made")
        self.out_taken = sem(f"{name}_out_taken")
        self.largest_found = sem(f"{name}_largest_found")
        self.fin_ready = sem(f"{name}_fin_ready")

    def keys(self, j):
        return (max(0, 32 * (j - 1)), 64 if j else 32) if self.window else (0, 32 * (j + 1))

    def offsets(self, blocks):
        at, out = 0, []
        for j in blocks:
            out.append((j, at))
            at += self.keys(j)[1]
        return out, at


def after(eng, sem, value):
    if isinstance(value, int) and value <= 0:
        return
    eng.wait_ge(sem, value)


def each(eng, begin, end, step):
    step(begin, 0, 0, False)
    step(begin + 1, 1, 1, False)
    if end - begin > 4:
        with eng.Fori(begin + 2, end - 2, 2) as n:
            step(n, 0, 2, False)
            step(n + 1, 1, 2, False)
    step(end - 2, 0, 2, False)
    step(end - 1, 1, 2, True)


class Chain:

    def __init__(self, eng, sem, base=0):
        self.eng, self.sem, self.base, self.k = eng, sem, base, 0

    def link(self, ins):
        ins.then_inc(self.sem, 1)
        self.k += 1
        self.eng.wait_ge(self.sem, self.base + self.k)


def two_blocks(nc, d, out):
    ds = bass.ds
    with ExitStack() as ctx:
        def sb(name, shape, dt=F32):
            return ctx.enter_context(nc.sbuf_tensor(name, shape, dt))

        def sem(name):
            return ctx.enter_context(nc.semaphore(name))

        xin_rows = nc.dram_tensor("xin_rows", (TRASH, D), F32).ap()
        y_rows = nc.dram_tensor("y_rows", (TRASH + 1, D), F32).ap()
        x_dram = d["L0_attn_x"].rearrange("a (s p) d -> p (a s) d", p=P)
        out_dram = out.rearrange("a (s p) d -> p (a s) d", p=P)

        cf = sb("cf", [P, _WIDTH])
        const = {k: cf[:, a:b] for k, (a, b) in _AT.items()}
        identrep = sb("identrep", [P, P], BF16)
        mask0 = sb("mask0", [P, 64], BF16)
        tri = sb("tri", [P, P], BF16)
        ones = sb("ones", [P, P], BF16)
        zeros = sb("zeros", [P, D])
        powc = sb("powc", [P, CT])
        w_qkv0 = sb("w_qkv0", [P, 3 * D])
        w_out0 = sb("w_out0", [P, D])
        wg = sb("wg", [P, EXPERTS])
        b1 = sb("b1", [P, EXPERTS * FC])
        b2 = sb("b2", [P, EXPERTS, D])
        w_qkv1 = sb("w_qkv1", [P, 3 * D])
        w_out1 = sb("w_out1", [P, D])
        bo = sb("bo", [P, D])
        ebias = sb("ebias", [P, HG])
        cn_w1 = sb("cn_w1", [P, 128])
        cn_w2 = sb("cn_w2", [P, 64])
        cn_w3 = sb("cn_w3", [P, 64])
        cn_w4 = sb("cn_w4", [64, 1])
        cn_w4r = sb("cn_w4r", [64, 2, P])
        cn_b = [sb("cn_b1", [P, 1]), sb("cn_b2", [P, 1]), sb("cn_b3", [64, 1]), sb("cn_b4", [P, 1])]
        gc_w = [sb("gc_w1", [P, 64]), sb("gc_w2", [64, 32]), sb("gc_w3", [32, 1])]
        gc_w3r = sb("gc_w3r", [32, P])
        gc_b = [sb("gc_b1", [64, 1]), sb("gc_b2", [32, 1]), sb("gc_b3", [P, 1])]
        arange = sb("arange", [P, 1])

        X = sb("X", [P, TILES, D])
        XN = sb("XN", [P, TILES, D])
        XNT = sb("XNT", [P, N])
        BIG = sb("BIG", [P, 2 * HG * JB * S])
        SRES = BIG[:, 0:N].rearrange("p (t d) -> p t d", d=D)
        G = BIG[:, N:2 * N].rearrange("p (t d) -> p t d", d=D)
        PT0 = BIG[:, 2 * N:3 * N].rearrange("p (a g c) -> p a g c", a=2, g=HG)
        PT1 = BIG[:, :].rearrange("p (a g k q) -> p a g k q", a=2, g=HG, k=JB)

        XNS = sb("XNS", [P, 2, CT, D])
        XTS = sb("XTS", [P, 2, CW])
        ST = sb("ST", [P, 2, CT, 6])
        MV = sb("MV", [P, 2, CT, 2])
        VE = sb("VE", [P, 2, CT])
        RS = sb("RS", [P, 2, CT])
        GATES = sb("GATES", [P, 4 * CT * D])
        TH, SG = (GATES[:, 2 * CT * D * i:2 * CT * D * (i + 1)].rearrange("p (a t d) -> p a t d", a=2, t=CT) for i in (0, 1))
        OB = sb("OB", [P, 2, 2, D])
        LG = OB[:, 0, :, :].rearrange("p a (t e) -> p (a t) e", e=EXPERTS)
        RA, RB = (TH[:, 0, 2 * i:2 * i + 2, :].rearrange("p a (t e) -> p (a t) e", e=EXPERTS) for i in (0, 1))
        OH = SG[:, 0, 0:2, :].rearrange("p a (e t) -> p (a e) t", t=TILES)
        OHB = sb("OHB", [P, EXPERTS, TILES], BF16)
        CN, CS = (SG[:, i, 2:4, :].rearrange("p a c -> p (a c)") for i in (0, 1))
        R1 = sb("R1", [P, TILES])
        R2 = sb("R2", [P, TILES])
        R3 = sb("R3", [P, TILES])
        R4 = sb("R4", [P, TILES])
        PROB = sb("PROB", [P, TILES])
        SLOT = sb("SLOT", [P, TILES], U32)
        xT = sb("xT", [P, 2, S])
        DT = sb("DT", [P, S])
        RC = sb("RC", [P, JB, HG])
        qkT = sb("qkT", [P, 2, 2 * S])
        qx = sb("qx", [P, 2, HG, JB, HG, QB])
        Vbd = sb("Vbd", [P, 2, JB, P])
        MX = sb("MX", [P, 2, 2, JB])
        PR = sb("PR", [P, 2, 2, 480])
        RD = sb("RD", [P, 2, S])
        oT = sb("oT", [P, 2, S])
        W1s = BIG[:, N:N + 2 * FF].rearrange("p (a f) -> p a f", a=2)
        W2s = BIG[:, N + 2 * FF:N + 4 * FF].rearrange("p (a f d) -> p a f d", a=2, f=FC)
        EB = BIG[0:ER, N + 4 * FF:N + 4 * FF + 2 * ET * D].rearrange("p (a i d) -> p a i d", a=2, i=ET)
        EBT = BIG[:, 3 * N:3 * N + 2 * EROWS].rearrange("p (a c) -> p a c", a=2)
        HT = BIG[:, 3 * N + 2 * EROWS:3 * N + (2 + FC) * EROWS].rearrange("p (f c) -> p f c", f=FC)
        YB = GATES[0:ER, 0:2 * ET * D].rearrange("p (a i d) -> p a i d", a=2, i=ET)
        U, UT, TC, TM, hA = (BIG[:, 4 * CW * i:4 * CW * (i + 1)].rearrange("p (a c) -> p a c", a=4) for i in range(5))
        hB = BIG[:, 20 * CW:22 * CW].rearrange("p (a c) -> p a c", a=2)
        hC = BIG[0:64, 22 * CW:24 * CW].rearrange("p (a c) -> p a c", a=2)
        CTX = sb("CTX", [P, B])
        g1 = sb("g1", [64, B])
        g2 = sb("g2", [32, B])
        GA = sb("GA", [P, B])
        AB = sb("AB", [P, B])
        sc = sb("sc", [P, 4])

        def spread_values(copy, psV, par, heads, *func):
            for hh in heads:
                for jj in range(4):
                    src = psV[32 * jj:32 * jj + 32, 0:2 * D].rearrange("p (t g h d) -> p t g h d", t=2, g=HG, d=HD)[:, :, :, hh]
                    dst = Vbd[32 * hh:32 * hh + 32, par, :, :].rearrange("p (t j) (g h d) -> p t j g h d", j=4, g=HG, d=HD)
                    last = copy(dst[:, :, jj, :, hh], src, *func)
            return last

        PS = [ctx.enter_context(nc.psum_tensor(f"ps{i}", [P, 2, 512], F32)) for i in range(4)]

        consts_in = sem("consts_in")
        gate_in = sem("gate_in")
        x_in = [sem(f"x_in{c}") for c in range(4)]
        first_in = sem("first_in")
        second_in = sem("second_in")
        zeros_made = sem("zeros_made")
        pool_consts = sem("pool_consts")
        vector_consts = sem("vector_consts")
        vbd_zeroed = sem("vbd_zeroed")
        bias_made = sem("bias_made")
        net_zeroed = sem("net_zeroed")
        net_consts = sem("net_consts")
        zero_filled = sem("zero_filled")
        norm = [{s: sem(f"n{i}_{s}") for s in ("weighted", "tanh", "gated", "product", "added", "summed", "stats", "shifted",
                                               "scale", "rows", "turned", "staged", "cols", "kept", "logits",
                                               "logits_kept", "ctx")} for i in (0, 1)]
        route = {s: sem(f"r_{s}") for s in ("vec", "shifted", "exp", "onehot", "counts", "tail", "slots")}
        scattered = sem("scattered")
        gathered = [sem(f"gathered{c}") for c in range(CHUNKS)]
        rows_in = [sem(f"m_rows_in{i}") for i in (0, 1)]
        experts_in = [sem(f"m_experts_in{i}") for i in (0, 1)]
        y_stored = [sem(f"m_y_stored{i}") for i in (0, 1)]
        moe = {s: sem(f"m_{s}") for s in ("turned", "cols", "up", "gelu", "down", "y")}
        L0 = Layer(sem, "a0", [list(range(JB))], True)
        L1 = Layer(sem, "a1", [[7, 2, 0], [6, 4], [5, 3, 1]], False)
        ffn = {s: sem(f"f_{s}") for s in ("state", "h1", "g1", "h2", "g2", "h3", "g3", "h4", "t4", "vec", "last", "t5",
                                          "gate", "c1", "e1", "c2", "e2", "c3", "e3", "ab")}
        swapped = [sem(f"f_swapped{q}") for q in range(4)]
        stored = [sem(f"stored{i}") for i in (0, 1)]
        out_buffers_free = sem("out_buffers_free")
        turn_of = {}
        HALF = B // 2

        block = ctx.enter_context(nc.Block())

        def alone(eng):
            name = str(eng.engine).split(".")[-1]
            if name not in turn_of:
                turn_of[name] = sem(f"turn_{name}")
            eng.sem_inc(turn_of[name], 1)

        def even(n, par):
            return 8 * (n - par)

        @block.sync
        def _(sp):
            def col(a):
                return a.rearrange("(p a) -> p a", a=1)

            def everywhere(a):
                return a.partition_broadcast(P)

            for c in range(4):
                sp.dma_start(X[:, 8 * c:8 * c + 8, :], x_dram[:, 8 * c:8 * c + 8, :]).then_inc(x_in[c], 16)
                if c == 0:
                    sp.dma_start(cf[:, :], d["consts"]).then_inc(consts_in, 16)
                    sp.dma_start(wg[:, :], d["L0_ffn_wg"]).then_inc(gate_in, 16)
            for dst, src in ((w_qkv0[:, :], d["L0_attn_W_qkv"]), (w_out0[:, :], d["L0_attn_W_out"]),
                             (b1[:, :], d["b1_cols"]), (b2[:, :, :], everywhere(d["L0_ffn_b2"]))):
                sp.dma_start(dst, src).then_inc(first_in, 16)
            sp.wait_ge(zeros_made, 1)
            rows = xin_rows.rearrange("(p r) d -> p r d", p=ER)
            sp.dma_start(rows, zeros[0:ER, :].unsqueeze(1).broadcast_to([ER, TRASH // ER, D])).then_inc(zero_filled, 16)
            sp.dma_start(y_rows[TRASH:TRASH + 1, :], zeros[0:1, 0:D]).then_inc(zero_filled, 16)
            sp.wait_ge(net_zeroed, 2)
            bias = d["L1_attn_denom_bias"].rearrange("a h b c -> (a b c) h")
            second = [
                (w_qkv1[:, :], d["w_qkv1"]), (w_out1[:, :], d["w_out1"]), (bo[:, :], everywhere(d["L1_attn_bo"])),
                (cn_w1[:, :], d["L1_ffn_cn_w1"]), (cn_w2[:, :], d["L1_ffn_cn_w2"]),
                (cn_w3[0:64, 0:32], d["L1_ffn_cn_w3"]), (cn_w3[64:128, 32:64], d["L1_ffn_cn_w3"]),
                (cn_w4[0:32, :], d["L1_ffn_cn_w4"]), (cn_w4[32:64, :], d["L1_ffn_cn_w4"]),
                (cn_b[0][:, :], col(d["L1_ffn_cn_b1"])),
                (cn_b[1][0:64, :], col(d["L1_ffn_cn_b2"])), (cn_b[1][64:128, :], col(d["L1_ffn_cn_b2"])),
                (cn_b[2][0:32, :], col(d["L1_ffn_cn_b3"])), (cn_b[2][32:64, :], col(d["L1_ffn_cn_b3"])),
                (cn_b[3][:, :], everywhere(d["L1_ffn_cn_b4"])),
                (gc_w[0][:, :], d["L1_ffn_gc_w1"]), (gc_w[1][:, :], d["L1_ffn_gc_w2"]), (gc_w[2][:, :], d["L1_ffn_gc_w3"]),
                (gc_b[0][:, :], col(d["L1_ffn_gc_b1"])), (gc_b[1][:, :], col(d["L1_ffn_gc_b2"])),
                (gc_b[2][:, :], everywhere(d["L1_ffn_gc_b3"])), (arange[:, :], everywhere(d["L1_ffn_adaptive_range"])),
            ] + [(ebias[32 * g:32 * g + 32, :], bias[0:1, HG * g:HG * g + HG].broadcast_to([32, HG])) for g in range(HG)]
            assert len(second) == N_SECOND
            for dst, src in second:
                sp.dma_start(dst, src).then_inc(second_in, 16)

            w1_dram, w2_dram = d["L0_ffn_W1"], d["L0_ffn_W2"]
            xin_view = xin_rows.rearrange("(e r i) d -> r e i d", r=ER, i=ET)
            y_view = y_rows[0:TRASH, :].rearrange("(e r i) d -> r e i d", r=ER, i=ET)

            def store(e, par):
                sp.wait_ge(moe["y"], 2 * e + 2)
                sp.dma_start(y_view[:, ds(e, 1), :, :].rearrange("r a i d -> r (a i) d"), YB[:, par, :, :]
                             ).then_inc(y_stored[par], 16)

            def expert(e, par, age, last):
                after(sp, moe["down"], 2 * e - 2)
                sp.dma_start(W1s[:, par, :], w1_dram[:, ds(e * FF, FF)]).then_inc(experts_in[par], 16)
                sp.dma_start(W2s[:, par, :, :], w2_dram[:, ds(e * FC, FC), :]).then_inc(experts_in[par], 16)
                if age == 0:
                    sp.wait_ge(scattered, 16 * TILES)
                sp.dma_start(EB[:, par, :, :], xin_view[:, ds(e, 1), :, :].rearrange("r a i d -> r (a i) d")
                             ).then_inc(rows_in[par], 16)
                if age:
                    store(e - 1, 1 - par)
                if last:
                    store(e, par)

            each(sp, 0, EXPERTS, expert)

            for i in range(2):
                for cyc in range(CYCLES):
                    for q in range(4):
                        sp.wait_ge(ffn["state"], 16 * i + 4 * cyc + q + 1)
                        for h in (0, 1):
                            sp.dma_start(UT[64 * h:64 * h + 64, q, :], U[64 - 64 * h:128 - 64 * h, q, :]
                                         ).then_inc(swapped[q], 16)

            def keep(n, par, age, last):
                sp.wait_ge(L1.fin_ready, n + 1)
                sp.dma_start(out_dram[:, ds(2 * n, 2), :], OB[:, par, :, :]).then_inc(stored[par], 16)

            each(sp, 0, B, keep)
            for par in (0, 1):
                sp.wait_ge(stored[par], 16 * (B // 2))

        @block.gpsimd
        def _(pool):
            pool.memset(powc[:, :], -0.5).then_inc(pool_consts, 1)
            pool.memset(zeros[:, :], 0.0).then_inc(zeros_made, 1)
            pool.memset(cn_w3[:, :], 0.0).then_inc(net_zeroed, 1)
            pool.memset(cn_w4r[:, :, :], 0.0).then_inc(net_zeroed, 1)
            pool.memset(ones[:, :], 1.0).then_inc(pool_consts, 1)
            pool.memset(Vbd[:, :, :, :], 0.0).then_inc(vbd_zeroed, 1)
            pool.wait_ge(pool_consts, 2)

            def inverse_root(i, c):
                m, par = norm[i], c % 2
                pool.wait_ge(m["stats"], c + 1)
                pool.tensor_scalar(VE[:, par, :], MV[:, par, :, 1], EPS, None, ALU.add).then_inc(m["shifted"], 1)
                pool.wait_ge(m["shifted"], c + 1)
                after(pool, m["rows"], c - 1)
                pool.tensor_tensor(RS[:, par, :], VE[:, par, :], powc[:, :], ALU.pow).then_inc(m["scale"], 1)

            for c in range(CHUNKS):
                inverse_root(0, c)

            pool.wait_ge(route["slots"], 1)
            pool.wait_ge(zero_filled, 2 * 16)
            pool.wait_ge(norm[0]["kept"], CHUNKS)
            for t in range(TILES):
                pool.indirect_dma_start(xin_rows, bass.IndirectOffsetOnAxis(SLOT[:, t:t + 1], 0), XN[:, t, :], None,
                                        bounds_check=TRASH - 1, oob_is_err=False).then_inc(scattered, 16)

            for par in (0, 1):
                pool.wait_ge(y_stored[par], 16 * (EXPERTS // 2))

            def fetch(c):
                for t in range(CT * c, CT * c + CT):
                    pool.indirect_dma_start(G[:, t, :], None, y_rows, bass.IndirectOffsetOnAxis(SLOT[:, t:t + 1], 0)
                                            ).then_inc(gathered[c], 16)

            for c in range(CHUNKS):
                fetch(c)
            for c in range(CHUNKS):
                m, par = norm[1], c % 2
                pool.wait_ge(m["product"], c + 1)
                pool.tensor_tensor(X[:, CT * c:CT * c + CT, :], X[:, CT * c:CT * c + CT, :], SG[:, par, :, :], ALU.add
                                   ).then_inc(m["added"], 1)
                if c:
                    inverse_root(1, c - 1)
            inverse_root(1, CHUNKS - 1)

            A = L1

            def stage(n, par):
                after(pool, A.v_made, n - 1)
                pool.tensor_copy(xT[:, par, :], XNT[:, ds(n * S, S)]).then_inc(A.x_staged, 1)

            def widen(n, par):
                pool.wait_ge(A.k_ready, n + 1)
                after(pool, A.scores_made, A.U * n - A.U)
                alone(pool)
                for g in (2, 3):
                    for hh in range(HG):
                        h = HG * g + hh
                        q = pool.tensor_scalar(qx[:, par, g, :, hh, :],
                                               qkT[:, par, 0:S].rearrange("p (j q) -> p j q", q=QB),
                                               const["qmask"][:, h:h + 1], None, ALU.mult)
                q.then_inc(A.q_ready_pool, 1)

            def finish(n, par):
                pool.wait_ge(A.out_taken, n + 1)
                pool.tensor_tensor(SG[:, par, 0:2, :], TH[:, par, 0:2, :], XN[:, ds(2 * n, 2), :], ALU.mult
                                   ).then_inc(A.shifted, 1)
                pool.wait_ge(A.shifted, n + 1)
                pool.sem_inc(out_buffers_free, 1)
                after(pool, stored[par], 16 * (n // 2) if isinstance(n, int) else even(n, par))
                pool.tensor_tensor(OB[:, par, :, :], X[:, ds(2 * n, 2), :], SG[:, par, 0:2, :], ALU.add
                                   ).then_inc(A.fin_ready, 1)

            def attend(n, par, age, last):
                if age == 0:
                    stage(n, par)
                    widen(n, par)
                if not last:
                    stage(n + 1, 1 - par)
                    widen(n + 1, 1 - par)
                if age == 2:
                    finish(n - 2, par)
                if last:
                    finish(n - 1, 1 - par)
                    finish(n, par)

            pool.wait_ge(ffn["gate"], CHUNKS)
            pool.sem_inc(out_buffers_free, 2)
            each(pool, 0, B, attend)

        @block.tensor
        def _(pe):
            def turn_rows(i, c):
                m, par = norm[i], c % 2
                pe.wait_ge(m["rows"], c + 1)
                after(pe, m["cols"], c - 1)
                for t in range(CT):
                    last = pe.transpose(PS[0][:, par, P * t:P * t + P], XNS[:, par, t, :], const["ident"])
                last.then_inc(m["turned"], 1)

            def gate_logits(c):
                m, par = norm[0], c % 2
                pe.wait_ge(m["staged"], c + 1)
                after(pe, m["logits_kept"], c - 1)
                for t in range(CT):
                    last = pe.matmul(PS[1][:, par, 8 * t:8 * t + 8], XTS[:, par, P * t:P * t + P], wg[:, :],
                                     start=True, stop=True)
                last.then_inc(m["logits"], 1)

            pe.wait_ge(consts_in, 16)
            for c in range(CHUNKS + 1):
                if c < CHUNKS:
                    turn_rows(0, c)
                if c == 1:
                    pe.wait_ge(gate_in, 16)
                if c > 0:
                    gate_logits(c - 1)

            pe.wait_ge(pool_consts, 2)
            pe.wait_ge(vector_consts, 3)
            pe.wait_ge(route["onehot"], 1)
            ohb = OHB[:, :, :].rearrange("p e t -> p (e t)")
            pe.matmul(PS[2][:, 0, 0:256], tri[:, :], ohb, start=True, stop=True)
            pe.matmul(PS[2][:, 1, 0:256], ones[:, :], ohb, start=True, stop=True).then_inc(route["counts"], 1)
            pe.wait_ge(first_in, 4 * 16)
            pe.wait_ge(route["vec"], 12)

            def attention(A, w_qkv, w_out, begin, end):
                psS = [PS[0], PS[1]]
                psO, psQK, psOut, psV = PS[2][:, 0, :], PS[2][:, 1, :], PS[3][:, 0, :], PS[3][:, 1, :]

                def qkv(n, par):
                    pe.wait_ge(A.x_staged, n + 1)
                    after(pe, A.q_ready, (2 if A.window else 1) * n)
                    for i in (0, 1):
                        last = pe.matmul(psQK[:, i * S:(i + 1) * S], w_qkv[:, i * D:(i + 1) * D], xT[:, par, :],
                                         start=True, stop=True)
                    last.then_inc(A.qk_made, 1)
                    after(pe, A.v_ready, n)
                    for t in (0, 1):
                        last = pe.matmul(psV[:, D * t:D * t + D], xT[:, par, P * t:P * t + P], w_qkv[:, 2 * D:3 * D],
                                         start=True, stop=True)
                    last.then_inc(A.v_made, 1)

                def scores(n, par, u):
                    blocks, pair = A.units[u]
                    slot = u % 2
                    if u == 0:
                        pe.wait_ge(A.q_ready, 2 * n + 1 if A.window else n + 1)
                    if u == 1 and A.window:
                        pe.wait_ge(A.q_ready, 2 * n + 2)
                    if u == 1 and not A.window:
                        pe.wait_ge(A.q_ready_pool, n + 1)
                    after(pe, A.shifted if A.window else A.probs_made, A.U * n + u - 1)
                    for j, at in A.offsets(blocks)[0]:
                        k0, kn = A.keys(j)
                        for i in (0, 1):
                            pe.matmul(psS[slot][:, i, at:at + kn],
                                      qx[:, par, 2 * pair + i, j, :, :].rearrange("p h q -> p (h q)"),
                                      qkT[:, par, S + k0:S + k0 + kn], start=True, stop=False)
                        for i in (0, 1):
                            mk = mask0[:, 64 - kn if A.window else 32:64]
                            last = pe.matmul(psS[slot][:, i, at + kn - mk.shape[1]:at + kn], identrep[:, :],
                                             mk, start=False, stop=True)
                    last.then_inc(A.scores_made, 1)

                def values(n, par, key_blocks):
                    if key_blocks[0] == 0:
                        pe.wait_ge(A.turned, A.U * (n + 1))
                        pe.wait_ge(A.v_ready, n + 1)
                        after(pe, A.o_ready, n)
                    for kb in key_blocks:
                        qn = min(S - 32 * kb, 64 if A.window else S)
                        q0 = 32 * kb
                        for part in (0, 1):
                            for g in range(HG):
                                rhs = PT0[:, par, g, 64 * kb:64 * kb + qn] if A.window else PT1[:, par, g, kb, q0:S]
                                w = Vbd[:, par, kb, 32 * g:32 * g + 32] if part == 0 else const["onesbd"]
                                last = pe.matmul(psO[32 * g:32 * g + 32, part * S + q0:part * S + q0 + qn], w, rhs,
                                                 start=(kb == 0 and part == 0), stop=(kb == JB - 1),
                                                 skip_group_check=True, tile_position=(0, 32 * g))
                    if key_blocks[-1] == JB - 1:
                        last.then_inc(A.pv_made, 1)

                def project(n, par):
                    pe.wait_ge(A.o_ready, n + 1)
                    after(pe, A.out_taken, n)
                    for t in (0, 1):
                        last = pe.matmul(psOut[:, t * D:t * D + D], oT[:, par, t * P:t * P + P], w_out[:, :],
                                         start=True, stop=True)
                    last.then_inc(A.out_made, 1)

                def step(n, par, age, last):
                    if age == 0:
                        qkv(n, par)
                    for u in range(A.U):
                        scores(n, par, u)
                        if u == (0 if A.window else 1) and not last:
                            qkv(n + 1, 1 - par)
                        if u == 0 and age == 2:
                            project(n - 2, par)
                        if A.window and u == 1 and age:
                            values(n - 1, 1 - par, range(JB))
                        if not A.window and 0 < u < 5 and age:
                            values(n - 1, 1 - par, (range(1), range(1, 3), range(3, 5), range(5, JB))[u - 1])
                    if last:
                        project(n - 1, 1 - par)
                        values(n, par, range(JB))
                        project(n, par)

                each(pe, begin, end, step)

            attention(L0, w_qkv0, w_out0, 0, HALF)

            def expert(e, par, age, last):
                arrived = 16 * (e // 2 + 1) if isinstance(e, int) else even(e, par) + 16
                pe.wait_ge(rows_in[par], arrived)
                after(pe, moe["cols"], 2 * e)
                for i in range(ET):
                    t = pe.transpose(PS[0][:, i // 3, ER * (i % 3):ER * (i % 3) + ER], EB[:, par, i, :],
                                     const["ident"][0:ER, 0:ER])
                    if i % 3 == 2:
                        t.then_inc(moe["turned"], 1)
                pe.wait_ge(experts_in[par], 2 * arrived)
                for f in range(FC):
                    for h in (0, 1):
                        k = 2 * f + h
                        if f == 0:
                            pe.wait_ge(moe["cols"], 2 * e + h + 1)
                        after(pe, moe["gelu"], 8 * e + k - 3)
                        pe.matmul(PS[1 + (k % 4) // 2][:, k % 2, 0:C2], W1s[:, par, P * f:P * f + P],
                                  EBT[:, par, C2 * h:C2 * h + C2], start=True, stop=True).then_inc(moe["up"], 1)
                for h in (0, 1):
                    pe.wait_ge(moe["gelu"], 8 * e + 8)
                    after(pe, moe["y"], 2 * e + h - 1)
                    for i in range(3):
                        for f in range(FC):
                            at = C2 * h + ER * i
                            t = pe.matmul(PS[3][0:ER, h, D * i:D * i + D], HT[:, f, at:at + ER], W2s[:, par, f, :],
                                          start=(f == 0), stop=(f == FC - 1))
                    t.then_inc(moe["down"], 1)

            pe.wait_ge(L0.out_taken, HALF)
            each(pe, 0, EXPERTS, expert)
            pe.wait_ge(moe["y"], 2 * EXPERTS)
            attention(L0, w_qkv0, w_out0, HALF, B)

            for c in range(CHUNKS):
                turn_rows(1, c)

            f = ffn
            pe.wait_ge(net_consts, 1)
            pe.wait_ge(norm[1]["ctx"], CHUNKS)
            pe.matmul(PS[3][0:64, 0, 0:B], gc_w[0][:, :], CTX[:, :], start=True, stop=True).then_inc(f["c1"], 1)
            pe.wait_ge(f["e1"], 1)
            pe.matmul(PS[3][0:32, 0, 64:64 + B], gc_w[1][:, :], g1[:, :], start=True, stop=True).then_inc(f["c2"], 1)
            pe.wait_ge(f["e2"], 1)
            pe.matmul(PS[3][:, 0, 128:128 + B], gc_w3r[:, :], g2[:, :], start=True, stop=True).then_inc(f["c3"], 1)
            pe.wait_ge(f["ab"], 1)
            pe.wait_ge(norm[1]["cols"], CHUNKS)

            for i in range(2):
                for cyc in range(CYCLES):
                    k = CYCLES * i + cyc
                    for q in range(4):
                        pe.wait_ge(f["state"], 16 * i + 4 * cyc + q + 1)
                        pe.matmul(PS[2 * (q // 2)][:, q % 2, :], cn_w1[:, :], U[:, q, :], start=True, stop=True
                                  ).then_inc(f["h1"], 1)
                    if i and cyc == 0:
                        pe.wait_ge(f["gate"], 4)
                    for p in (0, 1):
                        pe.wait_ge(f["g1"], 4 * k + 2 * p + 2)
                        for s in (0, 1):
                            last = pe.matmul(PS[2 * p + 1][64 * s:64 * s + 64, 0, :], cn_w2[:, :], hA[:, 2 * p + s, :],
                                             start=True, stop=True, tile_position=(0, 64 * s))
                        last.then_inc(f["h2"], 1)
                    for p in (0, 1):
                        pe.wait_ge(f["g2"], 2 * k + p + 1)
                        pe.matmul(PS[2 * p + 1][0:64, 1, :], cn_w3[:, :], hB[:, p, :], start=True, stop=True
                                  ).then_inc(f["h3"], 1)
                    for p in (0, 1):
                        pe.wait_ge(f["g3"], 2 * k + p + 1)
                        for s in (0, 1):
                            pe.matmul(PS[2 * p][:, s, :], cn_w4r[:, s, :], hC[:, p, :], start=True, stop=True
                                      ).then_inc(f["h4"], 1)
                for q in range(4):
                    pe.wait_ge(f["state"], 16 * i + 13 + q)
                    for t in range(CT):
                        last = pe.transpose(PS[2 * (q // 2) + 1][:, q % 2, P * t:P * t + P], U[:, q, P * t:P * t + P],
                                            const["ident"])
                    last.then_inc(f["last"], 1)

            pe.wait_ge(ffn["gate"], CHUNKS)
            attention(L1, w_qkv1, w_out1, 0, B)

        @block.scalar
        def _(act):
            def keep_columns(i, c):
                m, par = norm[i], c % 2
                act.wait_ge(m["turned"], c + 1)
                if i == 0:
                    after(act, m["logits"], c - 1)
                    act.activation(XTS[:, par, :], PS[0][:, par, :], ACT.Copy).then_inc(m["staged"], 1)
                act.activation(XNT[:, CW * c:CW * c + CW], PS[0][:, par, :], ACT.Copy).then_inc(m["cols"], 1)
                if i == 0:
                    act.activation(XN[:, CT * c:CT * c + CT, :], XNS[:, par, :, :], ACT.Copy).then_inc(m["kept"], 1)

            for c in range(CHUNKS):
                keep_columns(0, c)
            act.wait_ge(norm[0]["cols"], CHUNKS)
            act.wait_ge(route["shifted"], 1)
            act.activation(RB[:, :, :], RA[:, :, :], ACT.Exp).then_inc(route["exp"], 1)

            def attention(A, begin, end):
                psS = [PS[0], PS[1]]
                psQK, psOut, psV = PS[2][:, 1, :], PS[3][:, 0, :], PS[3][:, 1, :]

                def stage(n, par):
                    if not A.window:
                        return
                    after(act, A.v_made, n - 1)
                    alone(act)
                    act.activation(xT[:, par, :], XNT[:, ds(n * S, S)], ACT.Copy).then_inc(A.x_staged, 1)

                def split(n, par, heads):
                    if heads[0] == 0:
                        act.wait_ge(A.qk_made, n + 1)
                        after(act, A.scores_made, A.U * n - A.U)
                        if A.window:
                            act.activation(qkT[:, par, S:2 * S], psQK[:, S:2 * S], ACT.Copy)
                        else:
                            act.activation(qkT[:, par, :], psQK[:, :], ACT.Copy).then_inc(A.k_ready, 1)
                    for h in heads:
                        q = act.activation(qx[:, par, h // HG, :, h % HG, :], psQK[:, 0:S].rearrange("p (j q) -> p j q", q=QB),
                                           ACT.Copy, scale=const["qmask"][:, h:h + 1])
                    if heads[-1] % 8 == 7:
                        q.then_inc(A.q_ready, 1)

                def probs(n, par, u):
                    blocks, pair = A.units[u]
                    slot = u % 2
                    cols, width = A.offsets(blocks)
                    if A.window:
                        act.wait_ge(A.shifted, A.U * n + u + 1)
                        act.activation(PR[:, slot, :, 0:width], PR[:, slot, :, 0:width], ACT.Exp).then_inc(A.probs_made, 1)
                        return
                    after(act, A.turned, A.U * n + u - 1)
                    act.wait_ge(A.max_made, A.U * n + u + 1)
                    for j, at in cols:
                        kn = A.keys(j)[1]
                        for g in (0, 1):
                            last = act.activation(PR[:, slot, g, at:at + kn], psS[slot][:, g, at:at + kn], ACT.Exp,
                                                  bias=MX[:, slot, g, j:j + 1])
                    last.then_inc(A.probs_made, 1)

                def spread(n, par, heads):
                    if heads[0] == 0:
                        act.wait_ge(A.v_made, n + 1)
                        after(act, A.pv_made, n - 1)
                    v = spread_values(act.activation, psV, par, heads, ACT.Copy)
                    if heads[-1] == HG - 1:
                        v.then_inc(A.v_ready, 1)

                def keep(n, par):
                    if not A.window:
                        return
                    act.wait_ge(A.out_made, n + 1)
                    alone(act)
                    act.activation(SRES[:, ds(2 * n, 2), :].rearrange("p t d -> p (t d)"), psOut[:, 0:S], ACT.Copy
                                   ).then_inc(A.out_taken, 1)

                def window_step(n, par, age, last):
                    if age == 0:
                        stage(n, par)
                        split(n, par, range(HEADS // 2))
                        split(n, par, range(HEADS // 2, HEADS))
                    if not last:
                        stage(n + 1, 1 - par)
                    probs(n, par, 0)
                    if not last:
                        split(n + 1, 1 - par, range(HEADS // 2))
                    if age == 2:
                        keep(n - 2, par)
                    probs(n, par, 1)
                    if not last:
                        split(n + 1, 1 - par, range(HEADS // 2, HEADS))
                    if last:
                        keep(n - 1, 1 - par)
                        keep(n, par)

                def causal_step(n, par, age, last):
                    if age == 0:
                        split(n, par, range(HEADS // 2))
                        spread(n, par, range(HG))
                    for u in range(A.U):
                        probs(n, par, u)
                        if not last and u in (2, 3, 4):
                            split(n + 1, 1 - par, (range(2), range(2, 5), range(5, 8))[u - 2])
                    if not last:
                        spread(n + 1, 1 - par, range(HG))

                each(act, begin, end, window_step if A.window else causal_step)

            act.wait_ge(vbd_zeroed, 1)
            attention(L0, 0, HALF)

            def expert(e, par, age, last):
                for f in range(FC):
                    for h in (0, 1):
                        k = 2 * f + h
                        act.wait_ge(moe["up"], 8 * e + k + 1)
                        if k == 0:
                            after(act, moe["down"], 2 * e)
                        alone(act)
                        act.activation(HT[:, f, C2 * h:C2 * h + C2], PS[1 + (k % 4) // 2][:, k % 2, 0:C2], ACT.Gelu,
                                       bias=b1[:, ds(FC * e + f, 1)]).then_inc(moe["gelu"], 1)

            each(act, 0, EXPERTS, expert)
            attention(L0, HALF, B)

            for c in range(CHUNKS + 2):
                m = norm[1]
                if c == 0:
                    act.wait_ge(second_in, 16 * N_SECOND)
                    act.activation(ebias[:, :], ebias[:, :], ACT.Exp).then_inc(bias_made, 1)
                if c < CHUNKS:
                    act.wait_ge(m["weighted"], c + 1)
                    after(act, m["gated"], c - 1)
                    act.activation(TH[:, c % 2, :, :], G[:, CT * c:CT * c + CT, :], ACT.Tanh).then_inc(m["tanh"], 1)
                if c > 1:
                    keep_columns(1, c - 2)

            f = ffn
            act.wait_ge(f["c1"], 1)
            act.activation(g1[:, :], PS[3][0:64, 0, 0:B], ACT.Gelu, bias=gc_b[0][:, :], scale=1.0 / S).then_inc(f["e1"], 1)
            act.wait_ge(f["c2"], 1)
            act.activation(g2[:, :], PS[3][0:32, 0, 64:64 + B], ACT.Gelu, bias=gc_b[1][:, :]).then_inc(f["e2"], 1)
            act.wait_ge(f["c3"], 1)
            act.wait_ge(net_consts, 1)
            act.activation(GA[:, :], PS[3][:, 0, 128:128 + B], ACT.Tanh, bias=sc[:, 2:3], scale=0.5).then_inc(f["e3"], 1)

            for i in range(2):
                for cyc in range(CYCLES):
                    k = CYCLES * i + cyc
                    for q in range(4):
                        act.wait_ge(f["h1"], 4 * k + q + 1)
                        act.activation(hA[:, q, :], PS[2 * (q // 2)][:, q % 2, :], ACT.Gelu, bias=cn_b[0][:, :]
                                       ).then_inc(f["g1"], 1)
                    for p in (0, 1):
                        act.wait_ge(f["h2"], 2 * k + p + 1)
                        act.activation(hB[:, p, :], PS[2 * p + 1][:, 0, :], ACT.Gelu, bias=cn_b[1][:, :]).then_inc(f["g2"], 1)
                    for p in (0, 1):
                        act.wait_ge(f["h3"], 2 * k + p + 1)
                        act.activation(hC[:, p, :], PS[2 * p + 1][0:64, 1, :], ACT.Gelu, bias=cn_b[2][:, :]
                                       ).then_inc(f["g3"], 1)
                    for q in range(4):
                        act.wait_ge(f["h4"], 4 * k + q + 1)
                        act.activation(TC[:, q, :], PS[2 * (q // 2)][:, q % 2, :], ACT.Tanh, bias=sc[:, 3:4], scale=0.5
                                       ).then_inc(f["t4"], 1)
                for q in range(4):
                    act.wait_ge(f["last"], 4 * i + q + 1)
                    z = PS[2 * (q // 2) + 1][:, q % 2, :]
                    act.activation(TC[:, q, :], z, ACT.Tanh, scale=0.5)
                    act.activation(TM[:, q, :], z, ACT.Copy, scale=0.5).then_inc(f["t5"], 1)
            attention(L1, 0, B)

        @block.vector
        def _(dve):
            def statistics(i, c):
                m, par = norm[i], c % 2
                for t in range(CT):
                    a = dve.bn_stats(ST[:, par, t, :], X[:, CT * c + t, :])
                a.then_inc(m["summed"], 1)
                dve.wait_ge(m["summed"], c + 1)
                for t in range(CT):
                    a = dve.bn_aggr(MV[:, par, t, :], ST[:, par, t, :])
                a.then_inc(m["stats"], 1)

            def normalise(i, c):
                m, par = norm[i], c % 2
                dve.wait_ge(m["scale"], c + 1)
                after(dve, m["turned"], c - 1)
                if i == 0:
                    after(dve, m["kept"], c - 1)
                for t in range(CT):
                    a = dve.tensor_scalar(XNS[:, par, t, :], X[:, CT * c + t, :], MV[:, par, t, 0:1], RS[:, par, t:t + 1],
                                          ALU.subtract, ALU.mult)
                a.then_inc(m["rows"], 1)

            for c in range(CHUNKS + 2):
                if c < CHUNKS:
                    if c % 2 == 0:
                        dve.wait_ge(x_in[c // 2], 16)
                    statistics(0, c)
                if c == 1:
                    dve.wait_ge(consts_in, 16)
                    dve.tensor_copy(identrep[:, :], const["identrep"]).then_inc(vector_consts, 1)
                    dve.tensor_copy(mask0[:, :], const["mask0"]).then_inc(vector_consts, 1)
                    dve.tensor_copy(tri[:, :], const["tri"]).then_inc(vector_consts, 1)
                if 0 < c <= CHUNKS:
                    normalise(0, c - 1)
                if c > 1:
                    dve.wait_ge(norm[0]["logits"], c - 1)
                    dve.tensor_copy(LG[:, CT * (c - 2):CT * (c - 1), :].rearrange("p t e -> p (t e)"),
                                    PS[1][:, c % 2, 0:CT * EXPERTS]).then_inc(norm[0]["logits_kept"], 1)

            r = Chain(dve, route["vec"])
            dve.wait_ge(norm[0]["logits_kept"], CHUNKS)

            def over_e(a):
                return a.unsqueeze(2).broadcast_to([P, TILES, EXPERTS])

            def over_t(a):
                return a.unsqueeze(1).broadcast_to([P, TILES, EXPERTS])

            r.link(dve.tensor_reduce(R1[:, :], LG[:, :, :], AX.X, ALU.max))
            dve.tensor_tensor(RA[:, :, :], LG[:, :, :], over_e(R1[:, :]), ALU.subtract).then_inc(route["shifted"], 1)
            dve.wait_ge(route["shifted"], 1)
            r.link(dve.tensor_scalar(LG[:, :, :], RA[:, :, :], 0.0, None, ALU.is_ge))
            r.link(dve.tensor_tensor(LG[:, :, :], LG[:, :, :], over_t(const["iota"]), ALU.mult))
            r.link(dve.tensor_reduce(R2[:, :], LG[:, :, :], AX.X, ALU.min))
            r.link(dve.tensor_tensor(OH[:, :, :].rearrange("p e t -> p t e"), over_t(const["iota"]), over_e(R2[:, :]),
                                     ALU.is_equal))
            dve.tensor_copy(OHB[:, :, :], OH[:, :, :]).then_inc(route["onehot"], 1)
            dve.wait_ge(route["exp"], 1)
            r.link(dve.tensor_reduce(R1[:, :], RB[:, :, :], AX.X, ALU.add))
            r.link(dve.reciprocal(PROB[:, :], R1[:, :]))
            dve.wait_ge(route["counts"], 1)
            r.link(dve.tensor_copy(CN[:, :], PS[2][:, 1, 0:256]))
            r.link(dve.tensor_tensor_scan(CS[:, :], const["reset"], CN[:, :], 0.0, ALU.mult, ALU.add))
            r.link(dve.tensor_tensor(CS[:, :], CS[:, :], CN[:, :], ALU.subtract))
            r.link(dve.tensor_tensor(CS[:, :], PS[2][:, 0, 0:256], CS[:, :], ALU.add))
            r.link(dve.tensor_tensor(CS[:, :], CS[:, :], OH[:, :, :].rearrange("p e t -> p (e t)"), ALU.mult))
            assert r.k == 12
            q = Chain(dve, route["tail"])
            q.link(dve.tensor_reduce(R1[:, :], CS[:, :].rearrange("p (e t) -> p t e", e=EXPERTS), AX.X, ALU.add))
            q.link(dve.tensor_scalar(R3[:, :], R2[:, :], float(EXPERTS), float(EROWS), ALU.add, ALU.mult))
            q.link(dve.tensor_tensor(R3[:, :], R3[:, :], R1[:, :], ALU.add))
            q.link(dve.tensor_scalar(R3[:, :], R3[:, :], -1.0 - TRASH, None, ALU.add))
            q.link(dve.tensor_scalar(R4[:, :], R1[:, :], float(CAPACITY), None, ALU.is_le))
            q.link(dve.tensor_tensor(R3[:, :], R3[:, :], R4[:, :], ALU.mult))
            q.link(dve.tensor_scalar(R3[:, :], R3[:, :], float(TRASH), None, ALU.add))
            dve.tensor_copy(SLOT[:, :], R3[:, :]).then_inc(route["slots"], 1)
            q.link(dve.tensor_scalar(PROB[:, :], PROB[:, :], 0.5, None, ALU.mult))

            def attention(A, begin, end):
                psS = [PS[0], PS[1]]
                psO, psOut, psV = PS[2][:, 0, :], PS[3][:, 0, :], PS[3][:, 1, :]

                def spread(n, par):
                    dve.wait_ge(A.v_made, n + 1)
                    after(dve, A.pv_made, n - 1)
                    spread_values(dve.tensor_copy, psV, par, range(HG)).then_inc(A.v_ready, 1)

                def largest(n, par, u):
                    blocks, pair = A.units[u]
                    slot = u % 2
                    cols, width = A.offsets(blocks)
                    dve.wait_ge(A.scores_made, A.U * n + u + 1)
                    if A.window:
                        dve.tensor_reduce(MX[:, slot, :, 0:1], psS[slot][:, :, 0:32], AX.X, ALU.max)
                        wide = psS[slot][:, :, 32:480].rearrange("p g (j k) -> p g j k", k=64)
                        dve.tensor_reduce(MX[:, slot, :, 1:JB], wide, AX.X, ALU.max).then_inc(A.largest_found, 1)
                        dve.wait_ge(A.largest_found, A.U * n + u + 1)
                        dve.tensor_tensor(PR[:, slot, :, 0:32], psS[slot][:, :, 0:32],
                                          MX[:, slot, :, 0:1].broadcast_to([P, 2, 32]), ALU.subtract)
                        for g in (0, 1):
                            a = dve.tensor_tensor(PR[:, slot, g, 32:480].rearrange("p (j k) -> p j k", k=64), wide[:, g],
                                                  MX[:, slot, g, 1:JB].unsqueeze(2).broadcast_to([P, JB - 1, 64]),
                                                  ALU.subtract)
                        a.then_inc(A.shifted, 1)
                    else:
                        after(dve, A.probs_made, A.U * n + u - 1)
                        for j, at in cols:
                            kn = A.keys(j)[1]
                            a = dve.tensor_reduce(MX[:, slot, :, j:j + 1], psS[slot][:, :, at:at + kn], AX.X, ALU.max,
                                                  negate=True)
                        a.then_inc(A.max_made, 1)

                def turn(n, par, u):
                    blocks, pair = A.units[u]
                    slot = u % 2
                    dve.wait_ge(A.probs_made, A.U * n + u + 1)
                    if u == 0:
                        after(dve, A.pv_made, n - 1)
                    for i in (0, 1):
                        g = 2 * pair + i
                        if A.window:
                            a = dve.transpose(PT0[:, par, g, 0:480], PR[:, slot, i, 0:480])
                        else:
                            for j, at in A.offsets(blocks)[0]:
                                a = dve.transpose(PT1[:, par, g, 0:j + 1, 32 * j:32 * j + 32],
                                                  PR[:, slot, i, at:at + 32 * (j + 1)].rearrange("p (k q) -> p k q", q=32))
                    a.then_inc(A.turned, 1)

                def divide(n, par):
                    ch = Chain(dve, A.divided, n * (3 if A.window else 4))
                    dve.wait_ge(A.pv_made, n + 1)
                    ch.link(dve.transpose(DT[:, :], psO[:, S:2 * S]))
                    den = DT[:, :].rearrange("p (j h d) -> p j h d", j=JB, d=HD)[:, :, :, 0]
                    if not A.window:
                        ch.link(dve.tensor_tensor(RC[:, :, :], den, ebias[:, :].unsqueeze(1).broadcast_to([P, JB, HG]),
                                                  ALU.add))
                        den = RC[:, :, :]
                    ch.link(dve.reciprocal(RC[:, :, :], den))
                    ch.link(dve.transpose(RD[:, par, :], RC[:, :, :].rearrange("p j h -> p (j h)").unsqueeze(2)
                                          .broadcast_to([P, JB * HG, HD])))
                    after(dve, A.out_made, n - 1)
                    dve.tensor_tensor(oT[:, par, :], psO[:, 0:S], RD[:, par, :], ALU.mult).then_inc(A.o_ready, 1)

                def take(n, par):
                    if A.window:
                        return
                    dve.wait_ge(A.out_made, n + 1)
                    dve.wait_ge(out_buffers_free, n + 1)
                    dve.tensor_tensor(TH[:, par, 0:2, :], psOut[:, 0:S].rearrange("p (t d) -> p t d", d=D),
                                      bo[:, :].unsqueeze(1).broadcast_to([P, 2, D]), ALU.add).then_inc(A.out_taken, 1)

                def step(n, par, age, last):
                    if A.window and age == 0:
                        spread(n, par)
                    for u in range(A.U):
                        largest(n, par, u)
                        if u > 0:
                            turn(n, par, u - 1)
                        elif age:
                            turn(n - 1, 1 - par, A.U - 1)
                        if u == (1 if A.window else 5) and age:
                            divide(n - 1, 1 - par)
                        if u == 2 and age == 2:
                            take(n - 2, par)
                    if A.window and not last:
                        spread(n + 1, 1 - par)
                    if last:
                        take(n - 1, 1 - par)
                        turn(n, par, A.U - 1)
                        divide(n, par)
                        take(n, par)

                each(dve, begin, end, step)

            dve.wait_ge(vbd_zeroed, 1)
            attention(L0, 0, HALF)

            def expert(e, par, age, last):
                for h in (0, 1):
                    dve.wait_ge(moe["turned"], 2 * e + h + 1)
                    after(dve, moe["up"], 8 * e - 8)
                    dve.tensor_copy(EBT[:, par, C2 * h:C2 * h + C2], PS[0][:, h, 0:C2]).then_inc(moe["cols"], 1)
                after(dve, y_stored[par], 16 * (e // 2) if isinstance(e, int) else even(e, par))
                for h in (0, 1):
                    dve.wait_ge(moe["down"], 2 * e + h + 1)
                    dve.tensor_tensor(YB[:, par, 3 * h:3 * h + 3, :], PS[3][0:ER, h, 0:3 * D].rearrange("p (i d) -> p i d", d=D),
                                      b2[0:ER, ds(e, 1), :].broadcast_to([ER, 3, D]), ALU.add).then_inc(moe["y"], 1)

            each(dve, 0, EXPERTS, expert)
            attention(L0, HALF, B)

            dve.wait_ge(second_in, 16 * N_SECOND)
            for s in (0, 1):
                dve.tensor_copy(cn_w4r[32 * s:32 * s + 32, s, :], cn_w4[32 * s:32 * s + 32, 0:1].broadcast_to([32, P]))
            dve.tensor_copy(gc_w3r[:, :], gc_w[2][:, 0:1].broadcast_to([32, P]))
            dve.tensor_scalar(sc[:, 0:1], arange[:, :], 0.3, const["sign"], ALU.mult, ALU.mult)
            dve.tensor_scalar(sc[:, 2:3], gc_b[2][:, :], 0.5, None, ALU.mult)
            dve.tensor_scalar(sc[:, 3:4], cn_b[3][:, :], 0.5, None, ALU.mult).then_inc(net_consts, 1)
            dve.wait_ge(L0.out_taken, B)
            m = norm[1]
            for c in range(CHUNKS + 4):
                if c < CHUNKS:
                    Gc = G[:, CT * c:CT * c + CT, :]
                    dve.wait_ge(gathered[c], 16 * CT)
                    dve.tensor_tensor(Gc, Gc, PROB[:, CT * c:CT * c + CT].unsqueeze(2).broadcast_to([P, CT, D]), ALU.mult
                                      ).then_inc(m["weighted"], 1)
                if 0 < c <= CHUNKS:
                    k, par = c - 1, (c - 1) % 2
                    dve.wait_ge(m["tanh"], k + 1)
                    after(dve, m["added"], k - 1)
                    dve.scalar_tensor_tensor(SG[:, par, :, :].rearrange("p t d -> p (t d)"),
                                             TH[:, par, :, :].rearrange("p t d -> p (t d)"), 1.0,
                                             G[:, CT * k:CT * k + CT, :].rearrange("p t d -> p (t d)"), ALU.add, ALU.mult
                                             ).then_inc(m["gated"], 1)
                    dve.wait_ge(m["gated"], k + 1)
                    dve.tensor_tensor(SG[:, par, :, :], SG[:, par, :, :], SRES[:, CT * k:CT * k + CT, :], ALU.mult
                                      ).then_inc(m["product"], 1)
                if 1 < c <= CHUNKS + 1:
                    dve.wait_ge(m["added"], c - 1)
                    statistics(1, c - 2)
                if 2 < c <= CHUNKS + 2:
                    normalise(1, c - 3)
                if 3 < c:
                    k = c - 4
                    dve.wait_ge(m["cols"], k + 1)
                    dve.tensor_reduce(CTX[:, 2 * k:2 * k + 2], XNT[:, CW * k:CW * k + CW].rearrange("p (b s) -> p b s", s=S),
                                      AX.X, ALU.add).then_inc(m["ctx"], 1)

            f = ffn
            dve.wait_ge(f["e3"], 1)
            ab = Chain(dve, f["ab"])
            dve.tensor_scalar(AB[:, :], GA[:, :], 0.7, None, ALU.mult).then_inc(f["vec"], 1)
            dve.wait_ge(f["vec"], 1)
            dve.tensor_scalar(AB[:, :], AB[:, :], arange[:, 0:1], 0.1, ALU.mult, ALU.add).then_inc(f["vec"], 1)
            dve.wait_ge(f["vec"], 2)
            dve.tensor_scalar(AB[:, :], AB[:, :], const["sign"], None, ALU.mult).then_inc(f["ab"], 1)
            dve.wait_ge(f["ab"], 1)
            dve.wait_ge(norm[1]["cols"], CHUNKS)

            for i in range(2):
                for q in range(4):
                    after(dve, f["last"], 4 * i + q - 3)
                    c0 = CW * (4 * i + q)
                    dve.tensor_copy(U[:, q, :], XNT[:, c0:c0 + CW]).then_inc(f["state"], 1)
                for cyc in range(CYCLES):
                    k = CYCLES * i + cyc
                    for q in range(4):
                        v = 2 + 2 * (4 * k + q)
                        dve.wait_ge(f["t4"], 4 * k + q + 1)
                        for b in (0, 1):
                            n = 2 * (4 * i + q) + b
                            a = dve.tensor_scalar(TC[:, q, S * b:S * b + S], TC[:, q, S * b:S * b + S], sc[:, 0:1],
                                                  AB[:, n:n + 1], ALU.mult, ALU.add)
                        a.then_inc(f["vec"], 1)
                        dve.wait_ge(f["vec"], v + 1)
                        dve.wait_ge(swapped[q], 32 * (k + 1))
                        dve.tensor_tensor(TM[:, q, :], UT[:, q, :], TC[:, q, :], ALU.mult).then_inc(f["vec"], 1)
                        dve.wait_ge(f["vec"], v + 2)
                        dve.tensor_tensor(U[:, q, :], U[:, q, :], TM[:, q, :], ALU.add).then_inc(f["state"], 1)
                for q in range(4):
                    dve.wait_ge(f["t5"], 4 * i + q + 1)
                    t0 = CT * (4 * i + q)
                    dve.scalar_tensor_tensor(XN[:, t0:t0 + CT, :].rearrange("p t d -> p (t d)"), TC[:, q, :], 1.0, TM[:, q, :],
                                             ALU.add, ALU.mult).then_inc(f["gate"], 1)

            dve.wait_ge(bias_made, 1)
            attention(L1, 0, B)


_NATURAL = ["L0_attn_x", "L0_attn_W_qkv", "L0_attn_W_out", "L0_ffn_wg", "L0_ffn_b2", "L1_attn_bo", "L1_attn_denom_bias",
            "L1_ffn_cn_w1", "L1_ffn_cn_b1", "L1_ffn_cn_w2", "L1_ffn_cn_b2", "L1_ffn_cn_w3", "L1_ffn_cn_b3",
            "L1_ffn_cn_w4", "L1_ffn_cn_b4", "L1_ffn_gc_w1", "L1_ffn_gc_b1", "L1_ffn_gc_w2", "L1_ffn_gc_b2",
            "L1_ffn_gc_w3", "L1_ffn_gc_b3", "L1_ffn_adaptive_range"]


def host_arrays(inputs):
    a = {k: np.ascontiguousarray(inputs[k]) for k in _NATURAL}
    t = [np.ascontiguousarray(inputs[k]).T for k in ("L1_attn_Wq", "L1_attn_Wk", "L1_attn_Wv")]
    a["w_qkv1"] = np.ascontiguousarray(np.concatenate(t, axis=1))
    a["w_out1"] = np.ascontiguousarray(np.ascontiguousarray(inputs["L1_attn_Wo"]).T)
    a["b1_cols"] = np.ascontiguousarray(np.ascontiguousarray(inputs["L0_ffn_b1"]).reshape(EXPERTS * FC, P).T)
    a["L0_ffn_W1"] = np.ascontiguousarray(np.ascontiguousarray(inputs["L0_ffn_W1"]).transpose(1, 0, 2).reshape(D, -1))
    w2 = np.ascontiguousarray(inputs["L0_ffn_W2"]).reshape(EXPERTS * FC, P, D)
    a["L0_ffn_W2"] = np.ascontiguousarray(w2.transpose(1, 0, 2))
    a["consts"] = constants()
    return a


def kernel(**inputs):
    import concourse.bacc as _bacc
    from concourse.bass_utils import run_bass_kernel_spmd as _run

    arrays = host_arrays(inputs)
    nc = _bacc.Bacc("TRN2", target_bir_lowering=False, num_devices=1)
    d = {k: nc.dram_tensor(f"in_{k}_dram", a.shape, mybir.dt.from_np(a.dtype), kind="ExternalInput").ap()
         for k, a in arrays.items()}
    out = nc.dram_tensor("out_dram", (B, S, D), F32, kind="ExternalOutput").ap()
    two_blocks(nc, d, out)
    r = _run(nc, [{f"in_{k}_dram": a for k, a in arrays.items()}], core_ids=[0])
    return r.results[0]["out_dram"]
```

```python
from contextlib import ExitStack

import numpy as np

import concourse.bass as bass
from concourse import mybir

F32 = mybir.dt.float32
BF16 = mybir.dt.bfloat16
U32 = mybir.dt.uint32
ALU = mybir.AluOpType
ACT = mybir.ActivationFunctionType
AX = mybir.AxisListType

P = 128
B, S, D = 16, 256, 128
N = B * S
TILES = N // P
HEADS, HD = 16, 8
HG = 4
WINDOW = 32
QB = 32
JB = S // QB
EXPERTS, FF = 8, 512
FC = FF // P
CAPACITY = int(N / EXPERTS * 1.25) + 1
ET = 6
ER = -(-CAPACITY // ET)
EROWS = ET * ER
TRASH = EXPERTS * EROWS
CT = 4
CHUNKS = TILES // CT
CW = CT * P
CYCLES = 3
EPS = 1e-5
MASKED = -3.0e38
ACT_HEADS, DVE_HEADS = 4, 7
BANKS = 4
N_SECOND = 26
C2 = EROWS // 2

_AT = {}
_WIDTH = 0
for _name, _w in (("ident", 128), ("tri", 128), ("identrep", 128), ("onesbd", 32), ("delta", 32),
                  ("mask0", 64), ("qmask", HEADS), ("iota", 8), ("sign", 1), ("reset", 256)):
    _AT[_name] = (_WIDTH, _WIDTH + _w)
    _WIDTH += _w


def constants():
    c = np.zeros((P, _WIDTH), np.float32)
    p = np.arange(P)

    def put(name, a):
        c[:, _AT[name][0]:_AT[name][1]] = a

    put("ident", np.eye(P))
    put("tri", p[:, None] <= p[None, :])
    put("identrep", (p[:, None] % 32 == p[None, :] % 32) & (p[:, None] < 32))
    put("sign", np.where(p[:, None] // 32 % 3 == 0, 1, -1))
    put("onesbd", p[:, None] // 32 == np.arange(32)[None, :] // HD)
    q, k = (p % 32)[:, None], np.arange(32)[None, :]
    put("delta", q == k)
    put("mask0", np.concatenate([np.where(k > q, 0, MASKED), np.where(k <= q, 0, MASKED)], 1))
    put("qmask", (p[:, None] // HD == np.arange(HEADS)[None, :]) / np.sqrt(np.float32(HD)))
    put("iota", np.arange(8)[None, :] - 8.0)
    put("reset", (np.arange(256) % TILES != 0)[None, :])
    return c


class Layer:

    def __init__(self, sem, name, rounds, window):
        self.name, self.window = name, window
        self.span = 2 if window else 1
        self.slots = BANKS // self.span
        self.units = [(r, g) for r in rounds for g in range(0, HG, self.span)]
        self.U = len(self.units)
        self.x_staged = sem(f"{name}_x_staged")
        self.qk_made = sem(f"{name}_qk_made")
        self.v_made = sem(f"{name}_v_made")
        self.k_ready = sem(f"{name}_k_ready")
        self.q_ready = sem(f"{name}_q_ready")
        self.v_ready = sem(f"{name}_v_ready")
        self.scores_made = sem(f"{name}_scores_made")
        self.shifted = sem(f"{name}_shifted")
        self.probs_made = sem(f"{name}_probs_made")
        self.turned = sem(f"{name}_turned")
        self.pv_made = sem(f"{name}_pv_made")
        self.divided = sem(f"{name}_divided")
        self.o_ready = sem(f"{name}_o_ready")
        self.out_made = sem(f"{name}_out_made")
        self.out_taken = sem(f"{name}_out_taken")
        if window:
            self.largest_found = sem(f"{name}_largest_found")
        else:
            self.q_ready_dve = sem(f"{name}_q_ready_dve")
            self.q_ready_pool = sem(f"{name}_q_ready_pool")
            self.max_made = sem(f"{name}_max_made")
            self.fin_ready = sem(f"{name}_fin_ready")
            self.pv_part = sem(f"{name}_pv_part")
            self.inverted = sem(f"{name}_inverted")
            self.diagonals_made = sem(f"{name}_diagonals_made")
            self.inverses_kept = sem(f"{name}_inverses_kept")

    def keys(self, j):
        return (max(0, 32 * (j - 1)), 64 if j else 32) if self.window else (0, 32 * (j + 1))

    def offsets(self, blocks):
        at, out = 0, []
        for j in blocks:
            out.append((j, at))
            at += self.keys(j)[1]
        return out, at


def after(eng, sem, value):
    if isinstance(value, int) and value <= 0:
        return
    eng.wait_ge(sem, value)


def each(eng, begin, end, step):
    step(begin, 0, 0, 2)
    step(begin + 1, 1, 1, 2)
    if end - begin > 4:
        with eng.Fori(begin + 2, end - 3, 2) as n:
            step(n, 0, 2, 2)
            step(n + 1, 1, 2, 2)
    step(end - 2, 0, 2, 1)
    step(end - 1, 1, 2, 0)


def net_steps():
    end = 2 * CYCLES
    for k in range(end + 1):
        if k == 0:
            order = "0load0 0load1 1load0 1load1 0first0 0first1 1first0 0second 1first1 0third 0fourth0 0fourth1"
        elif k % CYCLES == 0:
            order = ("0turn0 1second 0turn1 1third 0load0 0load1 0gate 0first0 1fourth0 0first1 1fourth1 0second 0third "
                     "0fourth0 1turn0 0fourth1 1turn1 1load0 1load1 1gate 1first0 1first1")
        else:
            order = ("0first0 1second 0first1 1third 0second 1fourth0 0third 1fourth1 0fourth0 1first0 0fourth1 1first1")
        for word in order.split():
            p, step = int(word[0]), word[1:].rstrip("01")
            s = int(word[-1]) if word[-1] in "01" else 0
            late = p == 1 and step in ("second", "third", "fourth")
            cycle = k - 1 if late or step in ("turn", "gate") else k
            if 0 <= cycle < end:
                yield step, p, cycle, s


def state_before(k, s):
    return 2 * (k + k // CYCLES) + s + 1


class Chain:

    def __init__(self, eng, sem, base=0):
        self.eng, self.sem, self.base, self.k = eng, sem, base, 0

    def link(self, ins):
        ins.then_inc(self.sem, 1)
        self.k += 1
        self.eng.wait_ge(self.sem, self.base + self.k)


def two_blocks(nc, d, out):
    ds = bass.ds
    with ExitStack() as ctx:
        def sb(name, shape, dt=F32):
            return ctx.enter_context(nc.sbuf_tensor(name, shape, dt))

        def sem(name):
            return ctx.enter_context(nc.semaphore(name))

        xin_rows = nc.dram_tensor("xin_rows", (TRASH, D), F32).ap()
        y_rows = nc.dram_tensor("y_rows", (TRASH + 1, D), F32).ap()
        x_dram = d["L0_attn_x"].rearrange("a (s p) d -> p (a s) d", p=P)
        out_dram = out.rearrange("a (s p) d -> p (a s) d", p=P)

        cf = sb("cf", [P, _WIDTH])
        const = {k: cf[:, a:b] for k, (a, b) in _AT.items()}
        identrep = sb("identrep", [P, P], BF16)
        mask0 = sb("mask0", [P, 64], BF16)
        tri = sb("tri", [P, P], BF16)
        ones = sb("ones", [P, P], BF16)
        zeros = sb("zeros", [P, D])
        powc = sb("powc", [P, CT])
        w_qkv0 = sb("w_qkv0", [P, 3 * D])
        w_out0 = sb("w_out0", [P, D])
        wg = sb("wg", [P, EXPERTS])
        b1 = sb("b1", [P, EXPERTS * FC])
        b2 = sb("b2", [P, EXPERTS, D])
        w_qkv1 = sb("w_qkv1", [P, 3 * D])
        w_out1 = sb("w_out1", [P, D])
        bo = sb("bo", [P, D])
        ebias = sb("ebias", [P, HG])
        cn_w1 = sb("cn_w1", [P, 128])
        cn_w2 = sb("cn_w2", [P, 64])
        cn_w3 = sb("cn_w3", [P, 64])
        cn_w4 = sb("cn_w4", [64, 1])
        cn_w4r = sb("cn_w4r", [64, 2, P])
        cn_b = [sb("cn_b1", [P, 1]), sb("cn_b2", [P, 1]), sb("cn_b3", [64, 1]), sb("cn_b4", [P, 1])]
        gc_w = [sb("gc_w1", [P, 64]), sb("gc_w2", [64, 32]), sb("gc_w3", [32, 1])]
        gc_w3r = sb("gc_w3r", [32, P])
        gc_b = [sb("gc_b1", [64, 1]), sb("gc_b2", [32, 1]), sb("gc_b3", [P, 1])]
        arange = sb("arange", [P, 1])

        X = sb("X", [P, TILES, D])
        XN = sb("XN", [P, TILES, D])
        XNT = sb("XNT", [P, N])
        BIG = sb("BIG", [P, 2 * HG * JB * S])
        SRES = BIG[:, 0:N].rearrange("p (t d) -> p t d", d=D)
        G = BIG[:, N:2 * N].rearrange("p (t d) -> p t d", d=D)
        PT0 = BIG[:, 2 * N:3 * N].rearrange("p (a g c) -> p a g c", a=2, g=HG)
        PT1 = BIG[:, :].rearrange("p (a g k q) -> p a g k q", a=2, g=HG, k=JB)

        XNS = sb("XNS", [P, 2, CT, D])
        XTS = sb("XTS", [P, 2, CW])
        ST = sb("ST", [P, 2, CT, 6])
        MV = sb("MV", [P, 2, CT, 2])
        VE = sb("VE", [P, 2, CT])
        RS = sb("RS", [P, 2, CT])
        GATES = sb("GATES", [P, 4 * CT * D])
        TH, SG = (GATES[:, 2 * CT * D * i:2 * CT * D * (i + 1)].rearrange("p (a t d) -> p a t d", a=2, t=CT) for i in (0, 1))
        OB = sb("OB", [P, 2, 2, D])
        LG = OB[:, 0, :, :].rearrange("p a (t e) -> p (a t) e", e=EXPERTS)
        RA, RB = (TH[:, 0, 2 * i:2 * i + 2, :].rearrange("p a (t e) -> p (a t) e", e=EXPERTS) for i in (0, 1))
        OH = SG[:, 0, 0:2, :].rearrange("p a (e t) -> p (a e) t", t=TILES)
        OHB = sb("OHB", [P, EXPERTS, TILES], BF16)
        CN, CS = (SG[:, i, 2:4, :].rearrange("p a c -> p (a c)") for i in (0, 1))
        R1 = sb("R1", [P, TILES])
        R2 = sb("R2", [P, TILES])
        R3 = sb("R3", [P, TILES])
        R4 = sb("R4", [P, TILES])
        PROB = sb("PROB", [P, TILES])
        SLOT = sb("SLOT", [P, TILES], U32)
        xT = sb("xT", [P, 2, S])
        DT = sb("DT", [P, S])
        RC = sb("RC", [P, JB, HG])
        SUMS = sb("SUMS", [P, 2, HG, JB])
        RSUM = sb("RSUM", [P, HG, JB])
        DIAG = [a.rearrange("p a b -> p (a b)").rearrange("p (g j q) -> p (g j) q", g=HG, j=JB)
                for a in (XNS[:, :, :, :].rearrange("p a t d -> p a (t d)"), XTS[:, :, :])]
        qkT = sb("qkT", [P, 2, 2 * S])
        qx = sb("qx", [P, 2, HG, JB, HG, QB])
        Vbd = sb("Vbd", [P, 2, JB, P])
        MX = sb("MX", [P, BANKS, JB])
        PR = sb("PR", [P, BANKS, 480])
        RD = sb("RD", [P, 2, S])
        oT = sb("oT", [P, 2, S])
        W1s = BIG[:, N:N + 2 * FF].rearrange("p (a f) -> p a f", a=2)
        W2s = BIG[:, N + 2 * FF:N + 4 * FF].rearrange("p (a f d) -> p a f d", a=2, f=FC)
        EB = BIG[0:ER, N + 4 * FF:N + 4 * FF + 2 * ET * D].rearrange("p (a i d) -> p a i d", a=2, i=ET)
        EBT = BIG[:, 3 * N:3 * N + 2 * EROWS].rearrange("p (a c) -> p a c", a=2)
        HT = BIG[:, 3 * N + 2 * EROWS:3 * N + (2 + FC) * EROWS].rearrange("p (f c) -> p f c", f=FC)
        YB = GATES[0:ER, 0:2 * ET * D].rearrange("p (a i d) -> p a i d", a=2, i=ET)
        U, UT, TC, TM, hA = (BIG[:, 4 * CW * i:4 * CW * (i + 1)].rearrange("p (a c) -> p a c", a=4) for i in range(5))
        hB = BIG[:, 20 * CW:22 * CW].rearrange("p (a c) -> p a c", a=2)
        hC = BIG[0:64, 22 * CW:24 * CW].rearrange("p (a c) -> p a c", a=2)
        CTX = sb("CTX", [P, B])
        g1 = sb("g1", [64, B])
        g2 = sb("g2", [32, B])
        GA = sb("GA", [P, B])
        AB = sb("AB", [P, B])
        sc = sb("sc", [P, 4])

        def spread_values(copy, psV, par, heads, blocks, *func):
            for hh in heads:
                for jj in blocks:
                    src = psV[32 * jj:32 * jj + 32, 0:2 * D].rearrange("p (t g h d) -> p t g h d", t=2, g=HG, d=HD)[:, :, :, hh]
                    dst = Vbd[32 * hh:32 * hh + 32, par, :, :].rearrange("p (t j) (g h d) -> p t j g h d", j=4, g=HG, d=HD)
                    last = copy(dst[:, :, jj, :, hh], src, *func)
            return last

        PS = [ctx.enter_context(nc.psum_tensor(f"ps{i}", [P, 2, 512], F32)) for i in range(4)]

        consts_in = sem("consts_in")
        gate_in = sem("gate_in")
        x_in = [sem(f"x_in{c}") for c in range(4)]
        first_in = sem("first_in")
        second_in = sem("second_in")
        zeros_made = sem("zeros_made")
        pool_consts = sem("pool_consts")
        vector_consts = sem("vector_consts")
        vbd_zeroed = sem("vbd_zeroed")
        bias_made = sem("bias_made")
        net_zeroed = sem("net_zeroed")
        net_consts = sem("net_consts")
        zero_filled = sem("zero_filled")
        norm = [{s: sem(f"n{i}_{s}") for s in ("summed", "stats", "shifted", "scale", "rows", "turned", "cols") + own}
                for i, own in enumerate((("staged", "kept", "logits", "logits_kept"),
                                         ("weighted", "product", "tanh", "gated", "added")))]
        route = {s: sem(f"r_{s}") for s in ("vec", "shifted", "exp", "onehot", "counts", "tail", "slots")}
        scattered = sem("scattered")
        gathered = [sem(f"gathered{c}") for c in range(CHUNKS)]
        rows_in = [sem(f"m_rows_in{i}") for i in (0, 1)]
        experts_in = [sem(f"m_experts_in{i}") for i in (0, 1)]
        y_stored = [sem(f"m_y_stored{i}") for i in (0, 1)]
        moe = {s: sem(f"m_{s}") for s in ("turned", "cols", "up", "gelu", "down", "y")}
        L0 = Layer(sem, "a0", [list(range(JB))], True)
        L1 = Layer(sem, "a1", [[7, 2, 0], [6, 4], [5, 3, 1]], False)
        ffn = [{s: sem(f"f{p}_{s}") for s in ("state", "h1", "g1", "h2", "g2", "h3", "g3", "h4", "t4", "vec", "last", "t5",
                                              "gate")} for p in (0, 1)]
        mean = {s: sem(f"g_{s}") for s in ("c1", "e1", "c2", "e2", "c3", "e3", "ab")}
        swapped = [sem(f"f_swapped{q}") for q in range(4)]
        stored = [sem(f"stored{i}") for i in (0, 1)]
        out_buffers_free = sem("out_buffers_free")
        turn_of = {}
        HALF = B // 2

        block = ctx.enter_context(nc.Block())

        def alone(eng):
            name = str(eng.engine).split(".")[-1]
            if name not in turn_of:
                turn_of[name] = sem(f"turn_{name}")
            eng.sem_inc(turn_of[name], 1)

        def even(n, par):
            return 8 * (n - par)

        @block.sync
        def _(sp):
            def col(a):
                return a.rearrange("(p a) -> p a", a=1)

            def everywhere(a):
                return a.partition_broadcast(P)

            for c in range(4):
                sp.dma_start(X[:, 8 * c:8 * c + 8, :], x_dram[:, 8 * c:8 * c + 8, :]).then_inc(x_in[c], 16)
                if c == 0:
                    sp.dma_start(cf[:, :], d["consts"]).then_inc(consts_in, 16)
                    sp.dma_start(wg[:, :], d["L0_ffn_wg"]).then_inc(gate_in, 16)
            for dst, src in ((w_qkv0[:, :], d["L0_attn_W_qkv"]), (w_out0[:, :], d["L0_attn_W_out"]),
                             (b1[:, :], d["b1_cols"]), (b2[:, :, :], everywhere(d["L0_ffn_b2"]))):
                sp.dma_start(dst, src).then_inc(first_in, 16)
            sp.wait_ge(zeros_made, 1)
            rows = xin_rows.rearrange("(p r) d -> p r d", p=ER)
            sp.dma_start(rows, zeros[0:ER, :].unsqueeze(1).broadcast_to([ER, TRASH // ER, D])).then_inc(zero_filled, 16)
            sp.dma_start(y_rows[TRASH:TRASH + 1, :], zeros[0:1, 0:D]).then_inc(zero_filled, 16)
            sp.wait_ge(net_zeroed, 2)
            bias = d["bias_by_head"]
            second = [
                (w_qkv1[:, :], d["w_qkv1"]), (w_out1[:, :], d["w_out1"]), (bo[:, :], everywhere(d["L1_attn_bo"])),
                (cn_w1[:, :], d["L1_ffn_cn_w1"]), (cn_w2[:, :], d["L1_ffn_cn_w2"]),
                (cn_w3[0:64, 0:32], d["L1_ffn_cn_w3"]), (cn_w3[64:128, 32:64], d["L1_ffn_cn_w3"]),
                (cn_w4[0:32, :], d["L1_ffn_cn_w4"]), (cn_w4[32:64, :], d["L1_ffn_cn_w4"]),
                (cn_b[0][:, :], col(d["L1_ffn_cn_b1"])),
                (cn_b[1][0:64, :], col(d["L1_ffn_cn_b2"])), (cn_b[1][64:128, :], col(d["L1_ffn_cn_b2"])),
                (cn_b[2][0:32, :], col(d["L1_ffn_cn_b3"])), (cn_b[2][32:64, :], col(d["L1_ffn_cn_b3"])),
                (cn_b[3][:, :], everywhere(d["L1_ffn_cn_b4"])),
                (gc_w[0][:, :], d["L1_ffn_gc_w1"]), (gc_w[1][:, :], d["L1_ffn_gc_w2"]), (gc_w[2][:, :], d["L1_ffn_gc_w3"]),
                (gc_b[0][:, :], col(d["L1_ffn_gc_b1"])), (gc_b[1][:, :], col(d["L1_ffn_gc_b2"])),
                (gc_b[2][:, :], everywhere(d["L1_ffn_gc_b3"])), (arange[:, :], everywhere(d["L1_ffn_adaptive_range"])),
            ] + [(ebias[32 * h:32 * h + 32, :], bias[h:h + 1, :].broadcast_to([32, HG])) for h in range(HG)]
            assert len(second) == N_SECOND
            for dst, src in second:
                sp.dma_start(dst, src).then_inc(second_in, 16)

            w1_dram, w2_dram = d["L0_ffn_W1"], d["L0_ffn_W2"]
            xin_view = xin_rows.rearrange("(e r i) d -> r e i d", r=ER, i=ET)
            y_view = y_rows[0:TRASH, :].rearrange("(e r i) d -> r e i d", r=ER, i=ET)

            def store(e, par):
                sp.wait_ge(moe["y"], 2 * e + 2)
                sp.dma_start(y_view[:, ds(e, 1), :, :].rearrange("r a i d -> r (a i) d"), YB[:, par, :, :]
                             ).then_inc(y_stored[par], 16)

            def expert(e, par, age, left):
                after(sp, moe["down"], 2 * e - 2)
                sp.dma_start(W1s[:, par, :], w1_dram[:, ds(e * FF, FF)]).then_inc(experts_in[par], 16)
                sp.dma_start(W2s[:, par, :, :], w2_dram[:, ds(e * FC, FC), :]).then_inc(experts_in[par], 16)
                if age == 0:
                    sp.wait_ge(scattered, 16 * TILES)
                sp.dma_start(EB[:, par, :, :], xin_view[:, ds(e, 1), :, :].rearrange("r a i d -> r (a i) d")
                             ).then_inc(rows_in[par], 16)
                if age:
                    store(e - 1, 1 - par)
                if not left:
                    store(e, par)

            each(sp, 0, EXPERTS, expert)

            def swap(p, k, s):
                q = 2 * p + s
                """The state's halves change places: its twist but for the signs, which the coupling carries."""
                sp.wait_ge(ffn[p]["state"], state_before(k, s))
                for h in (0, 1):
                    sp.dma_start(UT[64 * h:64 * h + 64, q, :], U[64 - 64 * h:128 - 64 * h, q, :]).then_inc(swapped[q], 16)

            for step, p, k, s in net_steps():
                if step == "load":
                    swap(p, k, s)
                if step == "fourth" and (k + 1) % CYCLES:
                    swap(p, k + 1, s)

            def keep(n, par, age, left):
                sp.wait_ge(L1.fin_ready, n + 1)
                sp.dma_start(out_dram[:, ds(2 * n, 2), :], OB[:, par, :, :]).then_inc(stored[par], 16)

            each(sp, 0, B, keep)
            for par in (0, 1):
                sp.wait_ge(stored[par], 16 * (B // 2))

        @block.gpsimd
        def _(pool):
            pool.memset(powc[:, :], -0.5).then_inc(pool_consts, 1)
            pool.memset(zeros[:, :], 0.0).then_inc(zeros_made, 1)
            pool.memset(cn_w3[:, :], 0.0).then_inc(net_zeroed, 1)
            pool.memset(cn_w4r[:, :, :], 0.0).then_inc(net_zeroed, 1)
            pool.memset(ones[:, :], 1.0).then_inc(pool_consts, 1)
            pool.memset(Vbd[:, :, :, :], 0.0).then_inc(vbd_zeroed, 1)
            pool.wait_ge(pool_consts, 2)

            def inverse_root(i, c):
                m, par = norm[i], c % 2
                pool.wait_ge(m["stats"], c + 1)
                pool.tensor_scalar(VE[:, par, :], MV[:, par, :, 1], EPS, None, ALU.add).then_inc(m["shifted"], 1)
                pool.wait_ge(m["shifted"], c + 1)
                after(pool, m["rows"], c - 1)
                pool.tensor_tensor(RS[:, par, :], VE[:, par, :], powc[:, :], ALU.pow).then_inc(m["scale"], 1)

            for c in range(CHUNKS):
                inverse_root(0, c)

            pool.wait_ge(route["slots"], 1)
            pool.wait_ge(zero_filled, 2 * 16)
            pool.wait_ge(norm[0]["kept"], CHUNKS)
            for t in range(TILES):
                pool.indirect_dma_start(xin_rows, bass.IndirectOffsetOnAxis(SLOT[:, t:t + 1], 0), XN[:, t, :], None,
                                        bounds_check=TRASH - 1, oob_is_err=False).then_inc(scattered, 16)

            for par in (0, 1):
                pool.wait_ge(y_stored[par], 16 * (EXPERTS // 2))

            def fetch(c):
                for t in range(CT * c, CT * c + CT):
                    pool.indirect_dma_start(G[:, t, :], None, y_rows, bass.IndirectOffsetOnAxis(SLOT[:, t:t + 1], 0)
                                            ).then_inc(gathered[c], 16)

            for c in range(CHUNKS):
                fetch(c)
            for c in range(CHUNKS):
                Gc = G[:, CT * c:CT * c + CT, :]
                pool.wait_ge(gathered[c], 16 * CT)
                pool.tensor_tensor(Gc, Gc, PROB[:, CT * c:CT * c + CT].unsqueeze(2).broadcast_to([P, CT, D]), ALU.mult
                                   ).then_inc(norm[1]["weighted"], 1)
                pool.wait_ge(norm[1]["weighted"], c + 1)
                pool.wait_ge(L0.out_taken, 2 * c + 2)
                Sc = SRES[:, CT * c:CT * c + CT, :]
                pool.tensor_tensor(Sc, Sc, Gc, ALU.mult).then_inc(norm[1]["product"], 1)
            for c in range(CHUNKS):
                m, par = norm[1], c % 2
                pool.wait_ge(m["gated"], c + 1)
                pool.tensor_tensor(X[:, CT * c:CT * c + CT, :], X[:, CT * c:CT * c + CT, :], SG[:, par, :, :], ALU.add
                                   ).then_inc(m["added"], 1)
                if c:
                    inverse_root(1, c - 1)
            inverse_root(1, CHUNKS - 1)

            A = L1

            def stage(n, par):
                after(pool, A.v_made, n - 1)
                pool.tensor_copy(xT[:, par, :], XNT[:, ds(n * S, S)]).then_inc(A.x_staged, 1)

            def widen(n, par):
                pool.wait_ge(A.k_ready, n + 1)
                after(pool, A.scores_made, A.U * n - A.U)
                alone(pool)
                for h in range(DVE_HEADS, HEADS):
                    q = pool.tensor_scalar(qx[:, par, h // HG, :, h % HG, :],
                                           qkT[:, par, 0:S].rearrange("p (j q) -> p j q", q=QB),
                                           const["qmask"][:, h:h + 1], None, ALU.mult)
                    if h in (2 * HG - 1, HEADS - 1):
                        q.then_inc(A.q_ready_pool, 1)

            def diagonals(n, par):
                pool.wait_ge(A.inverted, n + 1)
                after(pool, A.pv_made, n - 1)
                pool.tensor_tensor(DIAG[par], const["delta"].unsqueeze(1).broadcast_to([P, HG * JB, QB]),
                                   RSUM[:, :, :].rearrange("p g j -> p (g j)").unsqueeze(2).broadcast_to([P, HG * JB, QB]),
                                   ALU.mult).then_inc(A.diagonals_made, 1)

            def finish(n, par):
                pool.wait_ge(A.out_taken, n + 1)
                pool.tensor_tensor(SG[:, par, 0:2, :], TH[:, par, 0:2, :], XN[:, ds(2 * n, 2), :], ALU.mult
                                   ).then_inc(A.shifted, 1)
                pool.wait_ge(A.shifted, n + 1)
                pool.sem_inc(out_buffers_free, 1)
                after(pool, stored[par], 16 * (n // 2) if isinstance(n, int) else even(n, par))
                pool.tensor_tensor(OB[:, par, :, :], X[:, ds(2 * n, 2), :], SG[:, par, 0:2, :], ALU.add
                                   ).then_inc(A.fin_ready, 1)

            def attend(n, par, age, left):
                if age == 0:
                    stage(n, par)
                    for p in (0, 1):
                        pool.wait_ge(ffn[p]["gate"], CHUNKS // 2)
                if left:
                    stage(n + 1, 1 - par)
                if age:
                    diagonals(n - 1, 1 - par)
                if left:
                    widen(n + 1, 1 - par)
                if age == 2:
                    finish(n - 2, par)
                if not left:
                    diagonals(n, par)
                    finish(n - 1, 1 - par)
                    finish(n, par)

            pool.wait_ge(L0.v_made, B)
            pool.sem_inc(out_buffers_free, 2)
            each(pool, 0, B, attend)

        @block.tensor
        def _(pe):
            def turn_rows(i, c):
                m, par = norm[i], c % 2
                pe.wait_ge(m["rows"], c + 1)
                after(pe, m["cols"], c - 1)
                for t in range(CT):
                    last = pe.transpose(PS[0][:, par, P * t:P * t + P], XNS[:, par, t, :], const["ident"])
                last.then_inc(m["turned"], 1)

            def gate_logits(c):
                m, par = norm[0], c % 2
                pe.wait_ge(m["staged"], c + 1)
                after(pe, m["logits_kept"], c - 1)
                for t in range(CT):
                    last = pe.matmul(PS[1][:, par, 8 * t:8 * t + 8], XTS[:, par, P * t:P * t + P], wg[:, :],
                                     start=True, stop=True)
                last.then_inc(m["logits"], 1)

            pe.wait_ge(consts_in, 16)
            for c in range(CHUNKS + 1):
                if c < CHUNKS:
                    turn_rows(0, c)
                if c == 1:
                    pe.wait_ge(gate_in, 16)
                if c > 0:
                    gate_logits(c - 1)

            pe.wait_ge(pool_consts, 2)
            pe.wait_ge(vector_consts, 3)
            pe.wait_ge(first_in, 4 * 16)

            def attention(A, w_qkv, w_out, begin, end):
                psS = [PS[i // 2][:, i % 2, :] for i in range(BANKS)]
                psO, psQK, psOut, psV = PS[2][:, 0, :], PS[2][:, 1, :], PS[3][:, 0, :], PS[3][:, 1, :]

                def qkv(n, par):
                    pe.wait_ge(A.x_staged, n + 1)
                    after(pe, A.k_ready, n)
                    for i in (0, 1):
                        last = pe.matmul(psQK[:, i * S:(i + 1) * S], w_qkv[:, i * D:(i + 1) * D], xT[:, par, :],
                                         start=True, stop=True)
                    last.then_inc(A.qk_made, 1)
                    after(pe, A.v_ready, n)
                    for t in (0, 1):
                        last = pe.matmul(psV[:, D * t:D * t + D], xT[:, par, P * t:P * t + P], w_qkv[:, 2 * D:3 * D],
                                         start=True, stop=True)
                    last.then_inc(A.v_made, 1)

                def scores(n, par, u):
                    blocks, g0 = A.units[u]
                    slot = u % A.slots
                    if g0 == 0 and u < HG:
                        pe.wait_ge(A.q_ready, 2 * n + 1 if A.window else n + 1)
                    if g0 == 2 and u < HG and A.window:
                        pe.wait_ge(A.q_ready, 2 * n + 2)
                    if u in (1, 2) and not A.window:
                        pe.wait_ge(A.q_ready_dve, n + 1)
                        after(pe, A.q_ready_pool, 2 * n - 2 + u)
                    after(pe, A.shifted if A.window else A.probs_made, A.U * n + u + 1 - A.slots)
                    for i in range(A.span):
                        bank = psS[A.span * slot + i]
                        for j, at in A.offsets(blocks)[0]:
                            k0, kn = A.keys(j)
                            q = qx[:, par, g0 + i, j, :, :].rearrange("p h q -> p (h q)")
                            rows = kn if kn < 96 else P
                            for r in range(0, P, rows):
                                pe.matmul(bank[r:r + rows, at:at + kn], q[:, r:r + rows], qkT[:, par, S + k0:S + k0 + kn],
                                          start=(at == 0), stop=False, skip_group_check=True, tile_position=(0, r))
                        for j, at in A.offsets(blocks)[0]:
                            kn = A.keys(j)[1]
                            mk = mask0[:, 64 - kn if A.window else 32:64]
                            last = pe.matmul(bank[:, at + kn - mk.shape[1]:at + kn], identrep[:, :], mk,
                                             start=False, stop=True, skip_group_check=True)
                    last.then_inc(A.scores_made, 1)

                def values(n, par, key_blocks):
                    if key_blocks[0] == 0:
                        pe.wait_ge(A.turned, A.U * (n + 1))
                        pe.wait_ge(A.v_ready, n + 1)
                        after(pe, A.o_ready, n)
                    for kb in key_blocks:
                        qn = min(S - 32 * kb, 64 if A.window else S)
                        q0 = 32 * kb
                        for part in (0, 1) if A.window else (0,):
                            for g in range(HG):
                                rhs = PT0[:, par, g, 64 * kb:64 * kb + qn] if A.window else PT1[:, par, g, kb, q0:S]
                                w = Vbd[:, par, kb, 32 * g:32 * g + 32] if part == 0 else const["onesbd"]
                                last = pe.matmul(psO[32 * g:32 * g + 32, part * S + q0:part * S + q0 + qn], w, rhs,
                                                 start=(kb == 0 and part == 0), stop=(kb == JB - 1),
                                                 skip_group_check=True, tile_position=(0, 32 * g))
                    if key_blocks[-1] == JB - 1:
                        if not A.window:
                            pe.wait_ge(A.diagonals_made, n + 1)
                            for g in range(HG):
                                last = pe.matmul(psO[32 * g:32 * g + 32, S:2 * S], const["onesbd"],
                                                 DIAG[par][:, JB * g:JB * g + JB, :].rearrange("p j q -> p (j q)"),
                                                 start=False, stop=True, skip_group_check=True, tile_position=(0, 32 * g))
                        last.then_inc(A.pv_made, 1)
                    elif not A.window:
                        last.then_inc(A.pv_part, 1)

                def project(n, par):
                    pe.wait_ge(A.o_ready, n + 1)
                    after(pe, A.out_taken, n)
                    for t in (0, 1):
                        last = pe.matmul(psOut[:, t * D:t * D + D], oT[:, par, t * P:t * P + P], w_out[:, :],
                                         start=True, stop=True)
                    last.then_inc(A.out_made, 1)

                def count_tokens():
                    pe.wait_ge(route["onehot"], 1)
                    ohb = OHB[:, :, :].rearrange("p e t -> p (e t)")
                    pe.matmul(PS[1][:, 0, 0:256], tri[:, :], ohb, start=True, stop=True)
                    pe.matmul(PS[1][:, 1, 0:256], ones[:, :], ohb, start=True, stop=True).then_inc(route["counts"], 1)

                def step(n, par, age, left):
                    if age == 0:
                        qkv(n, par)
                    if age == 0 and A.window and begin == 0:
                        count_tokens()
                        pe.wait_ge(norm[0]["cols"], CHUNKS)
                    if age == 0 and not A.window:
                        pe.wait_ge(ffn[1]["gate"], CHUNKS // 2)
                    for u in range(A.U):
                        if age == 0 and A.window and begin == 0 and u == 1:
                            pe.wait_ge(route["vec"], 12)
                        scores(n, par, u)
                        if u == (0 if A.window else 2) and left:
                            qkv(n + 1, 1 - par)
                        if u == (0 if A.window else 1) and age == 2:
                            project(n - 2, par)
                        if A.window and u == 1 and age:
                            values(n - 1, 1 - par, range(JB))
                        if not A.window and 2 < u < 7 and age:
                            values(n - 1, 1 - par, (u - 3, u + 1))
                    if not left:
                        project(n - 1, 1 - par)
                        for blocks in (range(JB),) if A.window else ((jj, jj + 4) for jj in range(4)):
                            values(n, par, blocks)
                        project(n, par)

                each(pe, begin, end, step)

            attention(L0, w_qkv0, w_out0, 0, HALF)

            def expert(e, par, age, left):
                arrived = 16 * (e // 2 + 1) if isinstance(e, int) else even(e, par) + 16
                pe.wait_ge(rows_in[par], arrived)
                after(pe, moe["cols"], 2 * e)
                for i in range(ET):
                    t = pe.transpose(PS[0][:, i // 3, ER * (i % 3):ER * (i % 3) + ER], EB[:, par, i, :],
                                     const["ident"][0:ER, 0:ER])
                    if i % 3 == 2:
                        t.then_inc(moe["turned"], 1)
                pe.wait_ge(experts_in[par], 2 * arrived)
                for f in range(FC):
                    for h in (0, 1):
                        k = 2 * f + h
                        if f == 0:
                            pe.wait_ge(moe["cols"], 2 * e + h + 1)
                        after(pe, moe["gelu"], 8 * e + k - 3)
                        pe.matmul(PS[1 + (k % 4) // 2][:, k % 2, 0:C2], W1s[:, par, P * f:P * f + P],
                                  EBT[:, par, C2 * h:C2 * h + C2], start=True, stop=True).then_inc(moe["up"], 1)
                for h in (0, 1):
                    pe.wait_ge(moe["gelu"], 8 * e + 8)
                    after(pe, moe["y"], 2 * e + h - 1)
                    for i in range(3):
                        for f in range(FC):
                            at = C2 * h + ER * i
                            t = pe.matmul(PS[3][0:ER, h, D * i:D * i + D], HT[:, f, at:at + ER], W2s[:, par, f, :],
                                          start=(f == 0), stop=(f == FC - 1))
                    t.then_inc(moe["down"], 1)

            pe.wait_ge(L0.out_taken, HALF)
            each(pe, 0, EXPERTS, expert)
            pe.wait_ge(moe["y"], 2 * EXPERTS)
            attention(L0, w_qkv0, w_out0, HALF, B)

            for c in range(CHUNKS):
                turn_rows(1, c)

            pe.wait_ge(net_consts, 1)
            pe.wait_ge(norm[1]["cols"], CHUNKS)
            pe.matmul(PS[1][0:64, 0, 0:B], gc_w[0][:, :], CTX[:, :], start=True, stop=True).then_inc(mean["c1"], 1)
            for step, p, k, s in net_steps():
                f = ffn[p]
                if step == "first":
                    pe.wait_ge(f["state"], state_before(k, s))
                    pe.matmul(PS[2 - 2 * p][:, s, :], cn_w1[:, :], U[:, 2 * p + s, :], start=True, stop=True
                              ).then_inc(f["h1"], 1)
                elif step == "second":
                    pe.wait_ge(f["g1"], 2 * k + 2)
                    if k == CYCLES:
                        pe.wait_ge(f["gate"], 2)
                    for h in (0, 1):
                        last = pe.matmul(PS[3 - 2 * p][64 * h:64 * h + 64, 0, :], cn_w2[:, :], hA[:, 2 * p + h, :],
                                         start=True, stop=True, tile_position=(0, 64 * h))
                    last.then_inc(f["h2"], 1)
                elif step == "third":
                    pe.wait_ge(f["g2"], k + 1)
                    pe.matmul(PS[3 - 2 * p][0:64, 1, :], cn_w3[:, :], hB[:, p, :], start=True, stop=True
                              ).then_inc(f["h3"], 1)
                elif step == "fourth":
                    pe.wait_ge(f["g3"], k + 1)
                    pe.matmul(PS[2 - 2 * p][:, s, :], cn_w4r[:, s, :], hC[:, p, :], start=True, stop=True
                              ).then_inc(f["h4"], 1)
                elif step == "turn":
                    pe.wait_ge(f["state"], state_before(k, s) + 2)
                    for t in range(CT):
                        last = pe.transpose(PS[3 - 2 * p][:, s, P * t:P * t + P], U[:, 2 * p + s, P * t:P * t + P],
                                            const["ident"])
                    last.then_inc(f["last"], 1)
                if (step, p, k, s) == ("first", 0, 0, 0):
                    pe.wait_ge(mean["e1"], 1)
                    pe.matmul(PS[1][0:32, 0, 64:64 + B], gc_w[1][:, :], g1[:, :], start=True, stop=True
                              ).then_inc(mean["c2"], 1)
                if (step, p, k, s) == ("second", 0, 0, 0):
                    pe.wait_ge(mean["e2"], 1)
                    pe.matmul(PS[1][:, 0, 128:128 + B], gc_w3r[:, :], g2[:, :], start=True, stop=True
                              ).then_inc(mean["c3"], 1)

            pe.wait_ge(ffn[0]["gate"], CHUNKS // 2)
            attention(L1, w_qkv1, w_out1, 0, B)

        @block.scalar
        def _(act):
            def keep_columns(i, c):
                m, par = norm[i], c % 2
                act.wait_ge(m["turned"], c + 1)
                if i == 0:
                    after(act, m["logits"], c - 1)
                    act.activation(XTS[:, par, :], PS[0][:, par, :], ACT.Copy).then_inc(m["staged"], 1)
                if i == 0:
                    act.activation(XNT[:, CW * c:CW * c + CW], PS[0][:, par, :], ACT.Copy).then_inc(m["cols"], 1)
                else:
                    for b in (0, 1):
                        a = act.activation(XNT[:, CW * c + S * b:CW * c + S * b + S], PS[0][:, par, S * b:S * b + S], ACT.Copy,
                                           accum_out=CTX[:, 2 * c + b:2 * c + b + 1])
                    a.then_inc(m["cols"], 1)
                if i == 0:
                    act.activation(XN[:, CT * c:CT * c + CT, :], XNS[:, par, :, :], ACT.Copy).then_inc(m["kept"], 1)

            for c in range(CHUNKS):
                keep_columns(0, c)
            act.wait_ge(norm[0]["cols"], CHUNKS)
            def attention(A, begin, end):
                psS = [PS[i // 2][:, i % 2, :] for i in range(BANKS)]
                psQK, psOut, psV = PS[2][:, 1, :], PS[3][:, 0, :], PS[3][:, 1, :]

                def stage(n, par):
                    if not A.window:
                        return
                    after(act, A.v_made, n - 1)
                    alone(act)
                    act.activation(xT[:, par, :], XNT[:, ds(n * S, S)], ACT.Copy).then_inc(A.x_staged, 1)

                def split(n, par, heads):
                    if heads[0] == 0:
                        act.wait_ge(A.qk_made, n + 1)
                        after(act, A.scores_made, A.U * n - A.U)
                        act.activation(qkT[:, par, :], psQK[:, :], ACT.Copy).then_inc(A.k_ready, 1)
                        act.wait_ge(A.k_ready, n + 1)
                    for h in heads:
                        q = act.activation(qx[:, par, h // HG, :, h % HG, :], qkT[:, par, 0:S].rearrange("p (j q) -> p j q", q=QB),
                                           ACT.Copy, scale=const["qmask"][:, h:h + 1])
                        if h % 8 == 7 if A.window else h == ACT_HEADS - 1:
                            q.then_inc(A.q_ready, 1)

                def probs(n, par, u):
                    blocks, g = A.units[u]
                    slot = u % A.slots
                    cols, width = A.offsets(blocks)
                    if A.window:
                        act.wait_ge(A.shifted, A.U * n + u + 1)
                        both = PR[:, 2 * slot:2 * slot + 2, 0:width]
                        act.activation(both, both, ACT.Exp).then_inc(A.probs_made, 1)
                        return
                    after(act, A.turned, A.U * n + u + 1 - A.slots)
                    act.wait_ge(A.max_made, A.U * n + u + 1)
                    for j, at in cols:
                        kn = A.keys(j)[1]
                        last = act.activation(PR[:, slot, at:at + kn], psS[slot][:, at:at + kn], ACT.Exp,
                                              bias=MX[:, slot, j:j + 1], accum_out=SUMS[:, par, g, j:j + 1])
                    last.then_inc(A.probs_made, 1)

                def spread(n, par, jj):
                    if jj == 0:
                        act.wait_ge(A.v_made, n + 1)
                    if jj < 3:
                        after(act, A.pv_part, 3 * n - 5 + jj)
                    else:
                        after(act, A.pv_made, n - 1)
                    v = spread_values(act.activation, psV, par, range(HG), (jj,), ACT.Copy)
                    if jj == 3:
                        v.then_inc(A.v_ready, 1)

                def keep(n, par):
                    if not A.window:
                        return
                    act.wait_ge(A.out_made, n + 1)
                    alone(act)
                    act.activation(SRES[:, ds(2 * n, 2), :].rearrange("p t d -> p (t d)"), psOut[:, 0:S], ACT.Copy
                                   ).then_inc(A.out_taken, 1)

                def keep_inverses(n, par):
                    act.wait_ge(A.pv_made, n + 1)
                    after(act, A.o_ready, n - 1)
                    act.activation(RD[:, par, :], PS[2][:, 0, S:2 * S], ACT.Copy).then_inc(A.inverses_kept, 1)

                def step(n, par, age, left):
                    if A.window and age == 0:
                        stage(n, par)
                        stage(n + 1, 1 - par)
                    if A.window and age == 0 and begin == 0:
                        act.wait_ge(route["shifted"], 1)
                        act.activation(RB[:, :, :], RA[:, :, :], ACT.Exp).then_inc(route["exp"], 1)
                    if age == 0:
                        split(n, par, range(HEADS if A.window else ACT_HEADS))
                        if not A.window:
                            for jj in range(4):
                                spread(n, par, jj)
                    for u in range(A.U):
                        if A.window and left == 2 and u == 1:
                            stage(n + 2, par)
                        probs(n, par, u)
                        if A.window and left:
                            split(n + 1, 1 - par, range(8 * u, 8 * u + 8))
                        if A.window and u == 0 and age == 2:
                            keep(n - 2, par)
                        if not A.window and u == 7 and age:
                            keep_inverses(n - 1, 1 - par)
                        if not A.window and left and 2 < u < 3 + ACT_HEADS:
                            split(n + 1, 1 - par, range(u - 3, u - 2))
                        if not A.window and left and 3 < u < 8:
                            spread(n + 1, 1 - par, u - 4)
                    if not A.window and not left:
                        keep_inverses(n, par)
                    if not left:
                        keep(n - 1, 1 - par)
                        keep(n, par)

                each(act, begin, end, step)

            act.wait_ge(vbd_zeroed, 1)
            attention(L0, 0, HALF)

            def expert(e, par, age, left):
                for f in range(FC):
                    for h in (0, 1):
                        k = 2 * f + h
                        act.wait_ge(moe["up"], 8 * e + k + 1)
                        if k == 0:
                            after(act, moe["down"], 2 * e)
                        alone(act)
                        act.activation(HT[:, f, C2 * h:C2 * h + C2], PS[1 + (k % 4) // 2][:, k % 2, 0:C2], ACT.Gelu,
                                       bias=b1[:, ds(FC * e + f, 1)]).then_inc(moe["gelu"], 1)

            each(act, 0, EXPERTS, expert)
            attention(L0, HALF, B)

            for c in range(CHUNKS + 3):
                m = norm[1]
                if c == 0:
                    act.wait_ge(second_in, 16 * N_SECOND)
                    act.activation(ebias[:, :], ebias[:, :], ACT.Exp).then_inc(bias_made, 1)
                if c < CHUNKS:
                    act.wait_ge(m["weighted"], c + 1)
                    after(act, m["gated"], c - 1)
                    act.activation(TH[:, c % 2, :, :], G[:, CT * c:CT * c + CT, :], ACT.Tanh).then_inc(m["tanh"], 1)
                if c > 2:
                    keep_columns(1, c - 3)

            act.wait_ge(mean["c1"], 1)
            act.activation(g1[:, :], PS[1][0:64, 0, 0:B], ACT.Gelu, bias=gc_b[0][:, :], scale=1.0 / S
                           ).then_inc(mean["e1"], 1)
            act.wait_ge(net_consts, 1)
            for step, p, k, s in net_steps():
                f = ffn[p]
                if step == "first":
                    act.wait_ge(f["h1"], 2 * k + s + 1)
                    act.activation(hA[:, 2 * p + s, :], PS[2 - 2 * p][:, s, :], ACT.Gelu, bias=cn_b[0][:, :]
                                   ).then_inc(f["g1"], 1)
                elif step == "second":
                    act.wait_ge(f["h2"], k + 1)
                    act.activation(hB[:, p, :], PS[3 - 2 * p][:, 0, :], ACT.Gelu, bias=cn_b[1][:, :]).then_inc(f["g2"], 1)
                elif step == "third":
                    act.wait_ge(f["h3"], k + 1)
                    act.activation(hC[:, p, :], PS[3 - 2 * p][0:64, 1, :], ACT.Gelu, bias=cn_b[2][:, :]
                                   ).then_inc(f["g3"], 1)
                elif step == "fourth":
                    act.wait_ge(f["h4"], 2 * k + s + 1)
                    act.activation(TC[:, 2 * p + s, :], PS[2 - 2 * p][:, s, :], ACT.Tanh, bias=sc[:, 3:4], scale=0.5
                                   ).then_inc(f["t4"], 1)
                elif step == "turn":
                    act.wait_ge(f["last"], 2 * (k // CYCLES) + s + 1)
                    act.activation(TC[:, 2 * p + s, :], PS[3 - 2 * p][:, s, :], ACT.Tanh, scale=0.5)
                    act.activation(TM[:, 2 * p + s, :], PS[3 - 2 * p][:, s, :], ACT.Copy, scale=0.5
                                   ).then_inc(f["t5"], 1)
                if (step, p, k, s) == ("first", 0, 0, 0):
                    act.wait_ge(mean["c2"], 1)
                    act.activation(g2[:, :], PS[1][0:32, 0, 64:64 + B], ACT.Gelu, bias=gc_b[1][:, :]
                                   ).then_inc(mean["e2"], 1)
                if (step, p, k, s) == ("second", 0, 0, 0):
                    act.wait_ge(mean["c3"], 1)
                    act.activation(GA[:, :], PS[1][:, 0, 128:128 + B], ACT.Tanh, bias=sc[:, 2:3], scale=0.5
                                   ).then_inc(mean["e3"], 1)

            attention(L1, 0, B)

        @block.vector
        def _(dve):
            def statistics(i, c):
                m, par = norm[i], c % 2
                for t in range(CT):
                    a = dve.bn_stats(ST[:, par, t, :], X[:, CT * c + t, :])
                a.then_inc(m["summed"], 1)
                dve.wait_ge(m["summed"], c + 1)
                for t in range(CT):
                    a = dve.bn_aggr(MV[:, par, t, :], ST[:, par, t, :])
                a.then_inc(m["stats"], 1)

            def normalise(i, c):
                m, par = norm[i], c % 2
                dve.wait_ge(m["scale"], c + 1)
                after(dve, m["turned"], c - 1)
                if i == 0:
                    after(dve, m["kept"], c - 1)
                for t in range(CT):
                    a = dve.tensor_scalar(XNS[:, par, t, :], X[:, CT * c + t, :], MV[:, par, t, 0:1], RS[:, par, t:t + 1],
                                          ALU.subtract, ALU.mult)
                a.then_inc(m["rows"], 1)

            for c in range(CHUNKS + 3):
                if c < CHUNKS:
                    if c % 2 == 0:
                        dve.wait_ge(x_in[c // 2], 16)
                    statistics(0, c)
                if c == 1:
                    dve.wait_ge(consts_in, 16)
                    dve.tensor_copy(identrep[:, :], const["identrep"]).then_inc(vector_consts, 1)
                    dve.tensor_copy(mask0[:, :], const["mask0"]).then_inc(vector_consts, 1)
                    dve.tensor_copy(tri[:, :], const["tri"]).then_inc(vector_consts, 1)
                if 0 < c <= CHUNKS:
                    normalise(0, c - 1)
                if c > 2:
                    dve.wait_ge(norm[0]["logits"], c - 2)
                    dve.tensor_copy(LG[:, CT * (c - 3):CT * (c - 2), :].rearrange("p t e -> p (t e)"),
                                    PS[1][:, (c - 3) % 2, 0:CT * EXPERTS]).then_inc(norm[0]["logits_kept"], 1)

            r = Chain(dve, route["vec"])
            dve.wait_ge(norm[0]["logits_kept"], CHUNKS)

            def over_e(a):
                return a.unsqueeze(2).broadcast_to([P, TILES, EXPERTS])

            def over_t(a):
                return a.unsqueeze(1).broadcast_to([P, TILES, EXPERTS])

            r.link(dve.tensor_reduce(R1[:, :], LG[:, :, :], AX.X, ALU.max))
            dve.tensor_tensor(RA[:, :, :], LG[:, :, :], over_e(R1[:, :]), ALU.subtract).then_inc(route["shifted"], 1)
            dve.wait_ge(route["shifted"], 1)
            r.link(dve.tensor_scalar(LG[:, :, :], RA[:, :, :], 0.0, None, ALU.is_ge))
            r.link(dve.tensor_tensor(LG[:, :, :], LG[:, :, :], over_t(const["iota"]), ALU.mult))
            r.link(dve.tensor_reduce(R2[:, :], LG[:, :, :], AX.X, ALU.min))
            r.link(dve.tensor_tensor(OH[:, :, :].rearrange("p e t -> p t e"), over_t(const["iota"]), over_e(R2[:, :]),
                                     ALU.is_equal))
            dve.tensor_copy(OHB[:, :, :], OH[:, :, :]).then_inc(route["onehot"], 1)
            dve.wait_ge(route["exp"], 1)
            r.link(dve.tensor_reduce(R1[:, :], RB[:, :, :], AX.X, ALU.add))
            r.link(dve.reciprocal(PROB[:, :], R1[:, :]))
            dve.wait_ge(route["counts"], 1)
            r.link(dve.tensor_copy(CN[:, :], PS[1][:, 1, 0:256]))
            r.link(dve.tensor_tensor_scan(CS[:, :], const["reset"], CN[:, :], 0.0, ALU.mult, ALU.add))
            r.link(dve.tensor_tensor(CS[:, :], CS[:, :], CN[:, :], ALU.subtract))
            r.link(dve.tensor_tensor(CS[:, :], PS[1][:, 0, 0:256], CS[:, :], ALU.add))
            r.link(dve.tensor_tensor(CS[:, :], CS[:, :], OH[:, :, :].rearrange("p e t -> p (e t)"), ALU.mult))
            assert r.k == 12
            q = Chain(dve, route["tail"])
            q.link(dve.tensor_reduce(R1[:, :], CS[:, :].rearrange("p (e t) -> p t e", e=EXPERTS), AX.X, ALU.add))
            q.link(dve.tensor_scalar(R3[:, :], R2[:, :], float(EXPERTS), float(EROWS), ALU.add, ALU.mult))
            q.link(dve.tensor_tensor(R3[:, :], R3[:, :], R1[:, :], ALU.add))
            q.link(dve.tensor_scalar(R3[:, :], R3[:, :], -1.0 - TRASH, None, ALU.add))
            q.link(dve.tensor_scalar(R4[:, :], R1[:, :], float(CAPACITY), None, ALU.is_le))
            q.link(dve.tensor_tensor(R3[:, :], R3[:, :], R4[:, :], ALU.mult))
            q.link(dve.tensor_scalar(R3[:, :], R3[:, :], float(TRASH), None, ALU.add))
            dve.tensor_copy(SLOT[:, :], R3[:, :]).then_inc(route["slots"], 1)
            q.link(dve.tensor_scalar(PROB[:, :], PROB[:, :], 0.5, None, ALU.mult))

            def attention(A, begin, end):
                psS = [PS[i // 2][:, i % 2, :] for i in range(BANKS)]
                psO, psOut, psV = PS[2][:, 0, :], PS[3][:, 0, :], PS[3][:, 1, :]

                def spread(n, par, heads):
                    if heads[0] == 0:
                        dve.wait_ge(A.v_made, n + 1)
                        after(dve, A.pv_made, n - 1)
                    v = spread_values(dve.tensor_copy, psV, par, heads, range(4))
                    if heads[-1] == HG - 1:
                        v.then_inc(A.v_ready, 1)

                def largest(n, par, u):
                    blocks, g = A.units[u]
                    slot = u % A.slots
                    cols, width = A.offsets(blocks)
                    dve.wait_ge(A.scores_made, A.U * n + u + 1)
                    if A.window:
                        both = PS[slot]
                        top = MX[:, 2 * slot:2 * slot + 2, :]
                        wide = both[:, :, 32:480].rearrange("p g (j k) -> p g j k", k=64)
                        dve.tensor_reduce(top[:, :, 0:1], both[:, :, 0:32], AX.X, ALU.max)
                        dve.tensor_reduce(top[:, :, 1:JB], wide, AX.X, ALU.max).then_inc(A.largest_found, 1)
                        dve.wait_ge(A.largest_found, A.U * n + u + 1)
                        dve.tensor_tensor(PR[:, 2 * slot:2 * slot + 2, 0:32], both[:, :, 0:32],
                                          top[:, :, 0:1].broadcast_to([P, 2, 32]), ALU.subtract)
                        for i in (0, 1):
                            a = dve.tensor_tensor(PR[:, 2 * slot + i, 32:480].rearrange("p (j k) -> p j k", k=64), wide[:, i],
                                                  top[:, i, 1:JB].unsqueeze(2).broadcast_to([P, JB - 1, 64]), ALU.subtract)
                        a.then_inc(A.shifted, 1)
                    else:
                        after(dve, A.probs_made, A.U * n + u + 1 - A.slots)
                        for j, at in cols:
                            kn = A.keys(j)[1]
                            a = dve.tensor_reduce(MX[:, slot, j:j + 1], psS[slot][:, at:at + kn], AX.X, ALU.max, negate=True)
                        a.then_inc(A.max_made, 1)

                def turn(n, par, u):
                    blocks, g = A.units[u]
                    slot = u % A.slots
                    dve.wait_ge(A.probs_made, A.U * n + u + 1)
                    if u == 0:
                        after(dve, A.pv_made, n - 1)
                    if A.window:
                        for i in (0, 1):
                            a = dve.transpose(PT0[:, par, g + i, 0:480], PR[:, 2 * slot + i, 0:480])
                    else:
                        for j, at in A.offsets(blocks)[0]:
                            a = dve.transpose(PT1[:, par, g, 0:j + 1, 32 * j:32 * j + 32],
                                              PR[:, slot, at:at + 32 * (j + 1)].rearrange("p (k q) -> p k q", q=32))
                    a.then_inc(A.turned, 1)

                def invert(n, par, part):
                    if part == 0:
                        dve.wait_ge(A.probs_made, A.U * n + A.U)
                        after(dve, A.diagonals_made, n)
                        dve.tensor_tensor(RSUM[:, :, :], SUMS[:, par, :, :],
                                          ebias[:, :].unsqueeze(2).broadcast_to([P, HG, JB]), ALU.add).then_inc(A.divided, 1)
                    else:
                        dve.wait_ge(A.divided, n + 1)
                        dve.reciprocal(RSUM[:, :, :], RSUM[:, :, :]).then_inc(A.inverted, 1)

                def divide(n, par, part):
                    done = 4 * n + part
                    if part == 0:
                        dve.wait_ge(A.pv_made, n + 1)
                        dve.transpose(DT[:, :], psO[:, S:2 * S]).then_inc(A.divided, 1)
                    if part == 1:
                        den = DT[:, :].rearrange("p (j h d) -> p j h d", j=JB, d=HD)[:, :, :, 0]
                        dve.wait_ge(A.divided, done)
                        dve.tensor_copy(RC[:, :, :], den).then_inc(A.divided, 1)
                    if part == 2:
                        dve.wait_ge(A.divided, done)
                        dve.reciprocal(RC[:, :, :], RC[:, :, :]).then_inc(A.divided, 1)
                    if part == 3:
                        dve.wait_ge(A.divided, done)
                        dve.transpose(RD[:, par, :], RC[:, :, :].rearrange("p j h -> p (j h)").unsqueeze(2)
                                      .broadcast_to([P, JB * HG, HD])).then_inc(A.divided, 1)
                    if part == 4:
                        dve.wait_ge(A.divided, done)
                        scale(n, par)

                def scale(n, par):
                    dve.wait_ge(A.pv_made if A.window else A.inverses_kept, n + 1)
                    after(dve, A.out_made, n - 1)
                    dve.tensor_tensor(oT[:, par, :], psO[:, 0:S], RD[:, par, :], ALU.mult).then_inc(A.o_ready, 1)

                def take(n, par):
                    if A.window:
                        return
                    dve.wait_ge(A.out_made, n + 1)
                    dve.wait_ge(out_buffers_free, n + 1)
                    dve.tensor_tensor(TH[:, par, 0:2, :], psOut[:, 0:S].rearrange("p (t d) -> p t d", d=D),
                                      bo[:, :].unsqueeze(1).broadcast_to([P, 2, D]), ALU.add).then_inc(A.out_taken, 1)

                def widen(n, par, heads):
                    dve.wait_ge(A.k_ready, n + 1)
                    alone(dve)
                    for h in heads:
                        q = dve.tensor_scalar(qx[:, par, h // HG, :, h % HG, :],
                                              qkT[:, par, 0:S].rearrange("p (j q) -> p j q", q=QB),
                                              const["qmask"][:, h:h + 1], None, ALU.mult)
                    return q

                def step(n, par, age, left):
                    if A.window and age == 0:
                        spread(n, par, range(HG))
                    if not A.window and age == 0:
                        widen(n, par, range(ACT_HEADS, HEADS)).then_inc(A.q_ready_dve, 1)
                    lag = 1 if A.window else 2
                    for u in range(A.U):
                        largest(n, par, u)
                        if not A.window and u == 8 and age:
                            scale(n - 1, 1 - par)
                        if u >= lag:
                            turn(n, par, u - lag)
                        elif age:
                            turn(n - 1, 1 - par, A.U - lag + u)
                        if not A.window and u in (1, 2) and age:
                            invert(n - 1, 1 - par, u - 1)
                        if u == 4 and age == 2:
                            take(n - 2, par)
                        if not A.window and u == 6 and left:
                            widen(n + 1, 1 - par, range(ACT_HEADS, DVE_HEADS)).then_inc(A.q_ready_dve, 1)
                    if A.window:
                        for part in range(5):
                            if age:
                                divide(n - 1, 1 - par, part)
                            if left and part < HG:
                                spread(n + 1, 1 - par, range(part, part + 1))
                    if not left:
                        take(n - 1, 1 - par)
                        for u in range(A.U - lag, A.U):
                            turn(n, par, u)
                        if A.window:
                            for part in range(5):
                                divide(n, par, part)
                        else:
                            for part in (0, 1):
                                invert(n, par, part)
                            scale(n, par)
                        take(n, par)

                each(dve, begin, end, step)

            dve.wait_ge(vbd_zeroed, 1)
            attention(L0, 0, HALF)

            def expert(e, par, age, left):
                for h in (0, 1):
                    dve.wait_ge(moe["turned"], 2 * e + h + 1)
                    after(dve, moe["up"], 8 * e - 8)
                    dve.tensor_copy(EBT[:, par, C2 * h:C2 * h + C2], PS[0][:, h, 0:C2]).then_inc(moe["cols"], 1)
                after(dve, y_stored[par], 16 * (e // 2) if isinstance(e, int) else even(e, par))
                for h in (0, 1):
                    dve.wait_ge(moe["down"], 2 * e + h + 1)
                    dve.tensor_tensor(YB[:, par, 3 * h:3 * h + 3, :], PS[3][0:ER, h, 0:3 * D].rearrange("p (i d) -> p i d", d=D),
                                      b2[0:ER, ds(e, 1), :].broadcast_to([ER, 3, D]), ALU.add).then_inc(moe["y"], 1)

            each(dve, 0, EXPERTS, expert)
            attention(L0, HALF, B)

            dve.wait_ge(second_in, 16 * N_SECOND)
            for s in (0, 1):
                dve.tensor_copy(cn_w4r[32 * s:32 * s + 32, s, :], cn_w4[32 * s:32 * s + 32, 0:1].broadcast_to([32, P]))
            dve.tensor_copy(gc_w3r[:, :], gc_w[2][:, 0:1].broadcast_to([32, P]))
            dve.tensor_scalar(sc[:, 0:1], arange[:, :], 0.3, const["sign"], ALU.mult, ALU.mult)
            dve.tensor_scalar(sc[:, 2:3], gc_b[2][:, :], 0.5, None, ALU.mult)
            dve.tensor_scalar(sc[:, 3:4], cn_b[3][:, :], 0.5, None, ALU.mult).then_inc(net_consts, 1)
            dve.wait_ge(L0.out_taken, B)
            m = norm[1]
            for c in range(CHUNKS + 2):
                if c < CHUNKS:
                    k, par = c, c % 2
                    dve.wait_ge(m["tanh"], k + 1)
                    after(dve, m["added"], k - 1)
                    dve.wait_ge(m["product"], k + 1)
                    dve.scalar_tensor_tensor(SG[:, par, :, :].rearrange("p t d -> p (t d)"),
                                             TH[:, par, :, :].rearrange("p t d -> p (t d)"), 1.0,
                                             SRES[:, CT * k:CT * k + CT, :].rearrange("p t d -> p (t d)"), ALU.add, ALU.mult
                                             ).then_inc(m["gated"], 1)
                if 0 < c <= CHUNKS:
                    dve.wait_ge(m["added"], c)
                    statistics(1, c - 1)
                if 1 < c:
                    normalise(1, c - 2)

            def coupling_parts():
                v = Chain(dve, mean["ab"])
                """0.7 r tanh g + 0.1 with the twist's sign, for each sequence"""
                dve.wait_ge(mean["e3"], 1)
                v.link(dve.tensor_scalar(AB[:, :], GA[:, :], 0.7, None, ALU.mult))
                v.link(dve.tensor_scalar(AB[:, :], AB[:, :], arange[:, 0:1], 0.1, ALU.mult, ALU.add))
                v.link(dve.tensor_scalar(AB[:, :], AB[:, :], const["sign"], None, ALU.mult))

            dve.wait_ge(norm[1]["cols"], CHUNKS)
            for step, p, k, s in net_steps():
                f = ffn[p]
                first_chunk = 4 * (k // CYCLES) + 2 * p
                if step == "load":
                    after(dve, f["last"], 2 * (k // CYCLES) + s - 1)
                    c0 = CW * (first_chunk + s)
                    dve.tensor_copy(U[:, 2 * p + s, :], XNT[:, c0:c0 + CW]).then_inc(f["state"], 1)
                elif step == "second":
                    if (p, k) == (0, 0):
                        coupling_parts()
                    if k == CYCLES:
                        dve.wait_ge(f["gate"], 2)
                    for h in (0, 1):
                        q = 2 * p + h
                        dve.wait_ge(swapped[q], 32 * (k + 1))
                        for b in (0, 1):
                            n = 2 * (first_chunk + h) + b
                            cols = slice(S * b, S * b + S)
                            a = dve.scalar_tensor_tensor(TM[:, q, cols], UT[:, q, cols], AB[:, n:n + 1], U[:, q, cols],
                                                         ALU.mult, ALU.add)
                        a.then_inc(f["vec"], 1)
                elif step == "fourth":
                    q = 2 * p + s
                    dve.wait_ge(f["t4"], 2 * k + s + 1)
                    dve.scalar_tensor_tensor(TC[:, q, :], TC[:, q, :], sc[:, 0:1], UT[:, q, :], ALU.mult, ALU.mult
                                             ).then_inc(f["vec"], 1)
                    dve.wait_ge(f["vec"], 4 * k + 3 + s)
                    dve.tensor_tensor(U[:, q, :], TM[:, q, :], TC[:, q, :], ALU.add).then_inc(f["state"], 1)
                elif step == "gate":
                    for h in (0, 1):
                        dve.wait_ge(f["t5"], 2 * (k // CYCLES) + h + 1)
                        t0 = CT * (first_chunk + h)
                        dve.scalar_tensor_tensor(XN[:, t0:t0 + CT, :].rearrange("p t d -> p (t d)"), TC[:, 2 * p + h, :], 1.0,
                                                 TM[:, 2 * p + h, :], ALU.add, ALU.mult).then_inc(f["gate"], 1)

            dve.wait_ge(bias_made, 1)
            attention(L1, 0, B)


_NATURAL = ["L0_attn_x", "L0_attn_W_qkv", "L0_attn_W_out", "L0_ffn_wg", "L0_ffn_b2", "L1_attn_bo",
            "L1_ffn_cn_w1", "L1_ffn_cn_b1", "L1_ffn_cn_w2", "L1_ffn_cn_b2", "L1_ffn_cn_w3", "L1_ffn_cn_b3",
            "L1_ffn_cn_w4", "L1_ffn_cn_b4", "L1_ffn_gc_w1", "L1_ffn_gc_b1", "L1_ffn_gc_w2", "L1_ffn_gc_b2",
            "L1_ffn_gc_w3", "L1_ffn_gc_b3", "L1_ffn_adaptive_range"]


def host_arrays(inputs):
    a = {k: np.ascontiguousarray(inputs[k]) for k in _NATURAL}
    t = [np.ascontiguousarray(inputs[k]).T for k in ("L1_attn_Wq", "L1_attn_Wk", "L1_attn_Wv")]
    a["w_qkv1"] = np.ascontiguousarray(np.concatenate(t, axis=1))
    a["w_out1"] = np.ascontiguousarray(np.ascontiguousarray(inputs["L1_attn_Wo"]).T)
    a["b1_cols"] = np.ascontiguousarray(np.ascontiguousarray(inputs["L0_ffn_b1"]).reshape(EXPERTS * FC, P).T)
    a["L0_ffn_W1"] = np.ascontiguousarray(np.ascontiguousarray(inputs["L0_ffn_W1"]).transpose(1, 0, 2).reshape(D, -1))
    w2 = np.ascontiguousarray(inputs["L0_ffn_W2"]).reshape(EXPERTS * FC, P, D)
    a["L0_ffn_W2"] = np.ascontiguousarray(w2.transpose(1, 0, 2))
    a["bias_by_head"] = np.ascontiguousarray(np.ascontiguousarray(inputs["L1_attn_denom_bias"]).reshape(HG, HG).T)
    a["consts"] = constants()
    return a


def kernel(**inputs):
    import concourse.bacc as _bacc
    from concourse.bass_utils import run_bass_kernel_spmd as _run

    arrays = host_arrays(inputs)
    nc = _bacc.Bacc("TRN2", target_bir_lowering=False, num_devices=1)
    d = {k: nc.dram_tensor(f"in_{k}_dram", a.shape, mybir.dt.from_np(a.dtype), kind="ExternalInput").ap()
         for k, a in arrays.items()}
    out = nc.dram_tensor("out_dram", (B, S, D), F32, kind="ExternalOutput").ap()
    two_blocks(nc, d, out)
    r = _run(nc, [{f"in_{k}_dram": a for k, a in arrays.items()}], core_ids=[0])
    return r.results[0]["out_dram"]
```
